# Optimizing a Trainium2 kernel written in Bass

```python
import numpy as np
import jax
import jax.numpy as jnp

def _softmax(x, axis=-1):
    return jax.nn.softmax(x, axis=axis)

def _gelu(x):
    return jax.nn.gelu(x, approximate=True)

def _silu(x):
    return jax.nn.silu(x)

def _sigmoid(x):
    return jax.nn.sigmoid(x)

def _layernorm(x, axis=-1, eps=1e-05):
    m = jnp.mean(x, axis=axis, keepdims=True)
    v = jnp.var(x, axis=axis, keepdims=True)
    return (x - m) / jnp.sqrt(v + eps)

def _scatter_add(tgt, idx, src, axis=0):
    return tgt.at[idx].add(src)

def _segment_sum(src, seg, n):
    return jax.ops.segment_sum(src, seg, n)
kernel_name = 'mk_decoder_postln_d1_seqx_r4_4b40fe'

def setup_inputs(seed: int=0):
    np.random.seed(seed)
    _w = jnp.asarray

    def _rec_inputs():
        import jax
        import jax.numpy as jnp
        _rk = jax.random.key(seed)
        x = 7.22e-05 + 1 * jax.random.normal(jax.random.fold_in(_rk, 1), (4, 1024, 256), jnp.float32)
        _lenS = 1024 - jax.random.randint(jax.random.fold_in(_rk, 7), (4,), 0, max(1, 1024 // 4) + 1, jnp.int32)
        _lenS2 = 64 - jax.random.randint(jax.random.fold_in(_rk, 8), (4,), 0, max(1, 64 // 4) + 1, jnp.int32)
        _ctx_1024P = jax.random.normal(jax.random.fold_in(_rk, 11), (4, 16, 256), jnp.float32)
        _ctx_1024c = jax.random.dirichlet(jax.random.fold_in(_rk, 511), 0.3 * jnp.ones((16,), jnp.float32), (4, 64))
        _ctx_1024t = jnp.einsum('bsk,bkd->bsd', _ctx_1024c, _ctx_1024P)
        _ctx_1024t = _ctx_1024t * jax.lax.rsqrt(jnp.mean(jnp.square(_ctx_1024t)) + 1e-12) * 0.953939
        ctx_1024 = 4.14335e-05 + 0.999786 * (_ctx_1024t + 0.3 * jax.random.normal(jax.random.fold_in(_rk, 611), (4, 64, 256), jnp.float32))
        return (x, ctx_1024)
    x, ctx_1024 = _rec_inputs()

    def _L0_attn_setup():
        import jax, jax.numpy as jnp
        import numpy as np
        from jax import lax
        D_MODEL = 256
        N_HEADS = 16
        FACTOR = 1
        key = jax.random.key(seed)
        ks = jax.random.split(key, 9)
        B, S, D = (8, 512, D_MODEL)
        x = jax.random.normal(ks[0], (B, S, D), dtype=jnp.float32)
        scale = 1.0 / np.sqrt(D)
        Wq = jax.random.normal(ks[1], (D, D), dtype=jnp.float32) * scale
        Wk = jax.random.normal(ks[2], (D, D), dtype=jnp.float32) * scale
        Wv = jax.random.normal(ks[3], (D, D), dtype=jnp.float32) * scale
        Wo = jax.random.normal(ks[4], (D, D), dtype=jnp.float32) * scale
        bq = jax.random.normal(ks[5], (D,), dtype=jnp.float32) * scale
        bk = jax.random.normal(ks[6], (D,), dtype=jnp.float32) * scale
        bv = jax.random.normal(ks[7], (D,), dtype=jnp.float32) * scale
        bo = jax.random.normal(ks[8], (D,), dtype=jnp.float32) * scale
        return {'x': x, 'Wq': Wq, 'bq': bq, 'Wk': Wk, 'bk': bk, 'Wv': Wv, 'bv': bv, 'Wo': Wo, 'bo': bo}
    _L0_attn_all = _L0_attn_setup()
    _L0_attn_in = {k: v for k, v in _L0_attn_all.items() if k in ('Wq', 'bq', 'Wk', 'bk', 'Wv', 'bv', 'Wo', 'bo')}
    del _L0_attn_all

    def _L0_xattn_setup():
        import jax, jax.numpy as jnp
        import numpy as np
        N_EMBD = 256
        N_HEAD = 16
        key = jax.random.key(seed)
        ks = jax.random.split(key, 8)
        C = N_EMBD
        s = 1.0 / np.sqrt(C)
        return {'x': jax.random.normal(ks[0], (8, 256, C), jnp.float32), 'encoder_output': jax.random.normal(ks[1], (8, 144, C), jnp.float32), 'Wq': jax.random.normal(ks[2], (C, C), jnp.float32) * s, 'bq': jnp.zeros((C,), jnp.float32), 'Wkv': jax.random.normal(ks[3], (2 * C, C), jnp.float32) * s, 'bkv': jnp.zeros((2 * C,), jnp.float32), 'Wo': jax.random.normal(ks[4], (C, C), jnp.float32) * s, 'bo': jnp.zeros((C,), jnp.float32)}
    _L0_xattn_all = _L0_xattn_setup()
    _L0_xattn_in = {k: v for k, v in _L0_xattn_all.items() if k in ('Wq', 'bq', 'Wkv', 'bkv', 'Wo', 'bo')}
    del _L0_xattn_all

    def _L0_ffn_setup():
        import jax, jax.numpy as jnp
        import numpy as np
        B, N, D, H, E = (4, 256, 256, 16, 8)
        DK = D // H
        HID = 4 * D
        EPS = 1e-05

        def _layernorm(x, w, b):
            m = jnp.mean(x, axis=-1, keepdims=True)
            v = jnp.mean(jnp.square(x - m), axis=-1, keepdims=True)
            return (x - m) * jax.lax.rsqrt(v + EPS) * w + b

        def _msa(x, w_qkv, w_proj):
            b, n, d = x.shape
            qkv = (x @ w_qkv).reshape(b, n, 3, H, DK)
            q = qkv[:, :, 0].transpose(0, 2, 1, 3)
            k = qkv[:, :, 1].transpose(0, 2, 1, 3)
            v = qkv[:, :, 2].transpose(0, 2, 1, 3)
            attn = jnp.einsum('bhnd,bhmd->bhnm', q, k) * (1.0 / np.sqrt(DK))
            attn = jax.nn.softmax(attn, axis=-1)
            y = jnp.einsum('bhnm,bhmd->bhnd', attn, v)
            y = y.transpose(0, 2, 1, 3).reshape(b, n, d)
            return y @ w_proj

        def _moe_mlp(x, gate_w, gate_b, w1, w2):
            b, n, d = x.shape
            xf = x.reshape(b * n, d)
            logits = xf @ gate_w + gate_b
            one_hot = jax.nn.one_hot(jnp.argmax(logits, axis=-1), E, dtype=xf.dtype)
            h = jax.nn.gelu(jnp.einsum('td,edh->teh', xf, w1), approximate=True)
            y = jnp.einsum('teh,ehd->ted', h, w2)
            out = jnp.einsum('te,ted->td', one_hot, y)
            return out.reshape(b, n, d)
        key = jax.random.key(seed)
        ks = jax.random.split(key, 8)
        s = 0.02
        return {'x': jax.random.normal(ks[0], (B, N, D), jnp.float32), 'ln1_w': jnp.ones((D,), jnp.float32), 'ln1_b': jnp.zeros((D,), jnp.float32), 'w_qkv': jax.random.normal(ks[1], (D, 3 * D), jnp.float32) * s, 'w_proj': jax.random.normal(ks[2], (D, D), jnp.float32) * s, 'ln2_w': jnp.ones((D,), jnp.float32), 'ln2_b': jnp.zeros((D,), jnp.float32), 'gate_w': jax.random.normal(ks[3], (D, E), jnp.float32) * s, 'gate_b': jnp.zeros((E,), jnp.float32), 'w1': jax.random.normal(ks[4], (E, D, HID), jnp.float32) * s, 'w2': jax.random.normal(ks[5], (E, HID, D), jnp.float32) * s}
    _L0_ffn_all = _L0_ffn_setup()
    _L0_ffn_in = {k: v for k, v in _L0_ffn_all.items() if k in ('ln1_w', 'ln1_b', 'w_qkv', 'w_proj', 'ln2_w', 'ln2_b', 'gate_w', 'gate_b', 'w1', 'w2')}
    del _L0_ffn_all
    return {'x': x, 'ctx_1024': ctx_1024, 'L0_attn_Wq': _L0_attn_in['Wq'], 'L0_attn_bq': _L0_attn_in['bq'], 'L0_attn_Wk': _L0_attn_in['Wk'], 'L0_attn_bk': _L0_attn_in['bk'], 'L0_attn_Wv': _L0_attn_in['Wv'], 'L0_attn_bv': _L0_attn_in['bv'], 'L0_attn_Wo': _L0_attn_in['Wo'], 'L0_attn_bo': _L0_attn_in['bo'], 'L0_xattn_Wq': _L0_xattn_in['Wq'], 'L0_xattn_bq': _L0_xattn_in['bq'], 'L0_xattn_Wkv': _L0_xattn_in['Wkv'], 'L0_xattn_bkv': _L0_xattn_in['bkv'], 'L0_xattn_Wo': _L0_xattn_in['Wo'], 'L0_xattn_bo': _L0_xattn_in['bo'], 'L0_ffn_ln1_w': _L0_ffn_in['ln1_w'], 'L0_ffn_ln1_b': _L0_ffn_in['ln1_b'], 'L0_ffn_w_qkv': _L0_ffn_in['w_qkv'], 'L0_ffn_w_proj': _L0_ffn_in['w_proj'], 'L0_ffn_ln2_w': _L0_ffn_in['ln2_w'], 'L0_ffn_ln2_b': _L0_ffn_in['ln2_b'], 'L0_ffn_gate_w': _L0_ffn_in['gate_w'], 'L0_ffn_gate_b': _L0_ffn_in['gate_b'], 'L0_ffn_w1': _L0_ffn_in['w1'], 'L0_ffn_w2': _L0_ffn_in['w2']}

def reference(x, ctx_1024, L0_attn_Wq, L0_attn_bq, L0_attn_Wk, L0_attn_bk, L0_attn_Wv, L0_attn_bv, L0_attn_Wo, L0_attn_bo, L0_xattn_Wq, L0_xattn_bq, L0_xattn_Wkv, L0_xattn_bkv, L0_xattn_Wo, L0_xattn_bo, L0_ffn_ln1_w, L0_ffn_ln1_b, L0_ffn_w_qkv, L0_ffn_w_proj, L0_ffn_ln2_w, L0_ffn_ln2_b, L0_ffn_gate_w, L0_ffn_gate_b, L0_ffn_w1, L0_ffn_w2):
    import jax
    import jax.numpy as jnp

    def _L0_attn_ref(x, Wq, bq, Wk, bk, Wv, bv, Wo, bo):
        import jax, jax.numpy as jnp
        import numpy as np
        from jax import lax
        D_MODEL = 256
        N_HEADS = 16
        FACTOR = 1
        B, S, D = x.shape
        H = N_HEADS
        dk = D // H
        topk = S * FACTOR

        def proj(W, b):
            y = x @ W + b
            return y.reshape(B, S, H, dk).transpose(0, 2, 1, 3)
        Q = proj(Wq, bq)
        K = proj(Wk, bk)
        V = proj(Wv, bv)
        qf = jnp.fft.rfft(Q, axis=-2)
        kf = jnp.fft.rfft(K, axis=-2)
        corr = jnp.fft.irfft(qf * jnp.conj(kf), n=S, axis=-2)
        w = lax.top_k(corr.transpose(0, 1, 3, 2), topk)[0]
        w = w.transpose(0, 1, 3, 2)
        w = jax.nn.softmax(w, axis=-2)
        out = jnp.einsum('bhti,bhij->bhtj', w, V[:, :, :dk, :])
        ctx = out.transpose(0, 2, 1, 3).reshape(B, topk, D)
        return ctx @ Wo + bo

    def _L0_xattn_ref(x, encoder_output, Wq, bq, Wkv, bkv, Wo, bo):
        import jax, jax.numpy as jnp
        import numpy as np
        N_EMBD = 256
        N_HEAD = 16
        B, T, C = x.shape
        I = encoder_output.shape[1]
        H, D = (N_HEAD, C // N_HEAD)
        q = jnp.einsum('btc,oc->bto', x, Wq) + bq
        kv = jnp.einsum('bic,oc->bio', encoder_output, Wkv) + bkv
        k, v = (kv[..., :C], kv[..., C:])
        q = q.reshape(B, T, H, D).transpose(0, 2, 1, 3)
        k = k.reshape(B, I, H, D).transpose(0, 2, 1, 3)
        v = v.reshape(B, I, H, D).transpose(0, 2, 1, 3)
        att = jnp.einsum('bhtd,bhid->bhti', q, k) * (1.0 / np.sqrt(D))
        att = jax.nn.softmax(att, axis=-1)
        y = jnp.einsum('bhti,bhid->bhtd', att, v)
        y = y.transpose(0, 2, 1, 3).reshape(B, T, C)
        return jnp.einsum('btc,oc->bto', y, Wo) + bo

    def _L0_ffn_ref(x, ln1_w, ln1_b, w_qkv, w_proj, ln2_w, ln2_b, gate_w, gate_b, w1, w2):
        import jax, jax.numpy as jnp
        import numpy as np
        B, N, D, H, E = (4, 256, 256, 16, 8)
        DK = D // H
        HID = 4 * D
        EPS = 1e-05

        def _layernorm(x, w, b):
            m = jnp.mean(x, axis=-1, keepdims=True)
            v = jnp.mean(jnp.square(x - m), axis=-1, keepdims=True)
            return (x - m) * jax.lax.rsqrt(v + EPS) * w + b

        def _msa(x, w_qkv, w_proj):
            b, n, d = x.shape
            qkv = (x @ w_qkv).reshape(b, n, 3, H, DK)
            q = qkv[:, :, 0].transpose(0, 2, 1, 3)
            k = qkv[:, :, 1].transpose(0, 2, 1, 3)
            v = qkv[:, :, 2].transpose(0, 2, 1, 3)
            attn = jnp.einsum('bhnd,bhmd->bhnm', q, k) * (1.0 / np.sqrt(DK))
            attn = jax.nn.softmax(attn, axis=-1)
            y = jnp.einsum('bhnm,bhmd->bhnd', attn, v)
            y = y.transpose(0, 2, 1, 3).reshape(b, n, d)
            return y @ w_proj

        def _moe_mlp(x, gate_w, gate_b, w1, w2):
            b, n, d = x.shape
            xf = x.reshape(b * n, d)
            logits = xf @ gate_w + gate_b
            one_hot = jax.nn.one_hot(jnp.argmax(logits, axis=-1), E, dtype=xf.dtype)
            h = jax.nn.gelu(jnp.einsum('td,edh->teh', xf, w1), approximate=True)
            y = jnp.einsum('teh,ehd->ted', h, w2)
            out = jnp.einsum('te,ted->td', one_hot, y)
            return out.reshape(b, n, d)
        x = x + _msa(_layernorm(x, ln1_w, ln1_b), w_qkv, w_proj)
        x = x + _moe_mlp(_layernorm(x, ln2_w, ln2_b), gate_w, gate_b, w1, w2)
        return x
    x = _layernorm(x + _L0_attn_ref(x, L0_attn_Wq, L0_attn_bq, L0_attn_Wk, L0_attn_bk, L0_attn_Wv, L0_attn_bv, L0_attn_Wo, L0_attn_bo), axis=-1)
    x = _layernorm(x + _L0_xattn_ref(x, ctx_1024, L0_xattn_Wq, L0_xattn_bq, L0_xattn_Wkv, L0_xattn_bkv, L0_xattn_Wo, L0_xattn_bo), axis=-1)
    x = _layernorm(x + _L0_ffn_ref(x, L0_ffn_ln1_w, L0_ffn_ln1_b, L0_ffn_w_qkv, L0_ffn_w_proj, L0_ffn_ln2_w, L0_ffn_ln2_b, L0_ffn_gate_w, L0_ffn_gate_b, L0_ffn_w1, L0_ffn_w2), axis=-1)
    return x

_drawn_inputs = setup_inputs


def setup_inputs(seed=0):
    import zlib

    import numpy as np

    out = dict(_drawn_inputs(seed))
    spreads = {'L0_xattn_bq': (0.0, 0.339),
     'L0_xattn_bkv': (0.0, 0.1),
     'L0_xattn_bo': (0.0, 0.1),
     'L0_ffn_ln1_w': (1.0, 0.6),
     'L0_ffn_ln1_b': (0.0, 0.8),
     'L0_ffn_ln2_w': (1.0, 0.2),
     'L0_ffn_ln2_b': (0.0, 0.349),
     'L0_ffn_gate_b': (0.0, 0.1)}
    factors = {'L0_attn_Wq': 200.0,
     'L0_attn_bq': 64.0,
     'L0_attn_Wk': 200.0,
     'L0_attn_bk': 64.0,
     'L0_attn_bv': 38.812,
     'L0_attn_Wv': 4.645}
    for name, (base, spread) in spreads.items():
        noise = np.random.default_rng([zlib.crc32(name.encode()), seed]).standard_normal(out[name].shape)
        drawn = base * np.exp(spread * noise) if base else spread * noise
        out[name] = jnp.asarray(drawn.astype(out[name].dtype))
    for name, factor in factors.items():
        out[name] = (out[name] * factor).astype(out[name].dtype)
    return out
```

```python
from contextlib import ExitStack

import numpy as np

import concourse.bass as bass
from concourse import mybir

F32 = mybir.dt.float32
BF16 = mybir.dt.bfloat16
I32 = mybir.dt.int32
U32 = mybir.dt.uint32
ALU = mybir.AluOpType
ACT = mybir.ActivationFunctionType
AX = mybir.AxisListType
ds = bass.ds

B, S, D, H = 4, 1024, 256, 16
DK = D // H
P = 128
TPB = S // P
NT = B * TPB
KT = D // P
EPS = 1e-5
TOP = 8
G = B * KT
EXP_ZERO = -104.0
LOWEST = -3.0e38


class Chain:

    def __init__(self, eng, sem, base=0):
        self.eng, self.sem, self.base, self.n = eng, sem, base, 0

    def link(self, ins):
        self.n += 1
        ins.then_inc(self.sem, 1)
        self.eng.wait_ge(self.sem, self.base + self.n)


def autocorrelation(nc, ctx, t, dram):
    def sb(name, shape, dt=F32):
        return ctx.enter_context(nc.sbuf_tensor("sb_" + name, shape, dt))

    def sem(name):
        return ctx.enter_context(nc.semaphore(name))

    X, ps = t["X"], t["ps"]
    fold = sb("fold", [P, TPB, D])
    even = sb("even", [P, 4, D])
    fwd_odd = sb("fwd_odd", [P, 4, 512])
    fwd_even = sb("fwd_even", [P, 4, 256])
    inv_odd = sb("inv_odd", [P, 4, 512])
    inv_even = sb("inv_even", [P, 4, 256])
    w_qk = sb("w_qk", [P, KT, 2 * D])
    w_v = sb("w_v", [P, KT, D])
    w_o = sb("w_o", [P, KT, D])
    b_qk = sb("b_qk", [1, 2 * D])
    b_v = sb("b_v", [P, KT])
    bo = sb("bo", [P, D])
    f0 = sb("f0", [1, P])
    xT16 = sb("xT16", [P, KT, B * DK])
    head_mask = sb("head_mask", [P, TOP])
    vT = sb("vT", [P, KT, B * DK])
    vblk = sb("vblk", [P, KT, B, P])
    vwo = sb("vwo", [P, G, D])
    xfT = sb("xfT", [P, KT, 2, 512])
    qk = sb("qk", [P, 8, 2 * D])
    cross = sb("cross", [P, 8, D])
    prod = sb("prod", [P, 4, D])
    corr = sb("corr", [P, G, S])
    w_sort = sb("w_sort", [P, G, S])
    uv = sb("uv", [P, 2, 256])
    m8 = sb("m8", [P, G, TOP])
    d8 = sb("d8", [P, G, TOP])
    e8 = sb("e8", [P, G, TOP])
    wsum = sb("wsum", [P, G])
    wrec = sb("wrec", [P, G])
    neg_m = sb("neg_m", [P, G])
    ones = sb("ones_a", [P, 1])
    tail = sb("tail", [P, 2])
    tail_flag = sb("tail_flag", [1, 1], I32)
    cur8 = sb("cur8", [P, TOP])

    consts_in, x_in = sem("a_consts_in"), sem("a_x_in")
    zeroed, folded, spectrum, spectrum_T = sem("a_zeroed"), sem("a_folded"), sem("a_spectrum"), sem("a_spectrum_T")
    qk_done, qk_copied, cross_done = sem("a_qk_done"), sem("a_qk_copied"), sem("a_cross_done")
    inv_done, corr_done = sem("a_inv_done"), sem("a_corr_done")
    bo_added = sem("a_bo_added")
    v_done, v_copied, vblk_done, vwo_done, vwo_copied = (sem("a_" + n) for n in (
        "v_done", "v_copied", "vblk_done", "vwo_done", "vwo_copied"))
    tail_local, tail_counted, flag_set = sem("a_tail_local"), sem("a_tail_counted"), sem("a_flag_set")
    diffs, exps, weights, y_done = sem("a_diffs"), sem("a_exps"), sem("a_weights"), sem("a_y_done")
    dve_steps, sort_steps = sem("a_dve_steps"), sem("a_sort_steps")
    sorted_done, gen_exps, gen_weights, gen_y, gen_added = (sem("a_" + n) for n in (
        "sorted", "gen_exps", "gen_weights", "gen_y", "gen_added"))
    n_consts = 13

    with nc.Block() as block:
        @block.sync
        def _(sp):
            for b in range(B):
                sp.dma_start(X[:, b * TPB:(b + 1) * TPB, :],
                             dram["x"][b].rearrange("(n p) d -> p n d", p=P)).then_inc(x_in, 16)
            for dst, src in (
                (fwd_odd[:, :, :], dram["fwd_odd"].rearrange("(k p) n -> p k n", p=P)),
                (fwd_even[:, :, :], dram["fwd_even"].rearrange("(k p) n -> p k n", p=P)),
                (w_qk[:, :, 0:D], dram["L0_attn_Wq"].rearrange("(k p) n -> p k n", p=P)),
                (w_qk[:, :, D:2 * D], dram["L0_attn_Wk"].rearrange("(k p) n -> p k n", p=P)),
                (b_qk[:, :], dram["b_qk"]),
                (f0[:, :], dram["f0"]),
                (inv_odd[:, :, :], dram["inv_odd"].rearrange("(k p) n -> p k n", p=P)),
                (inv_even[:, :, :], dram["inv_even"].rearrange("(k p) n -> p k n", p=P)),
                (w_v[:, :, :], dram["L0_attn_Wv"].rearrange("(k p) n -> p k n", p=P)),
                (w_o[:, :, :], dram["L0_attn_Wo"].rearrange("(k p) n -> p k n", p=P)),
                (b_v[:, :], dram["bv_attn"]),
                (xT16[:, :, :], dram["xT16"].rearrange("(k p) n -> p k n", p=P)),
                (head_mask[:, :], dram["head_mask"]),
            ):
                sp.dma_start(dst, src).then_inc(consts_in, 16)
            sp.dma_start(bo[:, :], dram["bo_attn"].partition_broadcast(P)).then_inc(x_in, 16)

        @block.gpsimd
        def _(pool):
            pool.memset(ones[:, :], 1.0).then_inc(zeroed, 1)
            pool.memset(w_sort[:, :, :], 0.0).then_inc(zeroed, 1)
            pool.wait_ge(x_in, 16 * (B + 1))
            with pool.Fori(0, B) as b:
                pool.wait_ge(folded, b + 1)
                pool.tensor_tensor(X[:, ds(b * TPB, TPB), :], X[:, ds(b * TPB, TPB), :],
                                   bo[:, :].unsqueeze(1).broadcast_to([P, TPB, D]), ALU.add).then_inc(bo_added, 1)

        @block.tensor
        def _(pe):
            pe.sem_inc(inv_done, 1)
            pe.sem_inc(spectrum, 1)
            pe.sem_inc(qk_done, 1)
            pe.wait_ge(consts_in, 16 * n_consts)
            for c in range(KT):
                for k in range(KT):
                    mm = pe.matmul(ps[c][:, 0:B * DK], w_v[:, k, c * P:(c + 1) * P], xT16[:, k, :],
                                   start=(k == 0), stop=(k == KT - 1))
                mm.then_inc(v_done, 1)
            pe.wait_ge(vblk_done, KT)
            for b in range(B):
                for c in range(KT):
                    pe.matmul(ps[4 + b][:, c * D:(c + 1) * D], vblk[:, c, b, :], w_o[:, c, :],
                              start=True, stop=True).then_inc(vwo_done, 1)
            with pe.Fori(0, B) as b:
                pe.wait_ge(folded, b + 1)
                pe.wait_ge(corr_done, 1 + b * KT)
                for c in range(KT):
                    for k in range(4):
                        mm = pe.matmul(ps[c][:, :], fold[:, k, c * P:(c + 1) * P], fwd_odd[:, k, :],
                                       start=(k == 0), stop=(k == 3))
                    mm.then_inc(spectrum, 1)
                    for h in range(2):
                        for k in range(2):
                            mm = pe.matmul(ps[2 + c][:, h * 256:(h + 1) * 256],
                                           fold[:, 4 + 2 * h + k, c * P:(c + 1) * P], fwd_even[:, 2 * h + k, :],
                                           start=(k == 0), stop=(k == 1))
                    mm.then_inc(spectrum, 1)
                pe.wait_ge(spectrum_T, 6 * (b + 1))
                pe.wait_ge(vwo_copied, B)
                for f in range(8):
                    r, q = f // 4, f % 4
                    pe.wait_ge(qk_copied, 8 * b + f + 1)
                    for k in range(KT):
                        mm = pe.matmul(ps[4 + f % 4][:, :], xfT[:, k, r, q * P:(q + 1) * P], w_qk[:, k, :],
                                       start=(k == 0), stop=(k == KT - 1 and f != 3))
                    if f == 3:
                        mm = pe.matmul(ps[7][:, :], f0[:, :], b_qk[:, :], start=False, stop=True)
                    mm.then_inc(qk_done, 1)
                pe.wait_ge(cross_done, b + 2)
                for c in range(KT):
                    cs = slice(c * P, (c + 1) * P)
                    for n, f in enumerate((0, 1, 4, 5)):
                        pe.matmul(ps[c][:, :], cross[:, f, cs], inv_odd[:, n, :], start=(n == 0), stop=(n == 3))
                    for h in range(2):
                        for n in range(2):
                            mm = pe.matmul(ps[2 + c][:, h * 256:(h + 1) * 256], cross[:, 2 + h + 4 * n, cs],
                                           inv_even[:, 2 * h + n, :], start=(n == 0), stop=(n == 1))
                    mm.then_inc(inv_done, 1)
            pe.wait_ge(tail_local, 1)
            pe.wait_ge(zeroed, 1)
            pe.matmul(ps[7][0:1, 0:1], tail[:, 1:2], ones[:, :], start=True, stop=True).then_inc(tail_counted, 1)
            pe.wait_ge(flag_set, 1)
            general = pe.value_load(tail_flag[0:1, 0:1], min_val=0, max_val=P)
            with pe.If(general > 0):
                pe.wait_ge(gen_weights, G)
                for b in range(B):
                    for i in range(1, TPB):
                        n = b * (TPB - 1) + i - 1
                        if n >= 4:
                            pe.wait_ge(gen_added, n - 3)
                        for k in range(KT):
                            mm = pe.matmul(ps[n % 4][:, 0:D], w_sort[:, b * KT + k, i * P:(i + 1) * P],
                                           vwo[:, b * KT + k, :], start=(k == 0), stop=(k == KT - 1))
                        mm.then_inc(gen_y, 1)
                pe.nop()
            pe.wait_ge(weights, 1)
            pe.wait_ge(qk_copied, 4 + 8 * B)
            for b in range(B):
                for k in range(KT):
                    mm = pe.matmul(ps[4 + b][:, 0:D], w_sort[:, b * KT + k, 0:P], vwo[:, b * KT + k, :],
                                   start=(k == 0), stop=(k == KT - 1))
                mm.then_inc(y_done, 1)

        @block.scalar
        def _(act):
            act.wait_ge(consts_in, 16 * n_consts)
            for c in range(KT):
                act.wait_ge(v_done, c + 1)
                act.activation(vT[:, c, :], ps[c][:, 0:B * DK], ACT.Identity, bias=b_v[:, c:c + 1]).then_inc(v_copied, 1)
            for b in range(B):
                act.wait_ge(vwo_done, 2 * (b + 1))
                act.activation(vwo[:, b * KT:(b + 1) * KT, :], ps[4 + b][:, :].rearrange("p (k n) -> p k n", k=KT),
                               ACT.Identity).then_inc(vwo_copied, 1)
            act.sem_inc(qk_copied, 4)
            with act.Fori(0, B) as b:
                act.wait_ge(qk_done, 1 + 8 * b)
                for c in range(KT):
                    act.wait_ge(spectrum, 1 + 4 * b + 2 * c + 1)
                    act.activation(xfT[:, c, :, 0:256], ps[c][:, :].rearrange("p (r n) -> p r n", r=2),
                                   ACT.Identity).then_inc(spectrum_T, 1)
                    act.wait_ge(spectrum, 1 + 4 * b + 2 * c + 2)
                    for h in range(2):
                        act.activation(xfT[:, c, :, 256 + h * P:256 + (h + 1) * P],
                                       ps[2 + c][:, h * 256:(h + 1) * 256].rearrange("p (r n) -> p r n", r=2),
                                       ACT.Identity).then_inc(spectrum_T, 1)
                act.wait_ge(cross_done, b + 1)
                for f in range(8):
                    act.wait_ge(qk_done, 1 + 8 * b + f + 1)
                    act.activation(qk[:, f, :], ps[4 + f % 4][:, :], ACT.Identity).then_inc(qk_copied, 1)
            act.wait_ge(diffs, 1)
            act.activation(e8[:, :, :], d8[:, :, :], ACT.Exp).then_inc(exps, 1)
            act.wait_ge(flag_set, 1)
            general = act.value_load(tail_flag[0:1, 0:1], min_val=0, max_val=P)
            with act.If(general > 0):
                for g in range(G):
                    act.wait_ge(sorted_done, g + 1)
                    act.activation(w_sort[:, g, :], w_sort[:, g, :], ACT.Exp, bias=neg_m[:, g:g + 1],
                                   accum_out=wsum[:, g:g + 1]).then_inc(gen_exps, 1)
                act.nop()

        @block.vector
        def _(dve):
            dve.sem_inc(corr_done, 1)
            dve.sem_inc(cross_done, 1)
            dve.wait_ge(consts_in, 16 * n_consts)
            for c in range(KT):
                dve.wait_ge(v_copied, c + 1)
                dve.tensor_tensor(
                    vblk[:, c, :, :].rearrange("p b (h i) -> p b h i", h=8),
                    vT[:, c, :].rearrange("p (b i) -> p b i", b=B).unsqueeze(2).broadcast_to([P, B, 8, DK]),
                    head_mask[:, :].unsqueeze(1).unsqueeze(3).broadcast_to([P, B, 8, DK]), ALU.mult).then_inc(vblk_done, 1)
            dve.wait_ge(x_in, 16 * (B + 1))
            LINKS = 9
            with dve.Fori(0, B) as b:
                ch = Chain(dve, dve_steps, b * LINKS)
                lo, hi = X[:, ds(b * TPB, 4), :], X[:, ds(b * TPB + 4, 4), :]
                dve.wait_ge(spectrum, 1 + 4 * b)
                dve.tensor_tensor(fold[:, 0:4, :], lo, hi, ALU.subtract)
                ch.link(dve.tensor_tensor(even[:, :, :], lo, hi, ALU.add))
                dve.tensor_tensor(fold[:, 4:6, :], even[:, 0:2, :], even[:, 2:4, :], ALU.subtract)
                dve.tensor_tensor(fold[:, 6:8, :], even[:, 0:2, :], even[:, 2:4, :], ALU.add).then_inc(folded, 1)
                dve.wait_ge(qk_copied, 4 + 8 * (b + 1))
                dve.wait_ge(inv_done, 1 + KT * b)
                qr, kr, qi, ki = qk[:, 0:4, 0:D], qk[:, 0:4, D:2 * D], qk[:, 4:8, 0:D], qk[:, 4:8, D:2 * D]
                dve.tensor_tensor(cross[:, 4:8, :], qi, kr, ALU.mult)
                ch.link(dve.tensor_tensor(prod[:, :, :], qr, ki, ALU.mult))
                ch.link(dve.tensor_tensor(cross[:, 4:8, :], cross[:, 4:8, :], prod[:, :, :], ALU.subtract))
                dve.tensor_tensor(cross[:, 0:4, :], qr, kr, ALU.mult)
                ch.link(dve.tensor_tensor(prod[:, :, :], qi, ki, ALU.mult))
                ch.link(dve.tensor_tensor(cross[:, 0:4, :], cross[:, 0:4, :], prod[:, :, :], ALU.add))
                dve.tensor_copy(cross[0:1, 7, :], prod[0:1, 3, :])
                dve.tensor_tensor(cross[0:1, 3, :], qk[0:1, 3, 0:D], qk[0:1, 3, D:2 * D],
                                  ALU.mult).then_inc(cross_done, 1)
                for c in range(KT):
                    dve.wait_ge(inv_done, 1 + KT * b + c + 1)
                    dve.tensor_copy(prod[:, c, :], ps[2 + c][:, 256:512]).then_inc(dve_steps, 1)
                    ch.n += 1
                    dve.wait_ge(dve_steps, ch.base + ch.n)
                    dve.tensor_tensor(uv[:, 0, :], ps[2 + c][:, 0:256], prod[:, c, :], ALU.add)
                    ch.link(dve.tensor_tensor(uv[:, 1, :], prod[:, c, :], ps[2 + c][:, 0:256], ALU.subtract))
                    odd = ps[c][:, :].rearrange("p (r n) -> p r n", r=2)
                    row = corr[:, ds(b * KT + c, 1), :].rearrange("p o (a r n) -> p (o a) r n", a=2, r=2)
                    dve.tensor_tensor(row[:, 0], uv[:, :, :], odd, ALU.add)
                    dve.tensor_tensor(row[:, 1], uv[:, :, :], odd, ALU.subtract).then_inc(corr_done, 1)
                    if c == 0:
                        dve.wait_ge(corr_done, 1 + KT * b + 1)
            assert ch.n == LINKS, ch.n
            ch = Chain(dve, dve_steps, B * LINKS)
            dve.wait_ge(corr_done, 1 + G)
            for g in range(G):
                last = dve.max(m8[:, g, :], corr[:, g, :])
            ch.link(last)
            ch.link(dve.tensor_tensor(d8[:, :, :], m8[:, :, :], m8[:, :, 0:1].broadcast_to([P, G, TOP]), ALU.subtract))
            dve.sem_inc(diffs, 1)
            ch.link(dve.tensor_reduce(tail[:, 0:1], d8[:, :, TOP - 1], AX.X, ALU.max))
            dve.tensor_scalar(tail[:, 1:2], tail[:, 0:1], EXP_ZERO, None, ALU.is_ge).then_inc(tail_local, 1)
            dve.wait_ge(tail_counted, 1)
            dve.tensor_copy(tail_flag[:, :], ps[7][0:1, 0:1]).then_inc(flag_set, 1)
            dve.wait_ge(exps, 1)
            ch.link(dve.tensor_reduce(wsum[:, :], e8[:, :, :], AX.X, ALU.add))
            ch.link(dve.reciprocal(wrec[:, :], wsum[:, :]))
            dve.wait_ge(zeroed, 2)
            ch.link(dve.tensor_tensor(w_sort[:, :, 0:TOP], e8[:, :, :],
                                      wrec[:, :].unsqueeze(2).broadcast_to([P, G, TOP]), ALU.mult))
            dve.wait_ge(flag_set, 1)
            dve.wait_ge(bo_added, B)
            general = dve.value_load(tail_flag[0:1, 0:1], min_val=0, max_val=P)
            with dve.If(general > 0):
                gs = Chain(dve, sort_steps)
                gs.link(dve.tensor_scalar(neg_m[:, :], m8[:, :, 0], -1.0, None, ALU.mult))
                STEPS = S // TOP
                for g in range(G):
                    with dve.Fori(0, STEPS) as i:
                        st = Chain(dve, sort_steps, 1 + g * STEPS * 2 + i * 2)
                        st.link(dve.max(cur8[:, :], corr[:, g, :]))
                        dve.tensor_copy(w_sort[:, g, ds(i * TOP, TOP)], cur8[:, :])
                        st.link(dve.match_replace(corr[:, g, :], cur8[:, :], corr[:, g, :], LOWEST))
                    dve.sem_inc(sorted_done, 1)
                for g in range(G):
                    dve.wait_ge(gen_exps, g + 1)
                    gs2 = Chain(dve, sort_steps, 1 + G * STEPS * 2 + g)
                    gs2.link(dve.reciprocal(wrec[:, g:g + 1], wsum[:, g:g + 1]))
                    dve.tensor_scalar(w_sort[:, g, :], w_sort[:, g, :], wrec[:, g:g + 1], None,
                                      ALU.mult).then_inc(gen_weights, 1)
                for b in range(B):
                    for i in range(1, TPB):
                        n = b * (TPB - 1) + i - 1
                        dve.wait_ge(gen_y, n + 1)
                        dve.tensor_tensor(X[:, b * TPB + i, :], X[:, b * TPB + i, :], ps[n % 4][:, 0:D],
                                          ALU.add).then_inc(gen_added, 1)
                dve.wait_ge(gen_added, B * (TPB - 1))
                dve.nop()
            dve.sem_inc(weights, 1)
            for b in range(B):
                dve.wait_ge(y_done, b + 1)
                dve.tensor_tensor(X[:, b * TPB, :], X[:, b * TPB, :], ps[4 + b][:, 0:D], ALU.add)



def alone(eng, spare):
    eng.sem_inc(spare, 1)


def layer_stats(dve, ch, tiles, stats, mv, spare):
    alone(dve, spare)
    for n in range(TPB):
        last = dve.bn_stats(stats[:, n, :], tiles[:, n, :])
    ch.link(last)
    alone(dve, spare)
    for n in range(TPB):
        last = dve.bn_aggr(mv[:, n, :], stats[:, n, :])
    ch.link(last)
    ch.link(dve.tensor_scalar(mv[:, :, 1], mv[:, :, 1], EPS, None, ALU.add))


def cross_attention(nc, ctx, t, dram):
    def sb(name, shape, dt=F32):
        return ctx.enter_context(nc.sbuf_tensor("sb_b_" + name, shape, dt))

    def sem(name):
        return ctx.enter_context(nc.semaphore("b_" + name))

    X, ps, pz, ident, neg_half = t["X"], t["ps"], t["pz"], t["ident"], t["neg_half"]
    C = dram["ctxT"].shape[1] // B
    HP = H // 2
    VW = 2 * (DK + 1)
    w_q = sb("w_q", [P, KT, D])
    w_kv = sb("w_kv", [P, KT, 2 * D])
    w_o = sb("w_o", [P, KT, D])
    bias_q = sb("bias_q", [P, KT])
    bias_k = sb("bias_k", [P, KT])
    bias_v = sb("bias_v", [1, D])
    bias_o = sb("bias_o", [1, D])
    mask = sb("mask", [P, TOP])
    ctxT = sb("ctxT", [P, KT, B * C])
    ctxT2 = sb("ctxT2", [P, KT, B, 2, C])
    ones_row = sb("ones_row", [1, P])
    kT = sb("kT", [P, KT, B * C])
    kblk = sb("kblk", [P, KT, B, 8 * C])
    vblk = sb("vblk", [P, B, HP, 2, DK + 1])
    stats = sb("stats", [P, TPB, 6])
    mv = sb("mv", [P, TPB, 2])
    rstd = sb("rstd", [P, TPB])
    xs = sb("xs", [P, TPB, D])
    xT = sb("xT", [P, KT, S])
    qT = sb("qT", [P, KT, S])
    mx = sb("mx", [P, 2, H])
    pr = sb("pr", [P, 2, H, C])
    prT = sb("prT", [P, 2, HP, P])
    rec = sb("rec", [P, 2, H])
    y = sb("y", [P, 2, D])
    yT = sb("yT", [P, 2, KT, P])

    w_in = sem("w_in")
    zeroed, k_done, k_copied, v_done = sem("zeroed"), sem("k_done"), sem("k_copied"), sem("v_done")
    kblk_done, vblk_done = sem("kblk_done"), sem("vblk_done")
    dve_steps = sem("dve_steps")
    spare = sem("spare")
    var_done, rstd_done, xs_done, xT_done, xT_copied, q_done, q_copied = (sem(n) for n in (
        "var_done", "rstd_done", "xs_done", "xT_done", "xT_copied", "q_done", "q_copied"))
    scores, shifted, probs, probsT, probsT_copied, pv, y_done, yT_done, yT_copied, out_done, res_done = (
        sem(n) for n in ("scores", "shifted", "probs", "probsT", "probsT_copied", "pv", "y_done", "yT_done",
                         "yT_copied", "out_done", "res_done"))
    loads = [
        (w_kv[:, :, :], dram["WkvT"].rearrange("(k p) n -> p k n", p=P)),
        (ctxT[:, :, :], dram["ctxT"].rearrange("(k p) n -> p k n", p=P)),
        (bias_k[:, :], dram["bk_cross"]),
        (bias_v[:, :], dram["bv_cross"]),
        (w_q[:, :, :], dram["WqT"].rearrange("(k p) n -> p k n", p=P)),
        (bias_q[:, :], dram["bq_cross"]),
        (mask[:, :], dram["head_mask"]),
        (w_o[:, :, :], dram["WoT"].rearrange("(k p) n -> p k n", p=P)),
        (bias_o[:, :], dram["bo_cross"]),
    ] + [(ctxT2[:, k, :, r, :], dram["ctxT"][k * P:(k + 1) * P].rearrange("p (b c) -> p b c", b=B))
         for k in range(KT) for r in range(2)]

    with nc.Block() as block:
        @block.sync
        def _(sp):
            for dst, src in loads:
                sp.dma_start(dst, src).then_inc(w_in, 16)

        @block.gpsimd
        def _(pool):
            pool.memset(ones_row[:, :], 1.0).then_inc(zeroed, 1)
            pool.memset(vblk[:, :, :, :, :], 0.0).then_inc(zeroed, 1)
            pool.wait_ge(zeroed, 2)
            pool.memset(vblk[0:C, :, :, 0, DK:DK + 1], 1.0).then_inc(zeroed, 1)
            pool.memset(vblk[C:2 * C, :, :, 1, DK:DK + 1], 1.0).then_inc(zeroed, 1)
            pool.wait_ge(zeroed, 4)
            with pool.Fori(0, B) as b:
                pool.wait_ge(var_done, b + 1)
                pool.tensor_tensor(rstd[:, :], mv[:, :, 1], neg_half[:, :], ALU.pow).then_inc(rstd_done, 1)

        @block.tensor
        def _(pe):
            pe.wait_ge(w_in, 16 * len(loads))
            for c in range(KT):
                for k in range(KT):
                    mm = pe.matmul(ps[c][:, 0:B * C], w_kv[:, k, c * P:(c + 1) * P], ctxT[:, k, :],
                                   start=(k == 0), stop=(k == KT - 1))
                mm.then_inc(k_done, 1)
            pe.wait_ge(zeroed, 1)
            for b in range(B):
                for k in range(KT):
                    pe.matmul(ps[4 + b][:, 0:D], ctxT2[:, k, b, :, :].rearrange("p r c -> p (r c)"),
                              w_kv[:, k, D:2 * D], start=(k == 0), stop=False)
                pe.matmul(ps[4 + b][:, 0:D], ones_row[:, :], bias_v[:, :], start=False, stop=True).then_inc(v_done, 1)
            pe.wait_ge(k_copied, KT)
            pe.wait_ge(kblk_done, KT)
            pe.wait_ge(vblk_done, 2 * B)
            with pe.Fori(0, B) as b:
                n0 = b * TPB
                pe.wait_ge(xs_done, b + 1)
                pe.wait_ge(res_done, n0)
                for n in range(TPB):
                    for k in range(KT):
                        tr = pe.transpose(ps[2 * (n // 4) + k][:, n % 4 * P:(n % 4 + 1) * P],
                                          xs[:, n, k * P:(k + 1) * P], ident[:, :])
                    if n % 4 == 3:
                        tr.then_inc(xT_done, 1)
                pe.wait_ge(xT_copied, 2 * (b + 1))
                for c in range(KT):
                    for h in range(2):
                        for k in range(KT):
                            mm = pe.matmul(ps[4 + 2 * c + h][:, :], w_q[:, k, c * P:(c + 1) * P],
                                           xT[:, k, h * 512:(h + 1) * 512], start=(k == 0), stop=(k == KT - 1))
                        mm.then_inc(q_done, 1)
                pe.wait_ge(q_copied, 4 * (b + 1))
                for s in range(TPB + 2):
                    if s < TPB:
                        if s >= 2:
                            pe.wait_ge(shifted, n0 + s - 1)
                        for c in range(KT):
                            mm = pe.matmul(ps[2 * (s % 2) + c][:, :], qT[:, c, s * P:(s + 1) * P],
                                           kblk[:, c, ds(b, 1), :].rearrange("p o n -> p (o n)"), start=True, stop=True)
                        mm.then_inc(scores, 1)
                    u = s - 1
                    if 0 <= u < TPB:
                        pe.wait_ge(probs, n0 + u + 1)
                        if u >= 1:
                            pe.wait_ge(probsT_copied, n0 + u)
                        for j in range(HP):
                            tr = pe.transpose(ps[4 + j // 4][:, j % 4 * P:(j % 4 + 1) * P],
                                              pr[:, u % 2, 2 * j:2 * j + 2, :].rearrange("p h c -> p (h c)"), ident[:, :])
                        tr.then_inc(probsT, 1)
                    v = s - 2
                    if 0 <= v < TPB:
                        pe.wait_ge(y_done, 1 + n0 + v + 1)
                        pe.wait_ge(res_done, 1 + n0 + v)
                        for k in range(KT):
                            tr = pe.transpose(ps[7][:, k * P:(k + 1) * P], y[:, v % 2, k * P:(k + 1) * P], ident[:, :])
                        tr.then_inc(yT_done, 1)
                    if 0 <= u < TPB:
                        pe.wait_ge(probsT_copied, n0 + u + 1)
                        pe.wait_ge(y_done, 1 + n0 + u)
                        for j in range(HP):
                            mm = pe.matmul(ps[6][:, j * VW:(j + 1) * VW], prT[:, u % 2, j, :],
                                           vblk[:, ds(b, 1), j, :, :].rearrange("p o r c -> p (o r c)"),
                                           start=True, stop=True)
                        mm.then_inc(pv, 1)
                    if 0 <= v < TPB:
                        pe.wait_ge(yT_copied, n0 + v + 1)
                        pe.matmul(ps[7][:, D:2 * D], ones_row[:, :], bias_o[:, :], start=True, stop=False)
                        for k in range(KT):
                            mm = pe.matmul(ps[7][:, D:2 * D], yT[:, v % 2, k, :], w_o[:, k, :],
                                           start=False, stop=(k == KT - 1))
                        mm.then_inc(out_done, 1)

        @block.scalar
        def _(act):
            act.wait_ge(w_in, 16 * len(loads))
            for c in range(KT):
                act.wait_ge(k_done, c + 1)
                act.activation(kT[:, c, :], ps[c][:, 0:B * C], ACT.Identity, bias=bias_k[:, c:c + 1]).then_inc(k_copied, 1)
            act.wait_ge(zeroed, 4)
            for b in range(B):
                act.wait_ge(v_done, b + 1)
                for r in range(2):
                    act.activation(vblk[r * C:(r + 1) * C, b, :, r, 0:DK],
                                   ps[4 + b][r * C:(r + 1) * C, 0:D].rearrange("p (j q d) -> p j q d", q=2, d=DK)[:, :, r, :],
                                   ACT.Identity).then_inc(vblk_done, 1)
            with act.Fori(0, B) as b:
                n0 = b * TPB
                for h in range(2):
                    act.wait_ge(xT_done, 2 * b + h + 1)
                    act.activation(xT[:, :, h * 512:(h + 1) * 512], pz[:, 2 * h:2 * h + 2, :], ACT.Identity).then_inc(xT_copied, 1)
                for c in range(KT):
                    for h in range(2):
                        act.wait_ge(q_done, 4 * b + 2 * c + h + 1)
                        act.activation(qT[:, c, h * 512:(h + 1) * 512], ps[4 + 2 * c + h][:, :], ACT.Identity,
                                       bias=bias_q[:, c:c + 1]).then_inc(q_copied, 1)
                for s in range(TPB + 2):
                    u, v = s - 1, s - 2
                    if 0 <= u < TPB:
                        act.wait_ge(probsT, n0 + u + 1)
                        if u >= 2:
                            act.wait_ge(pv, n0 + u - 1)
                        act.activation(prT[:, u % 2, :, :], pz[:, 4:6, :].rearrange("p q (j n) -> p (q j) n", j=4),
                                       ACT.Identity).then_inc(probsT_copied, 1)
                    if 0 <= v < TPB:
                        act.wait_ge(yT_done, n0 + v + 1)
                        if v >= 2:
                            act.wait_ge(out_done, n0 + v - 1)
                        act.activation(yT[:, v % 2, :, :], ps[7][:, 0:D].rearrange("p (k n) -> p k n", k=KT),
                                       ACT.Identity).then_inc(yT_copied, 1)
                    if s < TPB:
                        act.wait_ge(shifted, n0 + s + 1)
                        act.activation(pr[:, s % 2, :, :], pr[:, s % 2, :, :], ACT.Exp,
                                       scale=float(DK) ** -0.5).then_inc(probs, 1)

        @block.vector
        def _(dve):
            dve.sem_inc(y_done, 1)
            dve.sem_inc(res_done, 1)
            dve.wait_ge(w_in, 16 * len(loads))
            for c in range(KT):
                dve.wait_ge(k_copied, c + 1)
                dve.tensor_tensor(
                    kblk[:, c, :, :].rearrange("p b (h n) -> p b h n", h=8),
                    kT[:, c, :].rearrange("p (b n) -> p b n", b=B).unsqueeze(2).broadcast_to([P, B, 8, C]),
                    mask[:, :].unsqueeze(1).unsqueeze(3).broadcast_to([P, B, 8, C]), ALU.mult).then_inc(kblk_done, 1)
            LINKS = 3 + 2 * TPB
            with dve.Fori(0, B) as b:
                n0 = b * TPB
                ch = Chain(dve, dve_steps, b * LINKS)
                tiles = X[:, ds(n0, TPB), :]
                layer_stats(dve, ch, tiles, stats, mv, spare)
                dve.sem_inc(var_done, 1)
                dve.wait_ge(rstd_done, b + 1)
                for n in range(TPB):
                    tp = dve.tensor_scalar(xs[:, n, :], tiles[:, n, :], mv[:, n, 0:1], rstd[:, n:n + 1],
                                           ALU.subtract, ALU.mult)
                tp.then_inc(xs_done, 1)
                for s in range(TPB + 2):
                    u, v = s - 1, s - 2
                    if s < TPB:
                        dve.wait_ge(scores, n0 + s + 1)
                        sc = pz[:, 2 * (s % 2):2 * (s % 2) + 2, :].rearrange("p q (h n) -> p (q h) n", h=8)
                        ch.link(dve.tensor_reduce(mx[:, s % 2, :], sc, AX.X, ALU.max))
                        if s >= 2:
                            dve.wait_ge(probsT, n0 + s - 1)
                        dve.tensor_tensor(pr[:, s % 2, :, :], sc,
                                          mx[:, s % 2, :].unsqueeze(2).broadcast_to([P, H, C]), ALU.subtract).then_inc(shifted, 1)
                    if 0 <= u < TPB:
                        dve.wait_ge(pv, n0 + u + 1)
                        o = ps[6][:, 0:H * (DK + 1)].rearrange("p (h d) -> p h d", h=H)
                        ch.link(dve.reciprocal(rec[:, u % 2, :], o[:, :, DK]))
                        if u >= 2:
                            dve.wait_ge(yT_done, n0 + u - 1)
                        dve.tensor_tensor(y[:, u % 2, :].rearrange("p (h d) -> p h d", h=H), o[:, :, 0:DK],
                                          rec[:, u % 2, :].unsqueeze(2).broadcast_to([P, H, DK]), ALU.mult).then_inc(y_done, 1)
                    if 0 <= v < TPB:
                        dve.wait_ge(out_done, n0 + v + 1)
                        dve.tensor_tensor(tiles[:, v, :], xs[:, v, :], ps[7][:, D:2 * D], ALU.add).then_inc(res_done, 1)
                dve.wait_ge(res_done, 1 + n0 + TPB)
            assert ch.n == LINKS, ch.n


def project_qkv(nc, ctx, t, dram):
    def sb(name, shape, dt=F32):
        return ctx.enter_context(nc.sbuf_tensor("sb_c_" + name, shape, dt))

    def sem(name):
        return ctx.enter_context(nc.semaphore("c_" + name))

    X, ps, pz, ident, neg_half, v_all = t["X"], t["ps"], t["pz"], t["ident"], t["neg_half"], t["v_all"]
    w = sb("w", [P, KT, 3 * D])
    ln_w = sb("ln_w", [P, KT])
    ln_b = sb("ln_b", [P, KT])
    stats = sb("stats", [P, TPB, 6])
    mv = sb("mv", [P, TPB, 2])
    rstd = sb("rstd", [P, TPB])
    xs = sb("xs", [P, TPB, D])
    xT = sb("xT", [P, KT, S])
    parts = sb("parts", [P, 2, 3, S], BF16)
    rest = sb("rest", [P, 2, S])
    w_in, dve_steps = sem("w_in"), sem("dve_steps")
    spare = sem("spare")
    var_done, rstd_done, xs_done, xT_done, xT_copied = (sem(n) for n in (
        "var_done", "rstd_done", "xs_done", "xT_done", "xT_copied"))
    qk_done, high_done, rest_done, mid_done, low_done = (sem(n) for n in (
        "qk_done", "high_done", "rest_done", "mid_done", "low_done"))
    stored = [sem("stored0"), sem("stored1")]
    v_done, v_copied = sem("v_done"), sem("v_copied")
    U = 2 * KT
    loads = [(w[:, :, :], dram["w_qkv"].rearrange("(k p) n -> p k n", p=P)),
             (ln_w[:, :], dram["ln1_w"]), (ln_b[:, :], dram["ln1_b"])]

    with nc.Block() as block:
        @block.sync
        def _(sp):
            for q in stored:
                sp.sem_inc(q, 16)
            for dst, src in loads:
                sp.dma_start(dst, src).then_inc(w_in, 16)
            with sp.Fori(0, B) as b:
                for u in range(U):
                    dst = (dram["q_parts"], dram["k_parts"])[u // KT]
                    sp.wait_ge(high_done, U * b + u + 1)
                    sp.wait_ge(mid_done, U * b + u + 1)
                    sp.wait_ge(low_done, U * b + u + 1)
                    for i in range(3):
                        sp.dma_start(dst[i, ds(b * D + (u % KT) * P, P), :], parts[:, u % 2, i, :]).then_inc(stored[u % 2], 16)
            for q in stored:
                sp.wait_ge(q, 16 + 3 * 16 * B * U // 2)

        @block.gpsimd
        def _(pool):
            with pool.Fori(0, B) as b:
                for r in range(2):
                    pool.wait_ge(var_done, 2 * b + r + 1)
                    pool.tensor_tensor(rstd[:, :], mv[:, :, 1], neg_half[:, :], ALU.pow).then_inc(rstd_done, 1)
                for u in range(U):
                    pool.wait_ge(rest_done, 1 + U * b + u + 1)
                    pool.wait_ge(stored[u % 2], 16 + 48 * (U // 2 * b + u // 2))
                    alone(pool, spare)
                    pool.tensor_copy(parts[:, u % 2, 1, :], rest[:, u % 2, :]).then_inc(mid_done, 1)
                    pool.wait_ge(mid_done, U * b + u + 1)
                    pool.tensor_tensor(parts[:, u % 2, 2, :], rest[:, u % 2, :], parts[:, u % 2, 1, :],
                                       ALU.subtract).then_inc(low_done, 1)

        @block.tensor
        def _(pe):
            pe.wait_ge(w_in, 16 * len(loads))
            with pe.Fori(0, B) as b:
                pe.wait_ge(xs_done, 2 * (b + 1))
                pe.wait_ge(v_copied, 1 + TPB // 2 * b)
                for n in range(TPB):
                    for k in range(KT):
                        tr = pe.transpose(ps[2 * (n // 4) + k][:, n % 4 * P:(n % 4 + 1) * P],
                                          xs[:, n, k * P:(k + 1) * P], ident[:, :])
                    if n % 4 == 3:
                        tr.then_inc(xT_done, 1)
                pe.wait_ge(xT_copied, 4 * (b + 1))
                for u in range(U):
                    if u >= 2:
                        pe.wait_ge(rest_done, 1 + U * b + u - 1)
                    else:
                        pe.wait_ge(rest_done, 1 + U * b)
                    for h in range(2):
                        for k in range(KT):
                            mm = pe.matmul(ps[4 + 2 * (u % 2) + h][:, :], w[:, k, u * P:(u + 1) * P],
                                           xT[:, k, h * 512:(h + 1) * 512], start=(k == 0), stop=(k == KT - 1))
                    mm.then_inc(qk_done, 1)
                for n in range(TPB // 2):
                    for r in range(2):
                        i = 2 * n + r
                        for k in range(KT):
                            mm = pe.matmul(ps[n][:, r * D:(r + 1) * D], xT[:, k, i * P:(i + 1) * P],
                                           w[:, k, 2 * D:3 * D], start=(k == 0), stop=(k == KT - 1))
                    mm.then_inc(v_done, 1)

        @block.scalar
        def _(act):
            act.sem_inc(v_copied, 1)
            act.wait_ge(w_in, 16 * len(loads))
            with act.Fori(0, B) as b:
                for h in range(2):
                    act.wait_ge(xT_done, 2 * b + h + 1)
                    for k in range(KT):
                        act.activation(xT[:, k, h * 512:(h + 1) * 512], ps[2 * h + k][:, :], ACT.Identity,
                                       bias=ln_b[:, k:k + 1], scale=ln_w[:, k:k + 1]).then_inc(xT_copied, 1)
                for u in range(U):
                    act.wait_ge(qk_done, U * b + u + 1)
                    act.wait_ge(stored[u % 2], 16 + 48 * (U // 2 * b + u // 2))
                    act.activation(parts[:, u % 2, 0, :], pz[:, 4 + 2 * (u % 2):6 + 2 * (u % 2), :].rearrange("p q n -> p (q n)"),
                                   ACT.Identity, scale=float(DK) ** -0.5 if u < KT else 1.0).then_inc(high_done, 1)
                for n in range(TPB // 2):
                    act.wait_ge(v_done, TPB // 2 * b + n + 1)
                    act.activation(v_all[:, ds(b * H, H), 2 * n:2 * n + 2, :],
                                   ps[n][:, :].rearrange("p (r h d) -> p h r d", r=2, h=H), ACT.Identity).then_inc(v_copied, 1)

        @block.vector
        def _(dve):
            dve.sem_inc(rest_done, 1)
            LINKS = 6
            with dve.Fori(0, B) as b:
                ch = Chain(dve, dve_steps, b * LINKS)
                tiles = X[:, ds(b * TPB, TPB), :]
                for r in range(2):
                    layer_stats(dve, ch, tiles, stats, mv, spare)
                    dve.sem_inc(var_done, 1)
                    dve.wait_ge(rstd_done, 2 * b + r + 1)
                    for n in range(TPB):
                        tp = dve.tensor_scalar((tiles, xs)[r][:, n, :], tiles[:, n, :], mv[:, n, 0:1], rstd[:, n:n + 1],
                                               ALU.subtract, ALU.mult)
                    tp.then_inc(xs_done, 1)
                    dve.wait_ge(xs_done, 2 * b + r + 1)
                for u in range(U):
                    dve.wait_ge(high_done, U * b + u + 1)
                    if u >= 2:
                        dve.wait_ge(low_done, U * b + u - 1)
                    dve.scalar_tensor_tensor(out=rest[:, u % 2, :],
                                             in0=pz[:, 4 + 2 * (u % 2):6 + 2 * (u % 2), :].rearrange("p q n -> p (q n)"),
                                             scalar=float(DK) ** -0.5 if u < KT else 1.0, in1=parts[:, u % 2, 0, :],
                                             op0=ALU.mult, op1=ALU.subtract).then_inc(rest_done, 1)
                dve.wait_ge(low_done, U * (b + 1))
            assert ch.n == LINKS, ch.n


def self_attention(nc, ctx, t, dram):
    def sb(name, shape, dt=F32):
        return ctx.enter_context(nc.sbuf_tensor("sb_m_" + name, shape, dt))

    def sem(name):
        return ctx.enter_context(nc.semaphore("m_" + name))

    ps, ident, v_all, y_all = t["ps"], t["ident"], t["v_all"], t["y_all"]
    HEADS = B * H
    R = 6 * DK
    NB = 4
    q_s = sb("q", [R + 3, NB, S], BF16)
    k_s = sb("k", [R + 3, NB, S], BF16)
    v_s = sb("v", [P, 2, TPB, 32])
    pT = sb("pT", [P, 4, S])
    mx2 = sb("mx2", [P, 2, TPB, 2])
    neg_mx = sb("neg_mx", [P, 2, TPB])
    mxT = sb("mxT", [TPB, P])
    mx_rest = sb("mx_rest", [TPB, P])
    mx_parts = sb("mx_parts", [TPB, 2, 3, P], BF16)
    y_raw = sb("y_raw", [P, 256])
    rec = sb("rec", [P, 8])

    q_in = [sem(f"qk_in{i}") for i in range(NB)]
    max_in = [sem(f"max_in{i}") for i in range(NB)]
    set_up, v_in, scores1, maxed, neg_done, mxT_done, mxT_read, split_done = (sem(n) for n in (
        "set_up", "v_in", "scores1", "maxed", "neg_done", "mxT_done", "mxT_read", "split_done"))
    y_rec, spare = sem("y_rec"), sem("spare")
    scores2, exped, pv, y_copied, yT_done, y_stored, dve_steps = (sem(n) for n in (
        "scores2", "exped", "pv", "y_copied", "yT_done", "y_stored", "dve_steps"))
    LINKS1 = 3

    def slots(eng, body):
        for s in range(NB):
            body(s, s, s // NB, 0)
        with eng.Fori(1, HEADS // NB) as it:
            for q in range(NB):
                body(it * NB + q, q, it, None)
        for s in range(HEADS, HEADS + 3):
            body(s, s % NB, s // NB, HEADS)

    def has(s, lag, edge):
        return edge is None or 0 <= s - lag < HEADS

    def turn(par, it, lag):
        return (par - lag) % NB, it + 1 - (1 if par < lag else 0)

    with nc.Block() as block:
        @block.sync
        def _(sp):
            def load(g, i):
                for dst, src, rows in ((q_s, "q_parts", ((0, 3), (0, 2), (0, 1))), (k_s, "k_parts", (0, 1, 2))):
                    at = 0
                    for n, r in zip((3, 2, 1), rows):
                        for j in range(n):
                            part = (r[0] + j) if src == "q_parts" else r
                            sp.dma_start(dst[at:at + DK, i, :], dram[src][part, ds(g * DK, DK), :]).then_inc(q_in[i], 16)
                            at += DK

            load(0, 0)

            def slot(s, par, it, edge):
                if has(s, -1, edge):
                    if not (edge == 0 and s + 1 < NB):
                        sp.wait_ge(scores2, 2 * TPB * (s + 2 - NB))
                    load(s + 1, (par + 1) % NB)
                if has(s, 1, edge):
                    i, _ = turn(par, it, 1)
                    sp.wait_ge(split_done, s)
                    for r in range(3):
                        sp.dma_start(q_s[R + r:R + r + 1, i, :].rearrange("o (t n) -> o t n", t=TPB),
                                     mx_parts[:, (par - 1) % 2, r, :]).then_inc(max_in[i], 16)

            for s in range(NB):
                slot(s, s, 0, 0)
            with sp.Fori(1, HEADS // NB - 1) as it:
                for q in range(NB):
                    slot(it * NB + q, q, it, None)
            for s in range(HEADS - NB, HEADS + 3):
                slot(s, s % NB, s // NB, HEADS)

        @block.gpsimd
        def _(pool):
            pool.memset(v_s[:, :, :, DK + 1:32], 0.0).then_inc(set_up, 1)
            pool.memset(v_s[:, :, :, DK:DK + 1], 1.0).then_inc(set_up, 1)
            pool.wait_ge(set_up, 3)

            def slot(s, par, it, edge):
                if has(s, 2, edge):
                    if not (edge == 0 and s - 4 < 0):
                        pool.wait_ge(pv, TPB * (s - 3))
                    alone(pool, spare)
                    pool.tensor_copy(v_s[:, par % 2, :, 0:DK],
                                     v_all[:, ds(s - 2, 1), :, :].rearrange("p o n d -> p (o n) d")).then_inc(v_in, 1)

            slots(pool, slot)

        @block.tensor
        def _(pe):
            pe.wait_ge(set_up, 3)

            def sums(e, par2, m, edge_first):
                if m == 0 and not edge_first:
                    pe.wait_ge(y_copied, e)
                pe.wait_ge(exped, 2 * TPB * e + 2 * (m + 1))
                for j in range(4):
                    mm = pe.matmul(ps[6][32 * j:32 * j + 32, 0:256], v_s[:, par2, m, :],
                                   pT[:, m % 4, j * 256:(j + 1) * 256], start=(m == 0), stop=(m == TPB - 1),
                                   skip_group_check=True)
                mm.then_inc(pv, 1)

            def slot(s, par, it, edge):
                one, two, three = has(s, 0, edge), has(s, 2, edge), has(s, 3, edge)
                if one:
                    i, use = turn(par, it, 0)
                    pe.wait_ge(q_in[i], 12 * 16 * use)
                if two:
                    i2, use2 = turn(par, it, 2)
                for k in range(TPB):
                    if one:
                        for h in range(2):
                            j = 2 * k + h
                            if j == 0:
                                pe.wait_ge(maxed, 2 * TPB * s)
                            elif j >= 3:
                                pe.wait_ge(maxed, 2 * TPB * s + j - 2)
                            pe.matmul(ps[j % 3][:, :], q_s[0:R, i, k * P:(k + 1) * P],
                                      k_s[0:R, i, h * 512:(h + 1) * 512], start=True, stop=True).then_inc(scores1, 1)
                    if two:
                        e = s - 2
                        if k == 0:
                            pe.wait_ge(max_in[i2], 48 * use2)
                            pe.wait_ge(v_in, e + 1)
                        for h in range(2):
                            j = 2 * k + h
                            if j == 0:
                                pe.wait_ge(exped, 2 * TPB * e)
                            elif j >= 3:
                                pe.wait_ge(exped, 2 * TPB * e + j - 2)
                            mm = pe.matmul(ps[3 + j % 3][:, :], k_s[:, i2, k * P:(k + 1) * P],
                                           q_s[:, i2, h * 512:(h + 1) * 512], start=True, stop=True)
                            mm.then_inc(scores2, 1)
                    if k < 2:
                        if three:
                            sums(s - 3, (par - 3) % 2, TPB - 2 + k, False)
                    elif two:
                        sums(s - 2, par % 2, k - 2, edge == 0 and s == 2)
                    if k == 1 and has(s, 1, edge):
                        pe.wait_ge(neg_done, s)
                        if not (edge == 0 and s < 4):
                            pe.wait_ge(y_stored, s - 3)
                        pe.transpose(ps[7][0:TPB, 0:P], neg_mx[:, (par - 1) % 2, :], ident[:, :]).then_inc(mxT_done, 1)
                    if k == 4 and three:
                        pe.wait_ge(y_copied, s - 2)
                        if has(s, 1, edge):
                            pe.wait_ge(mxT_read, s)
                        else:
                            pe.wait_ge(y_stored, s - 3)
                        for r in range(2):
                            tr = pe.transpose(ps[7][:, r * P:(r + 1) * P], y_raw[:, r * P:(r + 1) * P], ident[:, :])
                        tr.then_inc(yT_done, 1)

            slots(pe, slot)

        @block.scalar
        def _(act):
            def slot(s, par, it, edge):
                two, three = has(s, 2, edge), has(s, 3, edge)
                for k in range(TPB):
                    if two:
                        e = s - 2
                        for h in range(2):
                            j = 2 * k + h
                            act.wait_ge(scores2, 2 * TPB * e + j + 1)
                            if h == 0 and not (edge == 0 and s == 2 and k < 4):
                                act.wait_ge(pv, TPB * e + k - 3)
                            act.activation(pT[:, k % 4, h * 512:(h + 1) * 512], ps[3 + j % 3][:, :],
                                           ACT.Exp).then_inc(exped, 1)
                    if k == 1 and three:
                        act.wait_ge(pv, TPB * (s - 2))
                        if not (edge == 0 and s == 3):
                            act.wait_ge(yT_done, s - 3)
                        act.activation(y_raw[:, :], ps[6][:, 0:256], ACT.Identity).then_inc(y_copied, 1)

            slots(act, slot)

        @block.vector
        def _(dve):
            dve.memset(k_s[R:R + 3, :, :], 1.0).then_inc(set_up, 1)

            def slot(s, par, it, edge):
                one, three = has(s, 0, edge), has(s, 3, edge)
                for k in range(TPB):
                    if one:
                        for h in range(2):
                            j = 2 * k + h
                            dve.wait_ge(scores1, 2 * TPB * s + j + 1)
                            dve.tensor_reduce(mx2[:, par % 2, k, h:h + 1], ps[j % 3][:, :], AX.X, ALU.max).then_inc(maxed, 1)
                    if k == 1 and has(s, 1, edge):
                        c = Chain(dve, dve_steps, (s - 1) * LINKS1)
                        mp = mx_parts[:, (par - 1) % 2, :, :]
                        i, use = turn(par, it, 3)
                        dve.wait_ge(mxT_done, s)
                        dve.tensor_copy(mxT[:, :], ps[7][0:TPB, 0:P]).then_inc(mxT_read, 1)
                        if not (edge == 0 and s < 3):
                            dve.wait_ge(max_in[i], 48 * use)
                        dve.wait_ge(mxT_read, s)
                        c.link(dve.tensor_copy(mp[:, 0, :], mxT[:, :]))
                        c.link(dve.tensor_tensor(mx_rest[:, :], mxT[:, :], mp[:, 0, :], ALU.subtract))
                        c.link(dve.tensor_copy(mp[:, 1, :], mx_rest[:, :]))
                        dve.tensor_tensor(mp[:, 2, :], mx_rest[:, :], mp[:, 1, :], ALU.subtract).then_inc(split_done, 1)
                    if k == 4 and three:
                        dve.wait_ge(yT_done, s - 2)
                        yt = ps[7][:, 0:256].rearrange("p (r j d) -> p j r d", r=2, j=4)
                        dve.reciprocal(rec[:, :].rearrange("p (j r) -> p j r", j=4), yt[:, :, :, DK]).then_inc(y_rec, 1)
                        dve.wait_ge(y_rec, s - 2)
                        dve.tensor_tensor(
                            y_all[:, ds(s - 3, 1), :, :].rearrange("p o (j r) d -> p (o j) r d", j=4), yt[:, :, :, 0:DK],
                            rec[:, :].rearrange("p (j r) -> p j r", j=4).unsqueeze(3).broadcast_to([P, 4, 2, DK]),
                            ALU.mult).then_inc(y_stored, 1)
                if one:
                    dve.wait_ge(maxed, 2 * TPB * (s + 1))
                    dve.tensor_reduce(neg_mx[:, par % 2, :], mx2[:, par % 2, :, :], AX.X, ALU.max,
                                      negate=True).then_inc(neg_done, 1)

            slots(dve, slot)


def gate(nc, ctx, t, dram):
    def sb(name, shape, dt=F32):
        return ctx.enter_context(nc.sbuf_tensor("sb_g_" + name, shape, dt))

    def sem(name):
        return ctx.enter_context(nc.semaphore("g_" + name))

    X, Z, ps, pz, ident, neg_half, y_all, logits = (t[n] for n in (
        "X", "Z", "ps", "pz", "ident", "neg_half", "y_all", "logits"))
    E = dram["gate_w"].shape[1]
    w = sb("w", [P, KT, D])
    w_gate = sb("w_gate", [P, KT, E])
    b_gate = sb("b_gate", [1, E])
    ln_w = sb("ln_w", [P, KT])
    ln_b = sb("ln_b", [P, KT])
    ones_row = sb("ones_row", [1, P])
    zeros = sb("zeros", [P, D])
    stats = sb("stats", [P, TPB, 6])
    mv = sb("mv", [P, TPB, 2])
    rstd = sb("rstd", [P, TPB])
    ys = sb("ys", [P, TPB, D])
    x3 = sb("x3", [P, TPB, D])
    yT = sb("yT", [P, KT, S])
    zs = sb("zs", [P, TPB, D])
    zT = sb("zT", [P, KT, S])
    w_in, dve_steps, ready, cleared = sem("w_in"), sem("dve_steps"), sem("ready"), sem("cleared")
    ys_done, yT_done, yT_copied, out_done, res_done = (sem(n) for n in (
        "ys_done", "yT_done", "yT_copied", "out_done", "res_done"))
    spare, x3_added = sem("spare"), sem("x3_added")
    var_done, rstd_done, zs_done, z_kept, zT_done, zT_copied, logits_done, logits_copied = (sem(n) for n in (
        "var_done", "rstd_done", "zs_done", "z_kept", "zT_done", "zT_copied", "logits_done", "logits_copied"))
    loads = [(w[:, :, :], dram["w_proj"].rearrange("(k p) n -> p k n", p=P)),
             (w_gate[:, :, :], dram["gate_w"].rearrange("(k p) n -> p k n", p=P)),
             (b_gate[:, :], dram["gate_b"]), (ln_w[:, :], dram["ln2_w"]), (ln_b[:, :], dram["ln2_b"])]

    with nc.Block() as block:
        @block.sync
        def _(sp):
            for dst, src in loads:
                sp.dma_start(dst, src).then_inc(w_in, 16)
            sp.wait_ge(ready, 2)
            sp.dma_start(dram["sorted"].rearrange("(j p) d -> p j d", p=P),
                         zeros[:, :].unsqueeze(1).broadcast_to([P, dram["sorted"].shape[0] // P, D])).then_inc(cleared, 16)
            sp.wait_ge(cleared, 16)

        @block.gpsimd
        def _(pool):
            pool.sem_inc(z_kept, 1)
            pool.memset(ones_row[:, :], 1.0).then_inc(ready, 1)
            pool.memset(zeros[:, :], 0.0).then_inc(ready, 1)
            pool.wait_ge(ready, 2)
            with pool.Fori(0, B) as b:
                pool.wait_ge(yT_done, 1 + 2 * b)
                alone(pool, spare)
                pool.tensor_copy(ys[:, :, :].rearrange("p n (h d) -> p h n d", h=H), y_all[:, ds(b * H, H), :, :]).then_inc(ys_done, 1)
                pool.wait_ge(var_done, b + 1)
                pool.tensor_tensor(rstd[:, :], mv[:, :, 1], neg_half[:, :], ALU.pow).then_inc(rstd_done, 1)
                pool.wait_ge(zs_done, b + 1)
                alone(pool, spare)
                pool.tensor_copy(Z[:, ds(b * TPB, TPB), :], zs[:, :, :]).then_inc(z_kept, 1)
                pool.tensor_tensor(X[:, ds(b * TPB, TPB), :], X[:, ds(b * TPB, TPB), :], x3[:, :, :], ALU.add).then_inc(x3_added, 1)

        @block.tensor
        def _(pe):
            pe.sem_inc(yT_done, 1)
            pe.wait_ge(w_in, 16 * len(loads))
            pe.wait_ge(ready, 2)
            with pe.Fori(0, B) as b:
                pe.wait_ge(ys_done, b + 1)
                pe.wait_ge(zT_copied, 1 + 4 * b)
                for n in range(TPB):
                    for k in range(KT):
                        tr = pe.transpose(ps[2 * (n // 4) + k][:, n % 4 * P:(n % 4 + 1) * P],
                                          ys[:, n, k * P:(k + 1) * P], ident[:, :])
                    if n % 4 == 3:
                        tr.then_inc(yT_done, 1)
                pe.wait_ge(yT_copied, 2 * (b + 1))
                pe.wait_ge(logits_copied, 1 + b)
                for n in range(TPB):
                    for k in range(KT):
                        mm = pe.matmul(ps[4 + n // 2][:, n % 2 * D:(n % 2 + 1) * D], yT[:, k, n * P:(n + 1) * P],
                                       w[:, k, :], start=(k == 0), stop=(k == KT - 1))
                    if n % 2 == 1:
                        mm.then_inc(out_done, 1)
                pe.wait_ge(zs_done, b + 1)
                for n in range(TPB):
                    for k in range(KT):
                        tr = pe.transpose(ps[2 * (n // 4) + k][:, n % 4 * P:(n % 4 + 1) * P],
                                          zs[:, n, k * P:(k + 1) * P], ident[:, :])
                    if n % 4 == 3:
                        tr.then_inc(zT_done, 1)
                pe.wait_ge(zT_copied, 1 + 4 * (b + 1))
                for n in range(TPB):
                    pe.matmul(ps[4][:, n * E:(n + 1) * E], ones_row[:, :], b_gate[:, :], start=True, stop=False)
                    for k in range(KT):
                        mm = pe.matmul(ps[4][:, n * E:(n + 1) * E], zT[:, k, n * P:(n + 1) * P], w_gate[:, k, :],
                                       start=False, stop=(k == KT - 1))
                mm.then_inc(logits_done, 1)

        @block.scalar
        def _(act):
            act.sem_inc(logits_copied, 1)
            act.sem_inc(zT_copied, 1)
            act.wait_ge(w_in, 16 * len(loads))
            with act.Fori(0, B) as b:
                for h in range(2):
                    act.wait_ge(yT_done, 1 + 2 * b + h + 1)
                    act.activation(yT[:, :, h * 512:(h + 1) * 512], pz[:, 2 * h:2 * h + 2, :], ACT.Identity).then_inc(yT_copied, 1)
                for h in range(2):
                    act.wait_ge(zT_done, 2 * b + h + 1)
                    for k in range(KT):
                        act.activation(zT[:, k, h * 512:(h + 1) * 512], ps[2 * h + k][:, :], ACT.Identity,
                                       bias=ln_b[:, k:k + 1], scale=ln_w[:, k:k + 1]).then_inc(zT_copied, 1)
                act.wait_ge(logits_done, b + 1)
                act.activation(logits[:, ds(b * TPB, TPB), :], ps[4][:, 0:TPB * E].rearrange("p (n e) -> p n e", n=TPB),
                               ACT.Identity).then_inc(logits_copied, 1)

        @block.vector
        def _(dve):
            LINKS = 3
            with dve.Fori(0, B) as b:
                ch = Chain(dve, dve_steps, b * LINKS)
                tiles = X[:, ds(b * TPB, TPB), :]
                for n in range(TPB // 2):
                    dve.wait_ge(out_done, TPB // 2 * b + n + 1)
                    dve.tensor_tensor(x3[:, 2 * n:2 * n + 2, :], tiles[:, 2 * n:2 * n + 2, :],
                                      ps[4 + n][:, :].rearrange("p (r d) -> p r d", r=2), ALU.add).then_inc(res_done, 1)
                dve.wait_ge(res_done, TPB // 2 * (b + 1))
                layer_stats(dve, ch, x3, stats, mv, spare)
                dve.sem_inc(var_done, 1)
                dve.wait_ge(rstd_done, b + 1)
                dve.wait_ge(z_kept, 1 + b)
                for n in range(TPB):
                    tp = dve.tensor_scalar(zs[:, n, :], x3[:, n, :], mv[:, n, 0:1], rstd[:, n:n + 1],
                                           ALU.subtract, ALU.mult)
                tp.then_inc(zs_done, 1)
                dve.wait_ge(x3_added, b + 1)
            assert ch.n == LINKS, ch.n


def route(nc, ctx, t, dram):
    def sb(name, shape, dt=F32):
        return ctx.enter_context(nc.sbuf_tensor("sb_r_" + name, shape, dt))

    def sem(name):
        return ctx.enter_context(nc.semaphore("r_" + name))

    ps, logits, dest, owner, Z = (t[n] for n in ("ps", "logits", "dest", "owner", "Z"))
    E = dram["gate_w"].shape[1]
    J = dram["sorted"].shape[0] // P
    before = sb("before", [P, P])
    every = sb("every", [P, P])
    prefer = sb("prefer", [P, E])
    starts = sb("starts", [P, NT])
    block_no = sb("block_no", [1, J])
    best = sb("best", [P, NT])
    hot = sb("hot", [P, NT, E])
    rank = sb("rank", [P, NT])
    ranked = sb("ranked", [P, NT, E])
    total = sb("total", [P, E, NT])
    until = sb("until", [P, E, NT])
    place = sb("place", [P, E, NT])
    wide = sb("wide", [P, E, NT])
    blocks = sb("blocks", [P, E])
    blocks_until = sb("blocks_until", [P, E])
    base = sb("base", [P, E])
    row = sb("row", [P, NT])
    reached = sb("reached", [1, J, E])
    owner_f = sb("owner_f", [1, J])
    w_in, ones_set, hot_done, counted, steps, dest_done, scattered = (sem(n) for n in (
        "w_in", "ones_set", "hot_done", "counted", "steps", "dest_done", "scattered"))
    loads = [(before[:, :], dram["before"]), (prefer[:, :], dram["prefer"]), (starts[:, :], dram["starts"]),
             (block_no[:, :], dram["block_no"])]

    with nc.Block() as block:
        @block.sync
        def _(sp):
            for dst, src in loads:
                sp.dma_start(dst, src).then_inc(w_in, 16)

        @block.gpsimd
        def _(pool):
            pool.memset(every[:, :], 1.0).then_inc(ones_set, 1)
            pool.wait_ge(dest_done, 1)
            for n in range(NT):
                pool.indirect_dma_start(dram["sorted"], bass.IndirectOffsetOnAxis(ap=dest[:, n:n + 1], axis=0),
                                        Z[:, n, :], None).then_inc(scattered, 16)
            pool.wait_ge(scattered, 16 * NT)

        @block.tensor
        def _(pe):
            pe.wait_ge(w_in, 16 * len(loads))
            pe.wait_ge(ones_set, 1)
            pe.wait_ge(hot_done, 1)
            flat = hot[:, :, :].rearrange("p n e -> p (n e)")
            pe.matmul(ps[0][:, 0:NT * E], before[:, :], flat, start=True, stop=True).then_inc(counted, 1)
            pe.matmul(ps[1][:, 0:NT * E], every[:, :], flat, start=True, stop=True).then_inc(counted, 1)

        @block.vector
        def _(dve):
            dve.wait_ge(w_in, 16 * len(loads))
            ch = Chain(dve, steps)

            def over_e(ap):
                return ap.unsqueeze(2).broadcast_to([P, NT, E])

            ch.link(dve.tensor_reduce(best[:, :], logits[:, :, :], AX.X, ALU.max))
            ch.link(dve.tensor_tensor(hot[:, :, :], logits[:, :, :], over_e(best[:, :]), ALU.is_equal))
            ch.link(dve.tensor_tensor(ranked[:, :, :], hot[:, :, :],
                                      prefer[:, :].unsqueeze(1).broadcast_to([P, NT, E]), ALU.mult))
            ch.link(dve.tensor_reduce(rank[:, :], ranked[:, :, :], AX.X, ALU.max))
            dve.tensor_tensor(hot[:, :, :], over_e(rank[:, :]),
                              prefer[:, :].unsqueeze(1).broadcast_to([P, NT, E]), ALU.is_equal).then_inc(hot_done, 1)
            dve.wait_ge(hot_done, 1)
            dve.wait_ge(counted, 2)
            ch.link(dve.tensor_copy(total[:, :, :], ps[1][:, 0:NT * E].rearrange("p (n e) -> p e n", e=E)))
            for e in range(E):
                sc = dve.tensor_tensor_scan(until[:, e, :], every[:, 0:NT], total[:, e, :], 0.0, ALU.mult, ALU.add)
            ch.link(sc)
            ch.link(dve.tensor_tensor(place[:, :, :], until[:, :, :], total[:, :, :], ALU.subtract))
            ch.link(dve.tensor_tensor(place[:, :, :], place[:, :, :],
                                      ps[0][:, 0:NT * E].rearrange("p (n e) -> p e n", e=E), ALU.add))
            ch.link(dve.tensor_tensor(wide[:, :, :], until[:, :, NT - 1:NT].broadcast_to([P, E, NT]),
                                      starts[:, :].unsqueeze(1).broadcast_to([P, E, NT]), ALU.is_gt))
            ch.link(dve.tensor_reduce(blocks[:, :], wide[:, :, :], AX.X, ALU.add))
            ch.link(dve.tensor_tensor_scan(blocks_until[:, :], every[:, 0:E], blocks[:, :], 0.0, ALU.mult, ALU.add))
            ch.link(dve.tensor_tensor(base[:, :], blocks_until[:, :], blocks[:, :], ALU.subtract))
            ch.link(dve.tensor_scalar(base[:, :], base[:, :], float(P), None, ALU.mult))
            ch.link(dve.tensor_tensor(place[:, :, :], place[:, :, :],
                                      base[:, :].unsqueeze(2).broadcast_to([P, E, NT]), ALU.add))
            ch.link(dve.tensor_tensor(ranked[:, :, :], place[:, :, :].rearrange("p e n -> p n e"), hot[:, :, :], ALU.mult))
            ch.link(dve.tensor_reduce(row[:, :], ranked[:, :, :], AX.X, ALU.add))
            dve.tensor_copy(dest[:, :], row[:, :]).then_inc(dest_done, 1)
            ch.link(dve.tensor_tensor(reached[:, :, :], blocks_until[0:1, :].unsqueeze(1).broadcast_to([1, J, E]),
                                      block_no[:, :].unsqueeze(2).broadcast_to([1, J, E]), ALU.is_le))
            ch.link(dve.tensor_reduce(owner_f[:, :], reached[:, :, :], AX.X, ALU.add))
            ch.link(dve.tensor_scalar(owner_f[:, :], owner_f[:, :], float(E - 1), None, ALU.min))
            ch.link(dve.tensor_copy(owner[:, :], owner_f[:, :]))


def experts(nc, ctx, t, dram):
    def sb(name, shape, dt=F32):
        return ctx.enter_context(nc.sbuf_tensor("sb_e_" + name, shape, dt))

    def sem(name):
        return ctx.enter_context(nc.semaphore("e_" + name))

    ps, pz, ident, owner = (t[n] for n in ("ps", "pz", "ident", "owner"))
    E, _, HID = dram["w1"].shape
    HT = HID // P
    J = dram["sorted"].shape[0] // P
    W = 3
    assert J % W == 0
    w1 = sb("w1", [P, W, KT, HID])
    w2 = sb("w2", [P, E, HT, D])
    ln_w = sb("ln_w", [P, KT])
    ln_b = sb("ln_b", [P, KT])
    x_in = sb("x_in", [P, W, D])
    xT = sb("xT", [P, W, KT, P])
    hT = sb("hT", [P, W, HT, P])
    y = sb("y", [P, W, D])
    w2_in, ln_in = sem("w2_in"), sem("ln_in")
    rows_in = [sem(f"rows_in{i}") for i in range(W)]
    w1_in = [sem(f"w1_in{i}") for i in range(W)]
    stored = [sem(f"stored{i}") for i in range(W)]
    xT_done, xT_copied, h_done, h_copied, y_done, y_copied = (sem(n) for n in (
        "xT_done", "xT_copied", "h_done", "h_copied", "y_done", "y_copied"))
    rows = dram["sorted"].rearrange("(j p) d -> j p d", p=P)
    rows_out = dram["sorted_out"].rearrange("(j p) d -> j p d", p=P)

    with nc.Block() as block:
        @block.sync
        def _(sp):
            for q in stored:
                sp.sem_inc(q, 16)
            sp.dma_start(ln_w[:, :], dram["ln2_w"]).then_inc(ln_in, 16)
            sp.dma_start(ln_b[:, :], dram["ln2_b"]).then_inc(ln_in, 16)

            def load(j, q, first):
                if not first:
                    sp.wait_ge(xT_done, j - W + 1)
                sp.dma_start(x_in[:, q, :], rows[ds(j, 1), :, :].rearrange("o p d -> p (o d)")).then_inc(rows_in[q], 16)
                e = sp.value_load(owner[0:1, ds(j, 1)], min_val=0, max_val=E - 1)
                if not first:
                    sp.wait_ge(h_done, 2 * (j - W + 1))
                sp.dma_start(w1[:, q, :, :], dram["w1"][ds(e, 1), :, :].rearrange("o (k p) n -> p (o k) n", p=P)).then_inc(w1_in[q], 16)

            for q in range(W):
                load(q, q, True)
                if q == 0:
                    for e in range(E):
                        sp.dma_start(w2[:, e, :, :], dram["w2"][e].rearrange("(k p) n -> p k n", p=P)).then_inc(w2_in, 16)

            def store(j, q):
                sp.wait_ge(y_copied, 1 + j + 1)
                sp.dma_start(rows_out[ds(j, 1), :, :].rearrange("o p d -> p (o d)"), y[:, q, :]).then_inc(stored[q], 16)

            with sp.Fori(1, J // W) as it:
                for q in range(W):
                    store(it * W + q - W, q)
                    load(it * W + q, q, False)
            for q in range(W):
                store(J - W + q, q)
            for q in range(W):
                sp.wait_ge(stored[q], 16 + 16 * (J // W))

        @block.tensor
        def _(pe):
            def turn(j, it, q):
                pe.wait_ge(rows_in[q], 16 * (it + 1))
                pe.wait_ge(xT_copied, 2 * j)
                for k in range(KT):
                    tr = pe.transpose(ps[7][:, k * P:(k + 1) * P], x_in[:, q, k * P:(k + 1) * P], ident[:, :])
                tr.then_inc(xT_done, 1)

            def up(j, it, q):
                pe.wait_ge(xT_copied, 2 * (j + 1))
                pe.wait_ge(w1_in[q], 16 * (it + 1))
                for m in range(HT):
                    for k in range(KT):
                        mm = pe.matmul(ps[2 * q + m // 4][:, m % 4 * P:(m % 4 + 1) * P],
                                       w1[:, q, k, m * P:(m + 1) * P], xT[:, q, k, :], start=(k == 0), stop=(k == KT - 1))
                    if m % 4 == 3:
                        mm.then_inc(h_done, 1)

            def down(j, q):
                e = pe.value_load(owner[0:1, ds(j, 1)], min_val=0, max_val=E - 1)
                pe.wait_ge(y_copied, 1 + j)
                for m in range(HT):
                    if m % 4 == 0:
                        pe.wait_ge(h_copied, 2 * j + m // 4 + 1)
                    mm = pe.matmul(ps[6][:, 0:D], hT[:, q, m, :],
                                   w2[:, ds(e, 1), m, :].rearrange("p o n -> p (o n)"), start=(m == 0), stop=(m == HT - 1))
                mm.then_inc(y_done, 1)

            turn(0, 0, 0)
            up(0, 0, 0)
            turn(1, 0, 1)
            pe.wait_ge(w2_in, 16 * E)
            with pe.Fori(0, J // W - 1) as it:
                for q in range(W):
                    j = it * W + q
                    up(j + 1, it + (q + 1) // W, (q + 1) % W)
                    turn(j + 2, it + (q + 2) // W, (q + 2) % W)
                    down(j, q)
            for q in range(W):
                j = J - W + q
                if j + 1 < J:
                    up(j + 1, J // W - 1, q + 1)
                if j + 2 < J:
                    turn(j + 2, J // W - 1, q + 2)
                down(j, q)

        @block.scalar
        def _(act):
            with act.Fori(0, J // W) as it:
                for q in range(W):
                    j = it * W + q
                    for h in range(2):
                        act.wait_ge(h_done, 2 * j + h + 1)
                        act.activation(hT[:, q, 4 * h:4 * h + 4, :], ps[2 * q + h][:, :].rearrange("p (m n) -> p m n", m=4),
                                       ACT.Gelu_apprx_tanh).then_inc(h_copied, 1)

        @block.vector
        def _(dve):
            dve.sem_inc(y_copied, 1)
            dve.wait_ge(ln_in, 32)

            def turned(j, q):
                dve.wait_ge(xT_done, j + 1)
                for k in range(KT):
                    dve.tensor_scalar(xT[:, q, k, :], ps[7][:, k * P:(k + 1) * P], ln_w[:, k:k + 1], ln_b[:, k:k + 1],
                                      ALU.mult, ALU.add).then_inc(xT_copied, 1)

            def result(j, it, q):
                dve.wait_ge(y_done, j + 1)
                dve.wait_ge(stored[q], 16 + 16 * it)
                dve.tensor_copy(y[:, q, :], ps[6][:, 0:D]).then_inc(y_copied, 1)

            turned(0, 0)
            turned(1, 1)
            with dve.Fori(0, J // W - 1) as it:
                for q in range(W):
                    turned(it * W + q + 2, (q + 2) % W)
                    result(it * W + q, it, q)
            for q in range(W):
                if q + 2 < W:
                    turned(J - W + q + 2, q + 2)
                result(J - W + q, J // W - 1, q)


def finish(nc, ctx, t, dram, out):
    def sb(name, shape, dt=F32):
        return ctx.enter_context(nc.sbuf_tensor("sb_f_" + name, shape, dt))

    def sem(name):
        return ctx.enter_context(nc.semaphore("f_" + name))

    X, dest, Y, neg_half = (t[n] for n in ("X", "dest", "Z", "neg_half"))
    stats = sb("stats", [P, TPB, 6])
    mv = sb("mv", [P, TPB, 2])
    rstd = sb("rstd", [P, TPB])
    gathered = [sem(f"gathered{b}") for b in range(B)]
    spare = sem("spare")
    summed, dve_steps, var_done, rstd_done, normed, stored = (sem(n) for n in (
        "summed", "dve_steps", "var_done", "rstd_done", "normed", "stored"))

    with nc.Block() as block:
        @block.gpsimd
        def _(pool):
            for n in range(NT):
                pool.indirect_dma_start(Y[:, n, :], None, dram["sorted_out"],
                                        bass.IndirectOffsetOnAxis(ap=dest[:, n:n + 1], axis=0)).then_inc(gathered[n // TPB], 16)
            for b in range(B):
                pool.wait_ge(var_done, b + 1)
                pool.tensor_tensor(rstd[:, :], mv[:, :, 1], neg_half[:, :], ALU.pow).then_inc(rstd_done, 1)

        @block.vector
        def _(dve):
            ch = Chain(dve, dve_steps)
            for b in range(B):
                dve.wait_ge(gathered[b], 16 * TPB)
                tiles = X[:, b * TPB:(b + 1) * TPB, :]
                ch.link(dve.tensor_tensor(tiles, tiles, Y[:, b * TPB:(b + 1) * TPB, :], ALU.add))
                layer_stats(dve, ch, tiles, stats, mv, spare)
                dve.sem_inc(var_done, 1)
                dve.wait_ge(rstd_done, b + 1)
                for n in range(TPB):
                    tp = dve.tensor_scalar(tiles[:, n, :], tiles[:, n, :], mv[:, n, 0:1], rstd[:, n:n + 1],
                                           ALU.subtract, ALU.mult)
                tp.then_inc(normed, 1)

        @block.sync
        def _(sp):
            for b in range(B):
                sp.wait_ge(normed, b + 1)
                sp.dma_start(out[b].rearrange("(n p) d -> p n d", p=P), X[:, b * TPB:(b + 1) * TPB, :]).then_inc(stored, 16)
            sp.wait_ge(stored, 16 * B)


def decoder(nc, dram, out):
    E = dram["gate_w"].shape[1]
    J = B * S // P + E - 1
    dram["q_parts"] = nc.dram_tensor("q_parts", (3, B * D, S), BF16).ap()
    dram["k_parts"] = nc.dram_tensor("k_parts", (3, B * D, S), BF16).ap()
    dram["sorted"] = nc.dram_tensor("sorted", (J * P, D), F32).ap()
    dram["sorted_out"] = nc.dram_tensor("sorted_out", (J * P, D), F32).ap()
    with ExitStack() as ctx:
        def sb(name, shape, dt=F32):
            return ctx.enter_context(nc.sbuf_tensor(name, shape, dt))

        t = {}
        pz = ctx.enter_context(nc.psum_tensor("banks", [P, 8, 512], F32))
        t["pz"], t["ps"] = pz, [pz[:, i, :] for i in range(8)]
        t["X"] = sb("X", [P, NT, D])
        t["ident"] = sb("ident_sb", [P, P])
        t["neg_half"] = sb("neg_half", [P, TPB])
        ident_in = ctx.enter_context(nc.semaphore("ident_in"))
        with nc.Block() as block:
            @block.sync
            def _(sp):
                sp.dma_start(t["ident"][:, :], dram["ident"]).then_inc(ident_in, 16)
                sp.wait_ge(ident_in, 17)

            @block.vector
            def _(dve):
                dve.memset(t["neg_half"][:, :], -0.5).then_inc(ident_in, 1)
        for stage in (autocorrelation, cross_attention):
            with ExitStack() as own:
                stage(nc, own, t, dram)
        with ExitStack() as attention:
            t["y_all"] = attention.enter_context(nc.sbuf_tensor("y_all", [P, B * H, TPB, DK], F32))
            with ExitStack() as own:
                t["v_all"] = own.enter_context(nc.sbuf_tensor("v_all", [P, B * H, TPB, DK], F32))
                with ExitStack() as inner:
                    project_qkv(nc, inner, t, dram)
                with ExitStack() as inner:
                    self_attention(nc, inner, t, dram)
            t["Z"] = attention.enter_context(nc.sbuf_tensor("Z", [P, NT, D], F32))
            t["logits"] = attention.enter_context(nc.sbuf_tensor("logits", [P, NT, E], F32))
            t["dest"] = attention.enter_context(nc.sbuf_tensor("dest", [P, NT], U32))
            t["owner"] = attention.enter_context(nc.sbuf_tensor("owner", [1, J], I32))
            for stage in (gate, route, experts):
                with ExitStack() as own:
                    stage(nc, own, t, dram)
            with ExitStack() as own:
                finish(nc, own, t, dram, out)


def dft_constants():
    s = np.arange(S)
    ang = 2 * np.pi / S
    odd, two, zero = np.arange(1, S // 2, 2), np.arange(2, S // 2, 4), np.arange(0, S // 2, 4)
    a = ang * ((s[:512, None] * odd[None]) % S)
    fwd_odd = np.concatenate([np.cos(a), -np.sin(a)], 1)
    inv_odd = np.concatenate([np.cos(a), -np.sin(a)], 1).T * (2 / S)
    q = s[:256, None]
    a2, a0 = ang * ((q * two[None]) % S), ang * ((q * zero[None]) % S)
    f2 = np.concatenate([np.cos(a2), -np.sin(a2)], 1)
    f0 = np.concatenate([np.cos(a0), -np.sin(a0)], 1)
    f0[:, 128] = (-1.0) ** s[:256]
    i2 = f2.T * (2 / S)
    i0 = f0.T * (2 / S)
    i0[0] /= 2
    i0[128] /= 2
    return (fwd_odd.astype(np.float32), np.concatenate([f2, f0], 0).astype(np.float32),
            inv_odd.astype(np.float32), np.concatenate([i2, i0], 0).astype(np.float32))


def kernel(**inputs):
    import concourse.bacc as bacc
    from concourse.bass_utils import run_bass_kernel_spmd

    def layout(a):
        return np.ascontiguousarray(a)

    def columns(v):
        return layout(np.asarray(v).reshape(-1, P).T)

    f = {n: np.asarray(v) for n, v in inputs.items()}
    E = f["L0_ffn_gate_w"].shape[1]
    J = B * S // P + E - 1
    fwd_odd, fwd_even, inv_odd, inv_even = dft_constants()
    p = np.arange(P)
    at_zero = np.zeros((1, P), np.float32)
    at_zero[0, 0] = S
    arrays = {
        "fwd_odd": fwd_odd, "fwd_even": fwd_even, "inv_odd": inv_odd, "inv_even": inv_even, "f0": at_zero,
        "head_mask": (p[:, None] // DK == np.arange(TOP)[None]).astype(np.float32),
        "ident": np.eye(P, dtype=np.float32),
        "before": (p[:, None] < p[None]).astype(np.float32),
        "prefer": np.tile(np.arange(E, 0, -1, dtype=np.float32), (P, 1)),
        "starts": np.tile(np.arange(NT, dtype=np.float32) * P, (P, 1)),
        "block_no": np.arange(J, dtype=np.float32)[None],
        "x": layout(f["x"]),
        "xT16": layout(f["x"][:, :DK, :].transpose(2, 0, 1).reshape(D, B * DK)),
        "L0_attn_Wq": layout(f["L0_attn_Wq"]), "L0_attn_Wk": layout(f["L0_attn_Wk"]),
        "L0_attn_Wv": layout(f["L0_attn_Wv"]), "L0_attn_Wo": layout(f["L0_attn_Wo"]),
        "b_qk": np.concatenate([f["L0_attn_bq"], f["L0_attn_bk"]])[None],
        "bv_attn": columns(f["L0_attn_bv"]), "bo_attn": layout(f["L0_attn_bo"][None]),
        "WqT": layout(f["L0_xattn_Wq"].T), "WkvT": layout(f["L0_xattn_Wkv"].T), "WoT": layout(f["L0_xattn_Wo"].T),
        "ctxT": layout(f["ctx_1024"].transpose(2, 0, 1).reshape(D, -1)),
        "bq_cross": columns(f["L0_xattn_bq"]), "bk_cross": columns(f["L0_xattn_bkv"][:D]),
        "bv_cross": layout(f["L0_xattn_bkv"][None, D:]), "bo_cross": layout(f["L0_xattn_bo"][None]),
        "w_qkv": layout(f["L0_ffn_w_qkv"]), "w_proj": layout(f["L0_ffn_w_proj"]),
        "ln1_w": columns(f["L0_ffn_ln1_w"]), "ln1_b": columns(f["L0_ffn_ln1_b"]),
        "ln2_w": columns(f["L0_ffn_ln2_w"]), "ln2_b": columns(f["L0_ffn_ln2_b"]),
        "gate_w": layout(f["L0_ffn_gate_w"]), "gate_b": layout(f["L0_ffn_gate_b"][None]),
        "w1": layout(f["L0_ffn_w1"]), "w2": layout(f["L0_ffn_w2"]),
    }
    nc = bacc.Bacc("TRN2", target_bir_lowering=False, num_devices=1)
    given, dram = {}, {}
    for name, a in arrays.items():
        given[f"in_{name}"] = a
        dram[name] = nc.dram_tensor(f"in_{name}", a.shape, mybir.dt.from_np(a.dtype), kind="ExternalInput").ap()
    out = nc.dram_tensor("out_x", (B, S, D), F32, kind="ExternalOutput").ap()
    decoder(nc, dram, out)
    r = run_bass_kernel_spmd(nc, [given], core_ids=[0])
    return r.results[0]["out_x"]
```

```python
from contextlib import ExitStack

import numpy as np

import concourse.bass as bass
from concourse import mybir

F32 = mybir.dt.float32
BF16 = mybir.dt.bfloat16
I32 = mybir.dt.int32
U32 = mybir.dt.uint32
ALU = mybir.AluOpType
ACT = mybir.ActivationFunctionType
AX = mybir.AxisListType
ds = bass.ds

B, S, D, H = 4, 1024, 256, 16
DK = D // H
P = 128
TPB = S // P
NT = B * TPB
KT = D // P
EPS = 1e-5
TOP = 8
G = B * KT
EXP_ZERO = -104.0
LOWEST = -3.0e38


class Chain:

    def __init__(self, eng, sem, base=0):
        self.eng, self.sem, self.base, self.n = eng, sem, base, 0

    def link(self, ins):
        self.n += 1
        ins.then_inc(self.sem, 1)
        self.eng.wait_ge(self.sem, self.base + self.n)


def autocorrelation(nc, ctx, t, dram):
    def sb(name, shape, dt=F32):
        return ctx.enter_context(nc.sbuf_tensor("sb_" + name, shape, dt))

    def sem(name):
        return ctx.enter_context(nc.semaphore(name))

    X, ps = t["X"], t["ps"]
    fold = sb("fold", [P, TPB, D])
    even = sb("even", [P, 4, D])
    fwd_odd = sb("fwd_odd", [P, 4, 512])
    fwd_even = sb("fwd_even", [P, 4, 256])
    inv_odd = sb("inv_odd", [P, 4, 512])
    inv_even = sb("inv_even", [P, 4, 256])
    w_qk = sb("w_qk", [P, KT, 2 * D])
    w_v = sb("w_v", [P, KT, D])
    w_o = sb("w_o", [P, KT, D])
    b_qk = sb("b_qk", [1, 2 * D])
    b_v = sb("b_v", [P, KT])
    bo = sb("bo", [P, D])
    f0 = sb("f0", [1, P])
    xT16 = sb("xT16", [P, KT, B * DK])
    head_mask = sb("head_mask", [P, TOP])
    vT = sb("vT", [P, KT, B * DK])
    vblk = sb("vblk", [P, KT, B, P])
    vwo = sb("vwo", [P, G, D])
    xfT = sb("xfT", [P, KT, 2, 512])
    qk = sb("qk", [P, 8, 2 * D])
    cross = sb("cross", [P, 8, D])
    prod = sb("prod", [P, 4, D])
    corr = sb("corr", [P, G, S])
    w_sort = sb("w_sort", [P, G, S])
    uv = sb("uv", [P, KT, 2, 256])
    m8 = sb("m8", [P, G, TOP])
    d8 = sb("d8", [P, G, TOP])
    e8 = sb("e8", [P, G, TOP])
    wsum = sb("wsum", [P, G])
    wrec = sb("wrec", [P, G])
    neg_m = sb("neg_m", [P, G])
    ones = sb("ones_a", [P, 1])
    tail = sb("tail", [P, 2])
    tail_flag = sb("tail_flag", [1, 1], I32)
    cur8 = sb("cur8", [P, TOP])

    x_in = [sem(f"a_x_in{b}") for b in range(B)]
    fwd_in, qk_in, inv_in, v_in, bo_in = (sem("a_" + n) for n in ("fwd_in", "qk_in", "inv_in", "v_in", "bo_in"))
    zeroed, folded, spectrum, spectrum_T = sem("a_zeroed"), sem("a_folded"), sem("a_spectrum"), sem("a_spectrum_T")
    qk_done, qk_copied, cross_done = sem("a_qk_done"), sem("a_qk_copied"), sem("a_cross_done")
    inv_done, corr_done = sem("a_inv_done"), sem("a_corr_done")
    bo_added = sem("a_bo_added")
    v_done, v_copied, vblk_done, vwo_done, vwo_copied = (sem("a_" + n) for n in (
        "v_done", "v_copied", "vblk_done", "vwo_done", "vwo_copied"))
    tail_local, tail_counted, flag_set = sem("a_tail_local"), sem("a_tail_counted"), sem("a_flag_set")
    diffs, exps, weights, y_done = sem("a_diffs"), sem("a_exps"), sem("a_weights"), sem("a_y_done")
    fold_steps, cross_steps, corr_steps, dve_steps, sort_steps = (sem("a_" + n) for n in (
        "fold_steps", "cross_steps", "corr_steps", "dve_steps", "sort_steps"))
    sorted_done, gen_exps, gen_weights, gen_y, gen_added = (sem("a_" + n) for n in (
        "sorted", "gen_exps", "gen_weights", "gen_y", "gen_added"))

    with nc.Block() as block:
        @block.sync
        def _(sp):
            def load(name, dst, signal):
                sp.dma_start(dst, dram[name].rearrange("(k p) n -> p k n", p=P)).then_inc(signal, 16)

            def load_x(b):
                sp.dma_start(X[:, b * TPB:(b + 1) * TPB, :],
                             dram["x"][b].rearrange("(n p) d -> p n d", p=P)).then_inc(x_in[b], 16)

            load_x(0)
            load("fwd_odd", fwd_odd[:, :, :], fwd_in)
            load("fwd_even", fwd_even[:, :, :], fwd_in)
            load("L0_attn_Wq", w_qk[:, :, 0:D], qk_in)
            load("L0_attn_Wk", w_qk[:, :, D:2 * D], qk_in)
            sp.dma_start(b_qk[:, :], dram["b_qk"]).then_inc(qk_in, 16)
            sp.dma_start(f0[:, :], dram["f0"]).then_inc(qk_in, 16)
            for b in range(1, B):
                load_x(b)
            load("inv_odd", inv_odd[:, :, :], inv_in)
            load("inv_even", inv_even[:, :, :], inv_in)
            sp.dma_start(bo[:, :], dram["bo_attn"].partition_broadcast(P)).then_inc(bo_in, 16)
            load("L0_attn_Wv", w_v[:, :, :], v_in)
            load("L0_attn_Wo", w_o[:, :, :], v_in)
            load("xT16", xT16[:, :, :], v_in)
            sp.dma_start(b_v[:, :], dram["bv_attn"]).then_inc(v_in, 16)
            sp.dma_start(head_mask[:, :], dram["head_mask"]).then_inc(v_in, 16)

        @block.gpsimd
        def _(pool):
            pool.memset(ones[:, :], 1.0).then_inc(zeroed, 1)
            pool.memset(w_sort[:, :, :], 0.0).then_inc(zeroed, 1)
            pool.wait_ge(bo_in, 16)
            with pool.Fori(0, B) as b:
                pool.wait_ge(folded, b + 1)
                pool.tensor_tensor(X[:, ds(b * TPB, TPB), :], X[:, ds(b * TPB, TPB), :],
                                   bo[:, :].unsqueeze(1).broadcast_to([P, TPB, D]), ALU.add).then_inc(bo_added, 1)

        @block.tensor
        def _(pe):
            def forward(b):
                pe.wait_ge(folded, b + 1)
                for c in range(KT):
                    for k in range(4):
                        mm = pe.matmul(ps[c][:, :], fold[:, k, c * P:(c + 1) * P], fwd_odd[:, k, :],
                                       start=(k == 0), stop=(k == 3))
                    mm.then_inc(spectrum, 1)
                    for h in range(2):
                        for k in range(2):
                            mm = pe.matmul(ps[2 + c][:, h * 256:(h + 1) * 256],
                                           fold[:, 4 + 2 * h + k, c * P:(c + 1) * P], fwd_even[:, 2 * h + k, :],
                                           start=(k == 0), stop=(k == 1))
                    mm.then_inc(spectrum, 1)

            def batch(b, last):
                pe.wait_ge(spectrum_T, 6 * (b + 1))
                for f in range(8):
                    r, q = f // 4, f % 4
                    if f < 4 and f % 2 == 0:
                        pe.wait_ge(corr_done, 2 + KT * b - 1 + f // 2)
                    elif f >= 4:
                        pe.wait_ge(qk_copied, 8 * b + f - 3)
                    for k in range(KT):
                        mm = pe.matmul(ps[4 + f % 4][:, :], xfT[:, k, r, q * P:(q + 1) * P], w_qk[:, k, :],
                                       start=(k == 0), stop=(k == KT - 1 and f != 3))
                    if f == 3:
                        mm = pe.matmul(ps[7][:, :], f0[:, :], b_qk[:, :], start=False, stop=True)
                    mm.then_inc(qk_done, 1)
                if not last:
                    forward(b + 1)
                pe.wait_ge(cross_done, b + 2)
                for c in range(KT):
                    cs = slice(c * P, (c + 1) * P)
                    for n, f in enumerate((0, 1, 4, 5)):
                        pe.matmul(ps[4 + 2 * c][:, :], cross[:, f, cs], inv_odd[:, n, :], start=(n == 0), stop=(n == 3))
                    for h in range(2):
                        for n in range(2):
                            mm = pe.matmul(ps[5 + 2 * c][:, h * 256:(h + 1) * 256], cross[:, 2 + h + 4 * n, cs],
                                           inv_even[:, 2 * h + n, :], start=(n == 0), stop=(n == 1))
                    mm.then_inc(inv_done, 1)

            pe.wait_ge(fwd_in, 32)
            forward(0)
            pe.wait_ge(qk_in, 64)
            pe.wait_ge(inv_in, 32)
            with pe.Fori(0, B - 1) as b:
                batch(b, False)
            batch(B - 1, True)
            pe.wait_ge(v_in, 80)
            for c in range(KT):
                for k in range(KT):
                    mm = pe.matmul(ps[c][:, 0:B * DK], w_v[:, k, c * P:(c + 1) * P], xT16[:, k, :],
                                   start=(k == 0), stop=(k == KT - 1))
                mm.then_inc(v_done, 1)
            pe.wait_ge(vblk_done, KT)
            pe.wait_ge(v_copied, KT)
            for b in range(B):
                for c in range(KT):
                    pe.matmul(ps[b][:, c * D:(c + 1) * D], vblk[:, c, b, :], w_o[:, c, :],
                              start=True, stop=True).then_inc(vwo_done, 1)
            pe.wait_ge(tail_local, 1)
            pe.wait_ge(zeroed, 1)
            pe.matmul(ps[7][0:1, 0:1], tail[:, 1:2], ones[:, :], start=True, stop=True).then_inc(tail_counted, 1)
            pe.wait_ge(flag_set, 1)
            pe.wait_ge(vwo_copied, B)
            general = pe.value_load(tail_flag[0:1, 0:1], min_val=0, max_val=P)
            with pe.If(general > 0):
                pe.wait_ge(gen_weights, G)
                for b in range(B):
                    for i in range(1, TPB):
                        n = b * (TPB - 1) + i - 1
                        if n >= 4:
                            pe.wait_ge(gen_added, n - 3)
                        for k in range(KT):
                            mm = pe.matmul(ps[n % 4][:, 0:D], w_sort[:, b * KT + k, i * P:(i + 1) * P],
                                           vwo[:, b * KT + k, :], start=(k == 0), stop=(k == KT - 1))
                        mm.then_inc(gen_y, 1)
                pe.nop()
            pe.wait_ge(weights, 1)
            for b in range(B):
                for k in range(KT):
                    mm = pe.matmul(ps[4 + b][:, 0:D], w_sort[:, b * KT + k, 0:P], vwo[:, b * KT + k, :],
                                   start=(k == 0), stop=(k == KT - 1))
                mm.then_inc(y_done, 1)

        @block.scalar
        def _(act):
            def turned(b):
                for c in range(KT):
                    act.wait_ge(spectrum, 4 * b + 2 * c + 1)
                    act.activation(xfT[:, c, :, 0:256], ps[c][:, :].rearrange("p (r n) -> p r n", r=2),
                                   ACT.Identity).then_inc(spectrum_T, 1)
                    act.wait_ge(spectrum, 4 * b + 2 * c + 2)
                    for h in range(2):
                        act.activation(xfT[:, c, :, 256 + h * P:256 + (h + 1) * P],
                                       ps[2 + c][:, h * 256:(h + 1) * 256].rearrange("p (r n) -> p r n", r=2),
                                       ACT.Identity).then_inc(spectrum_T, 1)

            def batch(b, last):
                act.wait_ge(cross_done, b + 1)
                for f in range(8):
                    act.wait_ge(qk_done, 8 * b + f + 1)
                    act.activation(qk[:, f, :], ps[4 + f % 4][:, :], ACT.Identity).then_inc(qk_copied, 1)
                if not last:
                    turned(b + 1)

            turned(0)
            with act.Fori(0, B - 1) as b:
                batch(b, False)
            batch(B - 1, True)
            act.wait_ge(v_in, 80)
            for c in range(KT):
                act.wait_ge(v_done, c + 1)
                act.activation(vT[:, c, :], ps[c][:, 0:B * DK], ACT.Identity, bias=b_v[:, c:c + 1]).then_inc(v_copied, 1)
            for b in range(B):
                act.wait_ge(vwo_done, 2 * (b + 1))
                act.activation(vwo[:, b * KT:(b + 1) * KT, :], ps[b][:, :].rearrange("p (k n) -> p k n", k=KT),
                               ACT.Identity).then_inc(vwo_copied, 1)
            act.wait_ge(diffs, 1)
            act.activation(e8[:, :, :], d8[:, :, :], ACT.Exp).then_inc(exps, 1)
            act.wait_ge(flag_set, 1)
            general = act.value_load(tail_flag[0:1, 0:1], min_val=0, max_val=P)
            with act.If(general > 0):
                for g in range(G):
                    act.wait_ge(sorted_done, g + 1)
                    act.activation(w_sort[:, g, :], w_sort[:, g, :], ACT.Exp, bias=neg_m[:, g:g + 1],
                                   accum_out=wsum[:, g:g + 1]).then_inc(gen_exps, 1)
                act.nop()

        @block.vector
        def _(dve):
            dve.sem_inc(cross_done, 1)
            dve.sem_inc(corr_done, 2)

            def folding(b):
                lo, hi = X[:, ds(b * TPB, 4), :], X[:, ds(b * TPB + 4, 4), :]
                ch = Chain(dve, fold_steps, b)
                dve.tensor_tensor(fold[:, 0:4, :], lo, hi, ALU.subtract)
                ch.link(dve.tensor_tensor(even[:, :, :], lo, hi, ALU.add))
                dve.tensor_tensor(fold[:, 4:6, :], even[:, 0:2, :], even[:, 2:4, :], ALU.subtract)
                dve.tensor_tensor(fold[:, 6:8, :], even[:, 0:2, :], even[:, 2:4, :], ALU.add).then_inc(folded, 1)

            def batch(b, last):
                if not last:
                    dve.wait_ge(spectrum, 4 * (b + 1))
                    folding(b + 1)
                dve.wait_ge(qk_copied, 8 * (b + 1))
                ch = Chain(dve, cross_steps, 4 * b)
                qr, kr, qi, ki = qk[:, 0:4, 0:D], qk[:, 0:4, D:2 * D], qk[:, 4:8, 0:D], qk[:, 4:8, D:2 * D]
                dve.tensor_tensor(cross[:, 4:8, :], qi, kr, ALU.mult)
                ch.link(dve.tensor_tensor(prod[:, :, :], qr, ki, ALU.mult))
                ch.link(dve.tensor_tensor(cross[:, 4:8, :], cross[:, 4:8, :], prod[:, :, :], ALU.subtract))
                dve.tensor_tensor(cross[:, 0:4, :], qr, kr, ALU.mult)
                ch.link(dve.tensor_tensor(prod[:, :, :], qi, ki, ALU.mult))
                ch.link(dve.tensor_tensor(cross[:, 0:4, :], cross[:, 0:4, :], prod[:, :, :], ALU.add))
                dve.tensor_copy(cross[0:1, 7, :], prod[0:1, 3, :])
                dve.tensor_tensor(cross[0:1, 3, :], qk[0:1, 3, 0:D], qk[0:1, 3, D:2 * D],
                                  ALU.mult).then_inc(cross_done, 1)
                ch = Chain(dve, corr_steps, 2 * KT * b)
                for c in range(KT):
                    dve.wait_ge(inv_done, KT * b + c + 1)
                    ch.link(dve.tensor_copy(prod[:, c, :], ps[5 + 2 * c][:, 256:512]))
                    dve.tensor_tensor(uv[:, c, 0, :], ps[5 + 2 * c][:, 0:256], prod[:, c, :], ALU.add)
                    ch.link(dve.tensor_tensor(uv[:, c, 1, :], prod[:, c, :], ps[5 + 2 * c][:, 0:256], ALU.subtract))
                    odd = ps[4 + 2 * c][:, :].rearrange("p (r n) -> p r n", r=2)
                    row = corr[:, ds(b * KT + c, 1), :].rearrange("p o (a r n) -> p (o a) r n", a=2, r=2)
                    dve.tensor_tensor(row[:, 0], uv[:, c, :, :], odd, ALU.add)
                    dve.tensor_tensor(row[:, 1], uv[:, c, :, :], odd, ALU.subtract).then_inc(corr_done, 1)

            dve.wait_ge(x_in[0], 16)
            folding(0)
            for b in range(1, B):
                dve.wait_ge(x_in[b], 16)
            with dve.Fori(0, B - 1) as b:
                batch(b, False)
            batch(B - 1, True)
            ch = Chain(dve, dve_steps)
            dve.wait_ge(corr_done, 2 + G)
            for g in range(G):
                last = dve.max(m8[:, g, :], corr[:, g, :])
            ch.link(last)
            ch.link(dve.tensor_tensor(d8[:, :, :], m8[:, :, :], m8[:, :, 0:1].broadcast_to([P, G, TOP]), ALU.subtract))
            dve.sem_inc(diffs, 1)
            ch.link(dve.tensor_reduce(tail[:, 0:1], d8[:, :, TOP - 1], AX.X, ALU.max))
            dve.tensor_scalar(tail[:, 1:2], tail[:, 0:1], EXP_ZERO, None, ALU.is_ge).then_inc(tail_local, 1)
            dve.wait_ge(v_in, 80)
            for c in range(KT):
                dve.wait_ge(v_copied, c + 1)
                dve.tensor_tensor(
                    vblk[:, c, :, :].rearrange("p b (h i) -> p b h i", h=8),
                    vT[:, c, :].rearrange("p (b i) -> p b i", b=B).unsqueeze(2).broadcast_to([P, B, 8, DK]),
                    head_mask[:, :].unsqueeze(1).unsqueeze(3).broadcast_to([P, B, 8, DK]), ALU.mult).then_inc(vblk_done, 1)
            dve.wait_ge(tail_counted, 1)
            dve.tensor_copy(tail_flag[:, :], ps[7][0:1, 0:1]).then_inc(flag_set, 1)
            dve.wait_ge(exps, 1)
            ch.link(dve.tensor_reduce(wsum[:, :], e8[:, :, :], AX.X, ALU.add))
            ch.link(dve.reciprocal(wrec[:, :], wsum[:, :]))
            dve.wait_ge(zeroed, 2)
            ch.link(dve.tensor_tensor(w_sort[:, :, 0:TOP], e8[:, :, :],
                                      wrec[:, :].unsqueeze(2).broadcast_to([P, G, TOP]), ALU.mult))
            dve.wait_ge(flag_set, 1)
            dve.wait_ge(bo_added, B)
            general = dve.value_load(tail_flag[0:1, 0:1], min_val=0, max_val=P)
            with dve.If(general > 0):
                gs = Chain(dve, sort_steps)
                gs.link(dve.tensor_scalar(neg_m[:, :], m8[:, :, 0], -1.0, None, ALU.mult))
                STEPS = S // TOP
                for g in range(G):
                    with dve.Fori(0, STEPS) as i:
                        st = Chain(dve, sort_steps, 1 + g * STEPS * 2 + i * 2)
                        st.link(dve.max(cur8[:, :], corr[:, g, :]))
                        dve.tensor_copy(w_sort[:, g, ds(i * TOP, TOP)], cur8[:, :])
                        st.link(dve.match_replace(corr[:, g, :], cur8[:, :], corr[:, g, :], LOWEST))
                    dve.sem_inc(sorted_done, 1)
                for g in range(G):
                    dve.wait_ge(gen_exps, g + 1)
                    gs2 = Chain(dve, sort_steps, 1 + G * STEPS * 2 + g)
                    gs2.link(dve.reciprocal(wrec[:, g:g + 1], wsum[:, g:g + 1]))
                    dve.tensor_scalar(w_sort[:, g, :], w_sort[:, g, :], wrec[:, g:g + 1], None,
                                      ALU.mult).then_inc(gen_weights, 1)
                for b in range(B):
                    for i in range(1, TPB):
                        n = b * (TPB - 1) + i - 1
                        dve.wait_ge(gen_y, n + 1)
                        dve.tensor_tensor(X[:, b * TPB + i, :], X[:, b * TPB + i, :], ps[n % 4][:, 0:D],
                                          ALU.add).then_inc(gen_added, 1)
                dve.wait_ge(gen_added, B * (TPB - 1))
                dve.nop()
            dve.sem_inc(weights, 1)
            for b in range(B):
                dve.wait_ge(y_done, b + 1)
                dve.tensor_tensor(X[:, b * TPB, :], X[:, b * TPB, :], ps[4 + b][:, 0:D], ALU.add)



def alone(eng, spare):
    eng.sem_inc(spare, 1)


def layer_stats(dve, ch, tiles, stats, mv, spare, count=TPB):
    alone(dve, spare)
    for n in range(count):
        last = dve.bn_stats(stats[:, n, :], tiles[:, n, :])
    ch.link(last)
    alone(dve, spare)
    for n in range(count):
        last = dve.bn_aggr(mv[:, n, :], stats[:, n, :])
    ch.link(last)
    ch.link(dve.tensor_scalar(mv[:, :, 1], mv[:, :, 1], EPS, None, ALU.add))


def cross_attention(nc, ctx, t, dram):
    def sb(name, shape, dt=F32):
        return ctx.enter_context(nc.sbuf_tensor("sb_b_" + name, shape, dt))

    def sem(name):
        return ctx.enter_context(nc.semaphore("b_" + name))

    X, ps, pz, ident, neg_half = t["X"], t["ps"], t["pz"], t["ident"], t["neg_half"]
    C = dram["ctxT"].shape[1] // B
    HP = H // 2
    VW = 2 * (DK + 1)
    w_q = sb("w_q", [P, KT, D])
    w_kv = sb("w_kv", [P, KT, 2 * D])
    w_o = sb("w_o", [P, KT, D])
    bias_q = sb("bias_q", [P, KT])
    bias_k = sb("bias_k", [P, KT])
    bias_v = sb("bias_v", [1, D])
    bias_o = sb("bias_o", [P, D])
    mask = sb("mask", [P, TOP])
    ctxT = sb("ctxT", [P, KT, B * C])
    ctxT2 = sb("ctxT2", [P, KT, B, 2, C])
    ones_row = sb("ones_row", [1, P])
    kT = sb("kT", [P, KT, B * C])
    kblk = sb("kblk", [P, KT, B, 8 * C])
    vblk = sb("vblk", [P, B, HP, 2, DK + 1])
    GT = 4
    NG = NT // GT
    assert TPB == 2 * GT
    stats = sb("stats", [P, GT, 6])
    mv = sb("mv", [P, GT, 2])
    rstd = sb("rstd", [P, GT])
    xs = sb("xs", [P, GT, D])
    xT = sb("xT", [P, KT, GT * P])
    qT = sb("qT", [P, KT, 2, GT * P])
    mx = sb("mx", [P, 2, H])
    pr = sb("pr", [P, 2, H, C])
    prT = sb("prT", [P, 2, HP, P])
    rec = sb("rec", [P, 2, H])
    y = sb("y", [P, 2, D])
    yT = sb("yT", [P, 2, KT, P])

    w_in = sem("w_in")
    zeroed, k_done, k_copied, v_done = sem("zeroed"), sem("k_done"), sem("k_copied"), sem("v_done")
    kblk_done, vblk_done = sem("kblk_done"), sem("vblk_done")
    dve_steps = sem("dve_steps")
    spare = t["spare"]
    var_done, rstd_done, x_done, xs_done, bo_added, piece_done, piece_copied = (sem(n) for n in (
        "var_done", "rstd_done", "x_done", "xs_done", "bo_added", "piece_done", "piece_copied"))
    max_done, rec_done = sem("max_done"), sem("rec_done")
    scores, shifted, probs, probsT, probsT_copied, pv, y_done, yT_done, yT_copied, out_done, res_done = (
        sem(n) for n in ("scores", "shifted", "probs", "probsT", "probsT_copied", "pv", "y_done", "yT_done",
                         "yT_copied", "out_done", "res_done"))
    AHEAD = 6

    def need(eng, signal, value):
        if not isinstance(value, int) or value > 0:
            eng.wait_ge(signal, value)

    def over_slots(eng, slot):
        for r in range(TPB):
            slot(0, r)
        with eng.Fori(1, B - 1) as b:
            for r in range(TPB):
                slot(b, r)
        for r in range(TPB):
            slot(B - 1, r)
        for r in range(3):
            slot(B, r)

    def tile(b, r, lag):
        n = b * TPB + r - lag
        return n if not isinstance(n, int) or 0 <= n < NT else None

    def piece(b, r):
        kind = r % GT // 2
        g = b * 2 + r // GT + 1 + kind
        if isinstance(g, int) and g >= NG:
            return None
        return AHEAD + b * TPB + r, kind, g, (r // GT + 1 + kind) % 2, r % 2

    first_pieces = [(0, 1, 0, 0, 0), (1, 1, 0, 0, 1), (2, 0, 0, 0, 0), (3, 0, 0, 0, 1), (4, 1, 1, 1, 0), (5, 1, 1, 1, 1)]

    loads = [
        (w_kv[:, :, :], dram["WkvT"].rearrange("(k p) n -> p k n", p=P)),
        (ctxT[:, :, :], dram["ctxT"].rearrange("(k p) n -> p k n", p=P)),
        (bias_k[:, :], dram["bk_cross"]),
        (bias_v[:, :], dram["bv_cross"]),
        (w_q[:, :, :], dram["WqT"].rearrange("(k p) n -> p k n", p=P)),
        (bias_q[:, :], dram["bq_cross"]),
        (mask[:, :], dram["head_mask"]),
        (w_o[:, :, :], dram["WoT"].rearrange("(k p) n -> p k n", p=P)),
        (bias_o[:, :], dram["bo_cross"].partition_broadcast(P)),
    ] + [(ctxT2[:, k, :, r, :], dram["ctxT"][k * P:(k + 1) * P].rearrange("p (b c) -> p b c", b=B))
         for k in range(KT) for r in range(2)]

    with nc.Block() as block:
        @block.sync
        def _(sp):
            for dst, src in loads:
                sp.dma_start(dst, src).then_inc(w_in, 16)

        @block.gpsimd
        def _(pool):
            pool.memset(ones_row[:, :], 1.0).then_inc(zeroed, 1)
            pool.memset(vblk[:, :, :, :, :], 0.0).then_inc(zeroed, 1)
            pool.wait_ge(zeroed, 2)
            pool.memset(vblk[0:C, :, :, 0, DK:DK + 1], 1.0).then_inc(zeroed, 1)
            pool.memset(vblk[C:2 * C, :, :, 1, DK:DK + 1], 1.0).then_inc(zeroed, 1)
            pool.wait_ge(zeroed, 4)

            def norm(g):
                need(pool, var_done, g + 1)
                pool.tensor_tensor(rstd[:, :], mv[:, :, 1], neg_half[:, 0:GT], ALU.pow).then_inc(rstd_done, 1)
                pool.wait_ge(x_done, g + 1)
                need(pool, piece_done, 4 * g - 2 if not isinstance(g, int) or g > 1 else 2 * g)
                alone(pool, spare)
                pool.tensor_copy(xs[:, :, :], X[:, ds(g * GT, GT), :]).then_inc(xs_done, 1)
                pool.tensor_tensor(X[:, ds(g * GT, GT), :], X[:, ds(g * GT, GT), :],
                                   bias_o[:, :].unsqueeze(1).broadcast_to([P, GT, D]), ALU.add).then_inc(bo_added, 1)

            pool.wait_ge(w_in, 16 * len(loads))
            for g in range(4):
                norm(g)
            with pool.Fori(2, NG // 2) as h:
                norm(2 * h)
                norm(2 * h + 1)

        @block.tensor
        def _(pe):
            pe.wait_ge(w_in, 16 * len(loads))
            for c in range(KT):
                for k in range(KT):
                    mm = pe.matmul(ps[c][:, 0:B * C], w_kv[:, k, c * P:(c + 1) * P], ctxT[:, k, :],
                                   start=(k == 0), stop=(k == KT - 1))
                mm.then_inc(k_done, 1)
            pe.wait_ge(zeroed, 1)
            for b in range(B):
                for k in range(KT):
                    pe.matmul(ps[4 + b][:, 0:D], ctxT2[:, k, b, :, :].rearrange("p r c -> p (r c)"),
                              w_kv[:, k, D:2 * D], start=(k == 0), stop=False)
                pe.matmul(ps[4 + b][:, 0:D], ones_row[:, :], bias_v[:, :], start=False, stop=True).then_inc(v_done, 1)
            pe.wait_ge(k_copied, KT)
            pe.wait_ge(kblk_done, KT)
            pe.wait_ge(vblk_done, 2 * B)

            def make(number, kind, g, parity, part):
                need(pe, piece_copied, number)
                if kind == 1:
                    pe.wait_ge(xs_done, g + 1)
                    for k in range(KT):
                        for n in range(2):
                            mm = pe.transpose(ps[4][:, (2 * k + n) * P:(2 * k + n + 1) * P],
                                              xs[:, 2 * part + n, k * P:(k + 1) * P], ident[:, :])
                else:
                    for k in range(KT):
                        mm = pe.matmul(ps[4][:, :], w_q[:, k, part * P:(part + 1) * P], xT[:, k, :],
                                       start=(k == 0), stop=(k == KT - 1))
                mm.then_inc(piece_done, 1)

            def slot(b, r):
                n, u, v = tile(b, r, 0), tile(b, r, 2), tile(b, r, 3)
                if u is not None:
                    pe.wait_ge(probs, u + 1)
                    need(pe, probsT_copied, u)
                    pe.wait_ge(piece_copied, AHEAD + u + 2 if not isinstance(u, int) else min(AHEAD + u + 2, 4 * NG))
                    for j in range(HP):
                        tr = pe.transpose(ps[4 + j // 4][:, j % 4 * P:(j % 4 + 1) * P],
                                          pr[:, r % 2, 2 * j:2 * j + 2, :].rearrange("p h c -> p (h c)"), ident[:, :])
                    tr.then_inc(probsT, 1)
                if v is not None:
                    pe.wait_ge(y_done, v + 1)
                    need(pe, res_done, v)
                    for k in range(KT):
                        tr = pe.transpose(ps[7][:, k * P:(k + 1) * P], y[:, (r - 3) % 2, k * P:(k + 1) * P], ident[:, :])
                    tr.then_inc(yT_done, 1)
                if n is not None:
                    if r % GT == 0:
                        pe.wait_ge(piece_copied, n + 4)
                    need(pe, shifted, n - 1)
                    for c in range(KT):
                        mm = pe.matmul(ps[2 * (r % 2) + c][:, :], qT[:, c, r // GT, r % GT * P:(r % GT + 1) * P],
                                       kblk[:, c, ds(b, 1), :].rearrange("p o n -> p (o n)"), start=True, stop=True)
                    mm.then_inc(scores, 1)
                    if piece(b, r):
                        if u is not None:
                            pe.wait_ge(probsT_copied, u + 1)
                        make(*piece(b, r))
                if u is not None:
                    pe.wait_ge(probsT_copied, u + 1)
                    need(pe, y_done, u)
                    for j in range(HP):
                        mm = pe.matmul(ps[6][:, j * VW:(j + 1) * VW], prT[:, r % 2, j, :],
                                       vblk[:, ds(b if r >= 2 else b - 1, 1), j, :, :].rearrange("p o r c -> p (o r c)"),
                                       start=True, stop=True)
                    mm.then_inc(pv, 1)
                if v is not None:
                    pe.wait_ge(yT_copied, v + 1)
                    for k in range(KT):
                        mm = pe.matmul(ps[7][:, D:2 * D], yT[:, (r - 3) % 2, k, :], w_o[:, k, :],
                                       start=(k == 0), stop=(k == KT - 1))
                    mm.then_inc(out_done, 1)

            for p in first_pieces:
                make(*p)
            over_slots(pe, slot)

        @block.scalar
        def _(act):
            act.wait_ge(w_in, 16 * len(loads))
            for c in range(KT):
                act.wait_ge(k_done, c + 1)
                act.activation(kT[:, c, :], ps[c][:, 0:B * C], ACT.Identity, bias=bias_k[:, c:c + 1]).then_inc(k_copied, 1)
            act.wait_ge(zeroed, 4)
            for b in range(B):
                act.wait_ge(v_done, b + 1)
                for r in range(2):
                    act.activation(vblk[r * C:(r + 1) * C, b, :, r, 0:DK],
                                   ps[4 + b][r * C:(r + 1) * C, 0:D].rearrange("p (j q d) -> p j q d", q=2, d=DK)[:, :, r, :],
                                   ACT.Identity).then_inc(vblk_done, 1)

            def take(number, kind, g, parity, part):
                act.wait_ge(piece_done, number + 1)
                if kind == 1:
                    act.activation(xT[:, :, part * 2 * P:(part + 1) * 2 * P], ps[4][:, :].rearrange("p (k n) -> p k n", k=KT),
                                   ACT.Identity).then_inc(piece_copied, 1)
                else:
                    act.activation(qT[:, part, parity, :], ps[4][:, :], ACT.Identity,
                                   bias=bias_q[:, part:part + 1]).then_inc(piece_copied, 1)

            def slot(b, r):
                n, u, v = tile(b, r, 0), tile(b, r, 2), tile(b, r, 3)
                if u is not None:
                    act.wait_ge(probsT, u + 1)
                    need(act, pv, u - 1)
                    act.activation(prT[:, r % 2, :, :], pz[:, 4:6, :].rearrange("p q (j n) -> p (q j) n", j=4),
                                   ACT.Identity).then_inc(probsT_copied, 1)
                if v is not None:
                    act.wait_ge(yT_done, v + 1)
                    need(act, out_done, v - 1)
                    act.activation(yT[:, (r - 3) % 2, :, :], ps[7][:, 0:D].rearrange("p (k n) -> p k n", k=KT),
                                   ACT.Identity).then_inc(yT_copied, 1)
                if n is not None:
                    if piece(b, r):
                        take(*piece(b, r))
                    act.wait_ge(shifted, n + 1)
                    act.activation(pr[:, r % 2, :, :], pr[:, r % 2, :, :], ACT.Exp,
                                   scale=float(DK) ** -0.5).then_inc(probs, 1)

            for p in first_pieces:
                take(*p)
            over_slots(act, slot)

        @block.vector
        def _(dve):
            dve.wait_ge(w_in, 16 * len(loads))
            for c in range(KT):
                dve.wait_ge(k_copied, c + 1)
                dve.tensor_tensor(
                    kblk[:, c, :, :].rearrange("p b (h n) -> p b h n", h=8),
                    kT[:, c, :].rearrange("p (b n) -> p b n", b=B).unsqueeze(2).broadcast_to([P, B, 8, C]),
                    mask[:, :].unsqueeze(1).unsqueeze(3).broadcast_to([P, B, 8, C]), ALU.mult).then_inc(kblk_done, 1)

            def norm(g):
                ch = Chain(dve, dve_steps, 3 * g)
                tiles = X[:, ds(g * GT, GT), :]
                need(dve, x_done, g)
                layer_stats(dve, ch, tiles, stats, mv, spare, GT)
                dve.sem_inc(var_done, 1)
                dve.wait_ge(rstd_done, g + 1)
                for n in range(GT):
                    tp = dve.tensor_scalar(tiles[:, n, :], tiles[:, n, :], mv[:, n, 0:1], rstd[:, n:n + 1],
                                           ALU.subtract, ALU.mult)
                tp.then_inc(x_done, 1)

            def slot(b, r):
                n, u, v = tile(b, r, 0), tile(b, r, 2), tile(b, r, 3)
                if n is not None:
                    dve.wait_ge(scores, n + 1)
                    sc = pz[:, 2 * (r % 2):2 * (r % 2) + 2, :].rearrange("p q (h n) -> p (q h) n", h=8)
                    dve.tensor_reduce(mx[:, r % 2, :], sc, AX.X, ALU.max).then_inc(max_done, 1)
                    dve.wait_ge(max_done, n + 1)
                    dve.tensor_tensor(pr[:, r % 2, :, :], sc,
                                      mx[:, r % 2, :].unsqueeze(2).broadcast_to([P, H, C]), ALU.subtract).then_inc(shifted, 1)
                if u is not None:
                    dve.wait_ge(pv, u + 1)
                    o = ps[6][:, 0:H * (DK + 1)].rearrange("p (h d) -> p h d", h=H)
                    dve.reciprocal(rec[:, r % 2, :], o[:, :, DK]).then_inc(rec_done, 1)
                    dve.wait_ge(rec_done, u + 1)
                    need(dve, yT_done, u - 1)
                    dve.tensor_tensor(y[:, r % 2, :].rearrange("p (h d) -> p h d", h=H), o[:, :, 0:DK],
                                      rec[:, r % 2, :].unsqueeze(2).broadcast_to([P, H, DK]), ALU.mult).then_inc(y_done, 1)
                if v is not None:
                    dve.wait_ge(out_done, v + 1)
                    if (r - 3) % GT == 0:
                        dve.wait_ge(bo_added, b * 2 + 1 + (r - 3) // GT)
                    row = X[:, ds(v, 1), :].rearrange("p o d -> p (o d)")
                    dve.tensor_tensor(row, row, ps[7][:, D:2 * D], ALU.add).then_inc(res_done, 1)
                g = b * 2 + r // GT + 2
                if r % GT == 0 and (not isinstance(b, int) or g < NG):
                    norm(g)

            norm(0)
            norm(1)
            over_slots(dve, slot)


def project_qkv(nc, ctx, t, dram):
    def sb(name, shape, dt=F32):
        return ctx.enter_context(nc.sbuf_tensor("sb_c_" + name, shape, dt))

    def sem(name):
        return ctx.enter_context(nc.semaphore("c_" + name))

    X, ps, pz, ident, neg_half, v_all = t["X"], t["ps"], t["pz"], t["ident"], t["neg_half"], t["v_all"]
    w = sb("w", [P, KT, 3 * D])
    ln_w = sb("ln_w", [P, KT])
    ln_b = sb("ln_b", [P, KT])
    stats = sb("stats", [P, TPB, 6])
    mv = sb("mv", [P, TPB, 2])
    rstd = sb("rstd", [P, TPB])
    xs = sb("xs", [P, TPB, D])
    xT = sb("xT", [P, KT, S])
    parts = sb("parts", [P, 2, 3, S], BF16)
    rest = sb("rest", [P, 2, S])
    w_in, dve_steps = sem("w_in"), sem("dve_steps")
    spare = t["spare"]
    var_done, rstd_done, xs_done, xT_done, xT_copied = (sem(n) for n in (
        "var_done", "rstd_done", "xs_done", "xT_done", "xT_copied"))
    qk_done, high_done, rest_done, mid_done, low_done = (sem(n) for n in (
        "qk_done", "high_done", "rest_done", "mid_done", "low_done"))
    stored = [sem("stored0"), sem("stored1")]
    v_done, v_copied = sem("v_done"), sem("v_copied")
    U = 2 * KT
    loads = [(w[:, :, :], dram["w_qkv"].rearrange("(k p) n -> p k n", p=P)),
             (ln_w[:, :], dram["ln1_w"]), (ln_b[:, :], dram["ln1_b"])]

    with nc.Block() as block:
        @block.sync
        def _(sp):
            for q in stored:
                sp.sem_inc(q, 16)
            for dst, src in loads:
                sp.dma_start(dst, src).then_inc(w_in, 16)
            with sp.Fori(0, B) as b:
                for u in range(U):
                    dst = (dram["q_parts"], dram["k_parts"])[u // KT]
                    sp.wait_ge(high_done, U * b + u + 1)
                    sp.wait_ge(mid_done, U * b + u + 1)
                    sp.wait_ge(low_done, U * b + u + 1)
                    for i in range(3):
                        sp.dma_start(dst[i, ds(b * D + (u % KT) * P, P), :], parts[:, u % 2, i, :]).then_inc(stored[u % 2], 16)
            for q in stored:
                sp.wait_ge(q, 16 + 3 * 16 * B * U // 2)

        @block.gpsimd
        def _(pool):
            def scale(b, r):
                pool.wait_ge(var_done, 2 * b + r + 1)
                pool.tensor_tensor(rstd[:, :], mv[:, :, 1], neg_half[:, :], ALU.pow).then_inc(rstd_done, 1)

            def units(b, last):
                for u in range(U):
                    if u % 2 == 0 and not last:
                        scale(b + 1, u // 2)
                    pool.wait_ge(mid_done, U * b + u + 1)
                    pool.tensor_tensor(parts[:, u % 2, 2, :], rest[:, u % 2, :], parts[:, u % 2, 1, :],
                                       ALU.subtract).then_inc(low_done, 1)

            scale(0, 0)
            scale(0, 1)
            with pool.Fori(0, B - 1) as b:
                units(b, False)
            units(B - 1, True)

        @block.tensor
        def _(pe):
            pe.wait_ge(w_in, 16 * len(loads))
            with pe.Fori(0, B) as b:
                pe.wait_ge(xs_done, 2 * (b + 1))
                pe.wait_ge(v_copied, 1 + TPB // 2 * b)
                for n in range(TPB):
                    for k in range(KT):
                        tr = pe.transpose(ps[2 * (n // 4) + k][:, n % 4 * P:(n % 4 + 1) * P],
                                          xs[:, n, k * P:(k + 1) * P], ident[:, :])
                    if n % 4 == 3:
                        tr.then_inc(xT_done, 1)
                pe.wait_ge(xT_copied, 4 * (b + 1))
                for u in range(U):
                    if u >= 2:
                        pe.wait_ge(rest_done, 1 + U * b + u - 1)
                    else:
                        pe.wait_ge(rest_done, 1 + U * b)
                    for h in range(2):
                        for k in range(KT):
                            mm = pe.matmul(ps[4 + 2 * (u % 2) + h][:, :], w[:, k, u * P:(u + 1) * P],
                                           xT[:, k, h * 512:(h + 1) * 512], start=(k == 0), stop=(k == KT - 1))
                    mm.then_inc(qk_done, 1)
                for n in range(TPB // 2):
                    for r in range(2):
                        i = 2 * n + r
                        for k in range(KT):
                            mm = pe.matmul(ps[n][:, r * D:(r + 1) * D], xT[:, k, i * P:(i + 1) * P],
                                           w[:, k, 2 * D:3 * D], start=(k == 0), stop=(k == KT - 1))
                    mm.then_inc(v_done, 1)

        @block.scalar
        def _(act):
            act.sem_inc(v_copied, 1)
            act.wait_ge(w_in, 16 * len(loads))
            def middle(b, u):
                act.wait_ge(rest_done, 1 + U * b + u + 1)
                act.activation(parts[:, u % 2, 1, :], rest[:, u % 2, :], ACT.Identity).then_inc(mid_done, 1)

            with act.Fori(0, B) as b:
                for h in range(2):
                    act.wait_ge(xT_done, 2 * b + h + 1)
                    for k in range(KT):
                        act.activation(xT[:, k, h * 512:(h + 1) * 512], ps[2 * h + k][:, :], ACT.Identity,
                                       bias=ln_b[:, k:k + 1], scale=ln_w[:, k:k + 1]).then_inc(xT_copied, 1)
                for u in range(U):
                    act.wait_ge(qk_done, U * b + u + 1)
                    act.wait_ge(stored[u % 2], 16 + 48 * (U // 2 * b + u // 2))
                    act.activation(parts[:, u % 2, 0, :], pz[:, 4 + 2 * (u % 2):6 + 2 * (u % 2), :].rearrange("p q n -> p (q n)"),
                                   ACT.Identity, scale=float(DK) ** -0.5 if u < KT else 1.0).then_inc(high_done, 1)
                    if u >= 1:
                        middle(b, u - 1)
                middle(b, U - 1)
                for n in range(TPB // 2):
                    act.wait_ge(v_done, TPB // 2 * b + n + 1)
                    act.activation(v_all[:, ds(b * H, H), 2 * n:2 * n + 2, :],
                                   ps[n][:, :].rearrange("p (r h d) -> p h r d", r=2, h=H), ACT.Identity).then_inc(v_copied, 1)

        @block.vector
        def _(dve):
            dve.sem_inc(rest_done, 1)
            def norm(b, r):
                ch = Chain(dve, dve_steps, 6 * b + 3 * r)
                tiles = X[:, ds(b * TPB, TPB), :]
                layer_stats(dve, ch, tiles, stats, mv, spare)
                dve.sem_inc(var_done, 1)
                dve.wait_ge(rstd_done, 2 * b + r + 1)
                for n in range(TPB):
                    tp = dve.tensor_scalar((tiles, xs)[r][:, n, :], tiles[:, n, :], mv[:, n, 0:1], rstd[:, n:n + 1],
                                           ALU.subtract, ALU.mult)
                tp.then_inc(xs_done, 1)
                dve.wait_ge(xs_done, 2 * b + r + 1)

            def units(b, last):
                for u in range(U):
                    dve.wait_ge(high_done, U * b + u + 1)
                    if u >= 2:
                        dve.wait_ge(low_done, U * b + u - 1)
                    dve.scalar_tensor_tensor(out=rest[:, u % 2, :],
                                             in0=pz[:, 4 + 2 * (u % 2):6 + 2 * (u % 2), :].rearrange("p q n -> p (q n)"),
                                             scalar=float(DK) ** -0.5 if u < KT else 1.0, in1=parts[:, u % 2, 0, :],
                                             op0=ALU.mult, op1=ALU.subtract).then_inc(rest_done, 1)
                    if u % 2 == 0 and not last:
                        norm(b + 1, u // 2)
                dve.wait_ge(low_done, U * (b + 1))

            norm(0, 0)
            norm(0, 1)
            with dve.Fori(0, B - 1) as b:
                units(b, False)
            units(B - 1, True)


def self_attention(nc, ctx, t, dram):
    def sb(name, shape, dt=F32):
        return ctx.enter_context(nc.sbuf_tensor("sb_m_" + name, shape, dt))

    def sem(name):
        return ctx.enter_context(nc.semaphore("m_" + name))

    ps, ident, v_all, y_all = t["ps"], t["ident"], t["v_all"], t["y_all"]
    HEADS = B * H
    R = 6 * DK
    NB = 4
    q_s = sb("q", [R + 3, NB, S], BF16)
    k_s = sb("k", [R + 3, NB, S], BF16)
    v_s = sb("v", [P, 2, TPB, 32])
    pT = sb("pT", [P, 4, S])
    mx2 = sb("mx2", [P, 2, TPB, 2])
    neg_mx = sb("neg_mx", [P, 2, TPB])
    mxT = sb("mxT", [TPB, P])
    mx_rest = sb("mx_rest", [TPB, P])
    mx_parts = sb("mx_parts", [TPB, 2, 3, P], BF16)
    y_raw = sb("y_raw", [P, 256])
    rec = sb("rec", [P, 8])

    q_in = [sem(f"qk_in{i}") for i in range(NB)]
    max_in = [sem(f"max_in{i}") for i in range(NB)]
    set_up, v_in, scores1, maxed, neg_done, mxT_done, mxT_read, split_done = (sem(n) for n in (
        "set_up", "v_in", "scores1", "maxed", "neg_done", "mxT_done", "mxT_read", "split_done"))
    y_rec, spare = sem("y_rec"), t["spare"]
    scores2, exped, pv, y_copied, yT_done, y_stored, pool_steps = (sem(n) for n in (
        "scores2", "exped", "pv", "y_copied", "yT_done", "y_stored", "pool_steps"))
    LINKS1 = 3

    def slots(eng, body):
        for s in range(NB):
            body(s, s, s // NB, 0)
        with eng.Fori(1, HEADS // NB) as it:
            for q in range(NB):
                body(it * NB + q, q, it, None)
        for s in range(HEADS, HEADS + 3):
            body(s, s % NB, s // NB, HEADS)

    def has(s, lag, edge):
        return edge is None or 0 <= s - lag < HEADS

    def turn(par, it, lag):
        return (par - lag) % NB, it + 1 - (1 if par < lag else 0)

    with nc.Block() as block:
        @block.sync
        def _(sp):
            def load(g, i):
                for dst, src, rows in ((q_s, "q_parts", ((0, 3), (0, 2), (0, 1))), (k_s, "k_parts", (0, 1, 2))):
                    at = 0
                    for n, r in zip((3, 2, 1), rows):
                        for j in range(n):
                            part = (r[0] + j) if src == "q_parts" else r
                            sp.dma_start(dst[at:at + DK, i, :], dram[src][part, ds(g * DK, DK), :]).then_inc(q_in[i], 16)
                            at += DK

            load(0, 0)

            def slot(s, par, it, edge):
                if has(s, -1, edge):
                    if not (edge == 0 and s + 1 < NB):
                        sp.wait_ge(scores2, 2 * TPB * (s + 2 - NB))
                    load(s + 1, (par + 1) % NB)
                if has(s, 1, edge):
                    i, _ = turn(par, it, 1)
                    sp.wait_ge(split_done, s)
                    for r in range(3):
                        sp.dma_start(q_s[R + r:R + r + 1, i, :].rearrange("o (t n) -> o t n", t=TPB),
                                     mx_parts[:, (par - 1) % 2, r, :]).then_inc(max_in[i], 16)

            for s in range(NB):
                slot(s, s, 0, 0)
            with sp.Fori(1, HEADS // NB - 1) as it:
                for q in range(NB):
                    slot(it * NB + q, q, it, None)
            for s in range(HEADS - NB, HEADS + 3):
                slot(s, s % NB, s // NB, HEADS)

        @block.gpsimd
        def _(pool):
            pool.memset(v_s[:, :, :, DK + 1:32], 0.0).then_inc(set_up, 1)
            pool.memset(v_s[:, :, :, DK:DK + 1], 1.0).then_inc(set_up, 1)
            pool.wait_ge(set_up, 3)

            def slot(s, par, it, edge):
                if has(s, 2, edge):
                    if not (edge == 0 and s - 4 < 0):
                        pool.wait_ge(pv, TPB * (s - 3))
                    alone(pool, spare)
                    pool.tensor_copy(v_s[:, par % 2, :, 0:DK],
                                     v_all[:, ds(s - 2, 1), :, :].rearrange("p o n d -> p (o n) d")).then_inc(v_in, 1)

                if has(s, 1, edge):
                    c = Chain(pool, pool_steps, (s - 1) * LINKS1)
                    mp = mx_parts[:, (par - 1) % 2, :, :]
                    i, use = turn(par, it, 3)
                    if not (edge == 0 and s < 3):
                        pool.wait_ge(max_in[i], 48 * use)
                    pool.wait_ge(mxT_read, s)
                    alone(pool, spare)
                    c.link(pool.tensor_copy(mp[:, 0, :], mxT[:, :]))
                    c.link(pool.tensor_tensor(mx_rest[:, :], mxT[:, :], mp[:, 0, :], ALU.subtract))
                    alone(pool, spare)
                    c.link(pool.tensor_copy(mp[:, 1, :], mx_rest[:, :]))
                    pool.tensor_tensor(mp[:, 2, :], mx_rest[:, :], mp[:, 1, :], ALU.subtract).then_inc(split_done, 1)

            slots(pool, slot)

        @block.tensor
        def _(pe):
            pe.wait_ge(set_up, 3)

            def free_bank(read, g, par, j, edge):
                n = 2 * TPB * par + j
                if n == 0:
                    need = 2 * TPB * g
                elif n < 3:
                    need = 0
                else:
                    need = 2 * TPB * g + j - 2
                if not isinstance(need, int) or need > 0:
                    pe.wait_ge(read, need)
                return n % 3

            def sums(e, par2, m, edge_first):
                if m == 0 and not edge_first:
                    pe.wait_ge(y_copied, e)
                pe.wait_ge(exped, 2 * TPB * e + 2 * (m + 1))
                for j in range(4):
                    mm = pe.matmul(ps[6][32 * j:32 * j + 32, 0:256], v_s[:, par2, m, :],
                                   pT[:, m % 4, j * 256:(j + 1) * 256], start=(m == 0), stop=(m == TPB - 1),
                                   skip_group_check=True)
                mm.then_inc(pv, 1)

            def slot(s, par, it, edge):
                one, two, three = has(s, 0, edge), has(s, 2, edge), has(s, 3, edge)
                if one:
                    i, use = turn(par, it, 0)
                    pe.wait_ge(q_in[i], 12 * 16 * use)
                if two:
                    i2, use2 = turn(par, it, 2)
                for k in range(TPB):
                    if one:
                        for h in range(2):
                            j = 2 * k + h
                            bank = free_bank(maxed, s, par, j, edge)
                            pe.matmul(ps[bank][:, :], q_s[0:R, i, k * P:(k + 1) * P],
                                      k_s[0:R, i, h * 512:(h + 1) * 512], start=True, stop=True).then_inc(scores1, 1)
                    if two:
                        e = s - 2
                        if k == 0:
                            pe.wait_ge(max_in[i2], 48 * use2)
                            pe.wait_ge(v_in, e + 1)
                        for h in range(2):
                            j = 2 * k + h
                            bank = 3 + free_bank(exped, e, par, j, edge)
                            mm = pe.matmul(ps[bank][:, :], k_s[:, i2, k * P:(k + 1) * P],
                                           q_s[:, i2, h * 512:(h + 1) * 512], start=True, stop=True)
                            mm.then_inc(scores2, 1)
                    if k < 2:
                        if three:
                            sums(s - 3, (par - 3) % 2, TPB - 2 + k, False)
                    elif two:
                        sums(s - 2, par % 2, k - 2, edge == 0 and s == 2)
                    if k == 1 and has(s, 1, edge):
                        pe.wait_ge(neg_done, s)
                        if not (edge == 0 and s < 4):
                            pe.wait_ge(y_stored, s - 3)
                        pe.transpose(ps[7][0:TPB, 0:P], neg_mx[:, (par - 1) % 2, :], ident[:, :]).then_inc(mxT_done, 1)
                    if k == 4 and three:
                        pe.wait_ge(y_copied, s - 2)
                        if has(s, 1, edge):
                            pe.wait_ge(mxT_read, s)
                        else:
                            pe.wait_ge(y_stored, s - 3)
                        for r in range(2):
                            tr = pe.transpose(ps[7][:, r * P:(r + 1) * P], y_raw[:, r * P:(r + 1) * P], ident[:, :])
                        tr.then_inc(yT_done, 1)

            slots(pe, slot)

        @block.scalar
        def _(act):
            def slot(s, par, it, edge):
                two, three = has(s, 2, edge), has(s, 3, edge)
                for k in range(TPB):
                    if two:
                        e = s - 2
                        for h in range(2):
                            j = 2 * k + h
                            act.wait_ge(scores2, 2 * TPB * e + j + 1)
                            if h == 0 and not (edge == 0 and s == 2 and k < 4):
                                act.wait_ge(pv, TPB * e + k - 3)
                            act.activation(pT[:, k % 4, h * 512:(h + 1) * 512], ps[3 + (2 * TPB * par + j) % 3][:, :],
                                           ACT.Exp).then_inc(exped, 1)
                    if k == 2 and has(s, 1, edge):
                        act.wait_ge(mxT_done, s)
                        if not (edge == 0 and s < 2):
                            act.wait_ge(split_done, s - 1)
                        act.activation(mxT[:, :], ps[7][0:TPB, 0:P], ACT.Identity).then_inc(mxT_read, 1)
                    if k == 1 and three:
                        act.wait_ge(pv, TPB * (s - 2))
                        if not (edge == 0 and s == 3):
                            act.wait_ge(yT_done, s - 3)
                        act.activation(y_raw[:, :], ps[6][:, 0:256], ACT.Identity).then_inc(y_copied, 1)

            slots(act, slot)

        @block.vector
        def _(dve):
            dve.memset(k_s[R:R + 3, :, :], 1.0).then_inc(set_up, 1)

            def slot(s, par, it, edge):
                one, three = has(s, 0, edge), has(s, 3, edge)
                for j in range(2 * TPB):
                    if one:
                        dve.wait_ge(scores1, 2 * TPB * s + j + 1)
                        dve.tensor_reduce(mx2[:, par % 2, j // 2, j % 2:j % 2 + 1], ps[(2 * TPB * par + j) % 3][:, :],
                                          AX.X, ALU.max).then_inc(maxed, 1)
                    if j == 0 and has(s, 1, edge):
                        dve.wait_ge(maxed, 2 * TPB * s)
                        dve.tensor_reduce(neg_mx[:, (par - 1) % 2, :], mx2[:, (par - 1) % 2, :, :], AX.X, ALU.max,
                                          negate=True).then_inc(neg_done, 1)
                    yt = ps[7][:, 0:256].rearrange("p (r j d) -> p j r d", r=2, j=4)
                    if j == 10 and three:
                        dve.wait_ge(yT_done, s - 2)
                        dve.reciprocal(rec[:, :].rearrange("p (j r) -> p j r", j=4), yt[:, :, :, DK]).then_inc(y_rec, 1)
                    if j == 11 and three:
                        dve.wait_ge(y_rec, s - 2)
                        dve.tensor_tensor(
                            y_all[:, ds(s - 3, 1), :, :].rearrange("p o (j r) d -> p (o j) r d", j=4), yt[:, :, :, 0:DK],
                            rec[:, :].rearrange("p (j r) -> p j r", j=4).unsqueeze(3).broadcast_to([P, 4, 2, DK]),
                            ALU.mult).then_inc(y_stored, 1)

            slots(dve, slot)


def gate(nc, ctx, t, dram):
    def sb(name, shape, dt=F32):
        return ctx.enter_context(nc.sbuf_tensor("sb_g_" + name, shape, dt))

    def sem(name):
        return ctx.enter_context(nc.semaphore("g_" + name))

    X, Z, ps, pz, ident, neg_half, y_all, logits = (t[n] for n in (
        "X", "Z", "ps", "pz", "ident", "neg_half", "y_all", "logits"))
    E = dram["gate_w"].shape[1]
    w = sb("w", [P, KT, D])
    w_gate = sb("w_gate", [P, KT, E])
    b_gate = sb("b_gate", [1, E])
    ln_w = sb("ln_w", [P, KT])
    ln_b = sb("ln_b", [P, KT])
    ones_row = sb("ones_row", [1, P])
    zeros = sb("zeros", [P, D])
    stats = sb("stats", [P, TPB, 6])
    mv = sb("mv", [P, TPB, 2])
    rstd = sb("rstd", [P, TPB])
    ys = sb("ys", [P, TPB, D])
    x3 = sb("x3", [P, TPB, D])
    yT = sb("yT", [P, KT, S])
    zs = sb("zs", [P, TPB, D])
    zT = sb("zT", [P, KT, S])
    w_in, dve_steps, ready, cleared = sem("w_in"), sem("dve_steps"), sem("ready"), sem("cleared")
    ys_done, yT_done, yT_copied, out_done, res_done = (sem(n) for n in (
        "ys_done", "yT_done", "yT_copied", "out_done", "res_done"))
    spare, x3_added = t["spare"], sem("x3_added")
    var_done, rstd_done, zs_done, z_kept, zT_done, zT_copied, logits_done, logits_copied = (sem(n) for n in (
        "var_done", "rstd_done", "zs_done", "z_kept", "zT_done", "zT_copied", "logits_done", "logits_copied"))
    loads = [(w[:, :, :], dram["w_proj"].rearrange("(k p) n -> p k n", p=P)),
             (w_gate[:, :, :], dram["gate_w"].rearrange("(k p) n -> p k n", p=P)),
             (b_gate[:, :], dram["gate_b"]), (ln_w[:, :], dram["ln2_w"]), (ln_b[:, :], dram["ln2_b"])]

    with nc.Block() as block:
        @block.sync
        def _(sp):
            for dst, src in loads:
                sp.dma_start(dst, src).then_inc(w_in, 16)
            sp.wait_ge(ready, 2)
            sp.dma_start(dram["sorted"].rearrange("(j p) d -> p j d", p=P),
                         zeros[:, :].unsqueeze(1).broadcast_to([P, dram["sorted"].shape[0] // P, D])).then_inc(cleared, 16)
            sp.wait_ge(cleared, 16)

        @block.gpsimd
        def _(pool):
            pool.memset(ones_row[:, :], 1.0).then_inc(ready, 1)
            pool.memset(zeros[:, :], 0.0).then_inc(ready, 1)
            pool.wait_ge(ready, 2)
            pool.sem_inc(x3_added, 1)

            def gather_heads(b):
                pool.wait_ge(yT_done, 1 + 2 * b)
                alone(pool, spare)
                pool.tensor_copy(ys[:, :, :].rearrange("p n (h d) -> p h n d", h=H), y_all[:, ds(b * H, H), :, :]).then_inc(ys_done, 1)

            def batch(b, more):
                pool.wait_ge(var_done, b + 1)
                pool.tensor_tensor(rstd[:, :], mv[:, :, 1], neg_half[:, :], ALU.pow).then_inc(rstd_done, 1)
                if more:
                    gather_heads(b + 2)
                pool.wait_ge(zs_done, b + 1)
                alone(pool, spare)
                pool.tensor_tensor(X[:, ds(b * TPB, TPB), :], X[:, ds(b * TPB, TPB), :], x3[:, :, :], ALU.add).then_inc(x3_added, 1)

            gather_heads(0)
            gather_heads(1)
            with pool.Fori(0, B - 2) as b:
                batch(b, True)
            batch(B - 2, False)
            batch(B - 1, False)

        @block.tensor
        def _(pe):
            pe.sem_inc(yT_done, 1)
            pe.sem_inc(zT_done, 1)

            def project(b):
                pe.wait_ge(ys_done, b + 1)
                if not isinstance(b, int):
                    pe.wait_ge(logits_copied, b)
                for n in range(TPB):
                    for k in range(KT):
                        tr = pe.transpose(ps[2 * (n // 4) + k][:, n % 4 * P:(n % 4 + 1) * P],
                                          ys[:, n, k * P:(k + 1) * P], ident[:, :])
                    if n % 4 == 3:
                        tr.then_inc(yT_done, 1)
                pe.wait_ge(yT_copied, 2 * (b + 1))
                for n in range(TPB):
                    if n == 0:
                        pe.wait_ge(res_done, 1 + TPB // 2 * b)
                    for k in range(KT):
                        mm = pe.matmul(ps[4 + n // 2][:, n % 2 * D:(n % 2 + 1) * D], yT[:, k, n * P:(n + 1) * P],
                                       w[:, k, :], start=(k == 0), stop=(k == KT - 1))
                    if n % 2 == 1:
                        mm.then_inc(out_done, 1)

            def score(b):
                pe.wait_ge(zs_done, b + 1)
                pe.wait_ge(logits_copied, 1 + b)
                for n in range(TPB):
                    for k in range(KT):
                        tr = pe.transpose(ps[2 * (n // 4) + k][:, n % 4 * P:(n % 4 + 1) * P],
                                          zs[:, n, k * P:(k + 1) * P], ident[:, :])
                    if n % 4 == 3:
                        tr.then_inc(zT_done, 1)
                pe.wait_ge(zT_copied, 1 + 4 * (b + 1))
                for n in range(TPB):
                    pe.matmul(ps[0][:, n * E:(n + 1) * E], ones_row[:, :], b_gate[:, :], start=True, stop=False)
                    for k in range(KT):
                        mm = pe.matmul(ps[0][:, n * E:(n + 1) * E], zT[:, k, n * P:(n + 1) * P], w_gate[:, k, :],
                                       start=False, stop=(k == KT - 1))
                mm.then_inc(logits_done, 1)

            pe.wait_ge(w_in, 16 * len(loads))
            pe.wait_ge(ready, 2)
            project(0)
            with pe.Fori(0, B - 1) as b:
                project(b + 1)
                score(b)
            score(B - 1)

        @block.scalar
        def _(act):
            def first(b):
                for h in range(2):
                    act.wait_ge(yT_done, 1 + 2 * b + h + 1)
                    act.activation(yT[:, :, h * 512:(h + 1) * 512], pz[:, 2 * h:2 * h + 2, :], ACT.Identity).then_inc(yT_copied, 1)

            def second(b):
                act.wait_ge(zs_done, b + 1)
                act.activation(Z[:, ds(b * TPB, TPB), :], zs[:, :, :], ACT.Identity).then_inc(z_kept, 1)
                for h in range(2):
                    act.wait_ge(zT_done, 1 + 2 * b + h + 1)
                    for k in range(KT):
                        act.activation(zT[:, k, h * 512:(h + 1) * 512], ps[2 * h + k][:, :], ACT.Identity,
                                       bias=ln_b[:, k:k + 1], scale=ln_w[:, k:k + 1]).then_inc(zT_copied, 1)
                act.wait_ge(logits_done, b + 1)
                act.activation(logits[:, ds(b * TPB, TPB), :], ps[0][:, 0:TPB * E].rearrange("p (n e) -> p n e", n=TPB),
                               ACT.Identity).then_inc(logits_copied, 1)

            act.wait_ge(w_in, 16 * len(loads))
            act.sem_inc(zT_copied, 1)
            act.sem_inc(logits_copied, 1)
            act.sem_inc(z_kept, 1)
            first(0)
            with act.Fori(0, B - 1) as b:
                first(b + 1)
                second(b)
            second(B - 1)

        @block.vector
        def _(dve):
            dve.sem_inc(res_done, 1)
            with dve.Fori(0, B) as b:
                ch = Chain(dve, dve_steps, b * 3)
                tiles = X[:, ds(b * TPB, TPB), :]
                for n in range(TPB // 2):
                    dve.wait_ge(out_done, TPB // 2 * b + n + 1)
                    if n == 0:
                        dve.wait_ge(x3_added, 1 + b)
                    dve.tensor_tensor(x3[:, 2 * n:2 * n + 2, :], tiles[:, 2 * n:2 * n + 2, :],
                                      ps[4 + n][:, :].rearrange("p (r d) -> p r d", r=2), ALU.add).then_inc(res_done, 1)
                dve.wait_ge(res_done, 1 + TPB // 2 * (b + 1))
                layer_stats(dve, ch, x3, stats, mv, spare)
                dve.sem_inc(var_done, 1)
                dve.wait_ge(rstd_done, b + 1)
                dve.wait_ge(z_kept, 1 + b)
                dve.wait_ge(zT_done, 1 + 2 * b)
                for n in range(TPB):
                    tp = dve.tensor_scalar(zs[:, n, :], x3[:, n, :], mv[:, n, 0:1], rstd[:, n:n + 1],
                                           ALU.subtract, ALU.mult)
                tp.then_inc(zs_done, 1)


def route(nc, ctx, t, dram):
    def sb(name, shape, dt=F32):
        return ctx.enter_context(nc.sbuf_tensor("sb_r_" + name, shape, dt))

    def sem(name):
        return ctx.enter_context(nc.semaphore("r_" + name))

    ps, logits, dest, owner, Z = (t[n] for n in ("ps", "logits", "dest", "owner", "Z"))
    E = dram["gate_w"].shape[1]
    J = dram["sorted"].shape[0] // P
    before = sb("before", [P, P])
    every = sb("every", [P, P])
    prefer = sb("prefer", [P, E])
    starts = sb("starts", [P, NT])
    block_no = sb("block_no", [1, J])
    best = sb("best", [P, NT])
    hot = sb("hot", [P, NT, E])
    rank = sb("rank", [P, NT])
    ranked = sb("ranked", [P, NT, E])
    total = sb("total", [P, E, NT])
    until = sb("until", [P, E, NT])
    place = sb("place", [P, E, NT])
    wide = sb("wide", [P, E, NT])
    blocks = sb("blocks", [P, E])
    blocks_until = sb("blocks_until", [P, E])
    base = sb("base", [P, E])
    row = sb("row", [P, NT])
    reached = sb("reached", [1, J, E])
    owner_f = sb("owner_f", [1, J])
    w_in, ones_set, hot_done, counted, steps, dest_done, scattered = (sem(n) for n in (
        "w_in", "ones_set", "hot_done", "counted", "steps", "dest_done", "scattered"))
    loads = [(before[:, :], dram["before"]), (prefer[:, :], dram["prefer"]), (starts[:, :], dram["starts"]),
             (block_no[:, :], dram["block_no"])]

    with nc.Block() as block:
        @block.sync
        def _(sp):
            for dst, src in loads:
                sp.dma_start(dst, src).then_inc(w_in, 16)

        @block.gpsimd
        def _(pool):
            pool.memset(every[:, :], 1.0).then_inc(ones_set, 1)
            pool.wait_ge(dest_done, 1)
            for n in range(NT):
                pool.indirect_dma_start(dram["sorted"], bass.IndirectOffsetOnAxis(ap=dest[:, n:n + 1], axis=0),
                                        Z[:, n, :], None).then_inc(scattered, 16)
            pool.wait_ge(scattered, 16 * NT)

        @block.tensor
        def _(pe):
            pe.wait_ge(w_in, 16 * len(loads))
            pe.wait_ge(ones_set, 1)
            pe.wait_ge(hot_done, 1)
            flat = hot[:, :, :].rearrange("p n e -> p (n e)")
            pe.matmul(ps[0][:, 0:NT * E], before[:, :], flat, start=True, stop=True).then_inc(counted, 1)
            pe.matmul(ps[1][:, 0:NT * E], every[:, :], flat, start=True, stop=True).then_inc(counted, 1)

        @block.vector
        def _(dve):
            dve.wait_ge(w_in, 16 * len(loads))
            ch = Chain(dve, steps)

            def over_e(ap):
                return ap.unsqueeze(2).broadcast_to([P, NT, E])

            ch.link(dve.tensor_reduce(best[:, :], logits[:, :, :], AX.X, ALU.max))
            ch.link(dve.tensor_tensor(hot[:, :, :], logits[:, :, :], over_e(best[:, :]), ALU.is_equal))
            ch.link(dve.tensor_tensor(ranked[:, :, :], hot[:, :, :],
                                      prefer[:, :].unsqueeze(1).broadcast_to([P, NT, E]), ALU.mult))
            ch.link(dve.tensor_reduce(rank[:, :], ranked[:, :, :], AX.X, ALU.max))
            dve.tensor_tensor(hot[:, :, :], over_e(rank[:, :]),
                              prefer[:, :].unsqueeze(1).broadcast_to([P, NT, E]), ALU.is_equal).then_inc(hot_done, 1)
            dve.wait_ge(hot_done, 1)
            dve.wait_ge(counted, 2)
            ch.link(dve.tensor_copy(total[:, :, :], ps[1][:, 0:NT * E].rearrange("p (n e) -> p e n", e=E)))
            for e in range(E):
                sc = dve.tensor_tensor_scan(until[:, e, :], every[:, 0:NT], total[:, e, :], 0.0, ALU.mult, ALU.add)
            ch.link(sc)
            ch.link(dve.tensor_tensor(place[:, :, :], until[:, :, :], total[:, :, :], ALU.subtract))
            ch.link(dve.tensor_tensor(place[:, :, :], place[:, :, :],
                                      ps[0][:, 0:NT * E].rearrange("p (n e) -> p e n", e=E), ALU.add))
            ch.link(dve.tensor_tensor(wide[:, :, :], until[:, :, NT - 1:NT].broadcast_to([P, E, NT]),
                                      starts[:, :].unsqueeze(1).broadcast_to([P, E, NT]), ALU.is_gt))
            ch.link(dve.tensor_reduce(blocks[:, :], wide[:, :, :], AX.X, ALU.add))
            ch.link(dve.tensor_tensor_scan(blocks_until[:, :], every[:, 0:E], blocks[:, :], 0.0, ALU.mult, ALU.add))
            ch.link(dve.tensor_tensor(base[:, :], blocks_until[:, :], blocks[:, :], ALU.subtract))
            ch.link(dve.tensor_scalar(base[:, :], base[:, :], float(P), None, ALU.mult))
            ch.link(dve.tensor_tensor(place[:, :, :], place[:, :, :],
                                      base[:, :].unsqueeze(2).broadcast_to([P, E, NT]), ALU.add))
            ch.link(dve.tensor_tensor(ranked[:, :, :], place[:, :, :].rearrange("p e n -> p n e"), hot[:, :, :], ALU.mult))
            ch.link(dve.tensor_reduce(row[:, :], ranked[:, :, :], AX.X, ALU.add))
            dve.tensor_copy(dest[:, :], row[:, :]).then_inc(dest_done, 1)
            ch.link(dve.tensor_tensor(reached[:, :, :], blocks_until[0:1, :].unsqueeze(1).broadcast_to([1, J, E]),
                                      block_no[:, :].unsqueeze(2).broadcast_to([1, J, E]), ALU.is_le))
            ch.link(dve.tensor_reduce(owner_f[:, :], reached[:, :, :], AX.X, ALU.add))
            ch.link(dve.tensor_scalar(owner_f[:, :], owner_f[:, :], float(E - 1), None, ALU.min))
            ch.link(dve.tensor_copy(owner[:, :], owner_f[:, :]))


def experts(nc, ctx, t, dram):
    def sb(name, shape, dt=F32):
        return ctx.enter_context(nc.sbuf_tensor("sb_e_" + name, shape, dt))

    def sem(name):
        return ctx.enter_context(nc.semaphore("e_" + name))

    ps, pz, ident, owner = (t[n] for n in ("ps", "pz", "ident", "owner"))
    E, _, HID = dram["w1"].shape
    HT = HID // P
    J = dram["sorted"].shape[0] // P
    W = 3
    assert J % W == 0
    w1 = sb("w1", [P, W, KT, HID])
    w2 = sb("w2", [P, E, HT, D])
    ln_w = sb("ln_w", [P, KT])
    ln_b = sb("ln_b", [P, KT])
    x_in = sb("x_in", [P, W, D])
    xT = sb("xT", [P, W, KT, P])
    hT = sb("hT", [P, W, HT, P])
    y = sb("y", [P, W, D])
    w2_in, ln_in = sem("w2_in"), sem("ln_in")
    rows_in = [sem(f"rows_in{i}") for i in range(W)]
    w1_in = [sem(f"w1_in{i}") for i in range(W)]
    stored = [sem(f"stored{i}") for i in range(W)]
    xT_done, xT_copied, h_done, h_copied, y_done, y_copied = (sem(n) for n in (
        "xT_done", "xT_copied", "h_done", "h_copied", "y_done", "y_copied"))
    rows = dram["sorted"].rearrange("(j p) d -> j p d", p=P)
    rows_out = dram["sorted_out"].rearrange("(j p) d -> j p d", p=P)

    with nc.Block() as block:
        @block.sync
        def _(sp):
            for q in stored:
                sp.sem_inc(q, 16)
            sp.dma_start(ln_w[:, :], dram["ln2_w"]).then_inc(ln_in, 16)
            sp.dma_start(ln_b[:, :], dram["ln2_b"]).then_inc(ln_in, 16)

            def load(j, q, first):
                if not first:
                    sp.wait_ge(xT_done, j - W + 1)
                sp.dma_start(x_in[:, q, :], rows[ds(j, 1), :, :].rearrange("o p d -> p (o d)")).then_inc(rows_in[q], 16)
                e = sp.value_load(owner[0:1, ds(j, 1)], min_val=0, max_val=E - 1)
                if not first:
                    sp.wait_ge(h_done, 2 * (j - W + 1))
                sp.dma_start(w1[:, q, :, :], dram["w1"][ds(e, 1), :, :].rearrange("o (k p) n -> p (o k) n", p=P)).then_inc(w1_in[q], 16)

            for q in range(W):
                load(q, q, True)
                if q == 0:
                    for e in range(E):
                        sp.dma_start(w2[:, e, :, :], dram["w2"][e].rearrange("(k p) n -> p k n", p=P)).then_inc(w2_in, 16)

            def store(j, q):
                sp.wait_ge(y_copied, 1 + j + 1)
                sp.dma_start(rows_out[ds(j, 1), :, :].rearrange("o p d -> p (o d)"), y[:, q, :]).then_inc(stored[q], 16)

            with sp.Fori(1, J // W) as it:
                for q in range(W):
                    store(it * W + q - W, q)
                    load(it * W + q, q, False)
            for q in range(W):
                store(J - W + q, q)
            for q in range(W):
                sp.wait_ge(stored[q], 16 + 16 * (J // W))

        @block.tensor
        def _(pe):
            def turn(j, it, q):
                pe.wait_ge(rows_in[q], 16 * (it + 1))
                pe.wait_ge(xT_copied, 2 * j)
                for k in range(KT):
                    tr = pe.transpose(ps[7][:, k * P:(k + 1) * P], x_in[:, q, k * P:(k + 1) * P], ident[:, :])
                tr.then_inc(xT_done, 1)

            def up(j, it, q):
                pe.wait_ge(xT_copied, 2 * (j + 1))
                pe.wait_ge(w1_in[q], 16 * (it + 1))
                for m in range(HT):
                    for k in range(KT):
                        mm = pe.matmul(ps[2 * q + m // 4][:, m % 4 * P:(m % 4 + 1) * P],
                                       w1[:, q, k, m * P:(m + 1) * P], xT[:, q, k, :], start=(k == 0), stop=(k == KT - 1))
                    if m % 4 == 3:
                        mm.then_inc(h_done, 1)

            def down(j, q):
                e = pe.value_load(owner[0:1, ds(j, 1)], min_val=0, max_val=E - 1)
                pe.wait_ge(y_copied, 1 + j)
                for m in range(HT):
                    if m % 4 == 0:
                        pe.wait_ge(h_copied, 2 * j + m // 4 + 1)
                    mm = pe.matmul(ps[6][:, 0:D], hT[:, q, m, :],
                                   w2[:, ds(e, 1), m, :].rearrange("p o n -> p (o n)"), start=(m == 0), stop=(m == HT - 1))
                mm.then_inc(y_done, 1)

            turn(0, 0, 0)
            up(0, 0, 0)
            turn(1, 0, 1)
            pe.wait_ge(w2_in, 16 * E)
            with pe.Fori(0, J // W - 1) as it:
                for q in range(W):
                    j = it * W + q
                    up(j + 1, it + (q + 1) // W, (q + 1) % W)
                    turn(j + 2, it + (q + 2) // W, (q + 2) % W)
                    down(j, q)
            for q in range(W):
                j = J - W + q
                if j + 1 < J:
                    up(j + 1, J // W - 1, q + 1)
                if j + 2 < J:
                    turn(j + 2, J // W - 1, q + 2)
                down(j, q)

        @block.scalar
        def _(act):
            with act.Fori(0, J // W) as it:
                for q in range(W):
                    j = it * W + q
                    for h in range(2):
                        act.wait_ge(h_done, 2 * j + h + 1)
                        act.activation(hT[:, q, 4 * h:4 * h + 4, :], ps[2 * q + h][:, :].rearrange("p (m n) -> p m n", m=4),
                                       ACT.Gelu_apprx_tanh).then_inc(h_copied, 1)

        @block.vector
        def _(dve):
            dve.sem_inc(y_copied, 1)
            dve.wait_ge(ln_in, 32)

            def turned(j, q):
                dve.wait_ge(xT_done, j + 1)
                for k in range(KT):
                    dve.tensor_scalar(xT[:, q, k, :], ps[7][:, k * P:(k + 1) * P], ln_w[:, k:k + 1], ln_b[:, k:k + 1],
                                      ALU.mult, ALU.add).then_inc(xT_copied, 1)

            def result(j, it, q):
                dve.wait_ge(y_done, j + 1)
                dve.wait_ge(stored[q], 16 + 16 * it)
                dve.tensor_copy(y[:, q, :], ps[6][:, 0:D]).then_inc(y_copied, 1)

            turned(0, 0)
            turned(1, 1)
            with dve.Fori(0, J // W - 1) as it:
                for q in range(W):
                    turned(it * W + q + 2, (q + 2) % W)
                    result(it * W + q, it, q)
            for q in range(W):
                if q + 2 < W:
                    turned(J - W + q + 2, q + 2)
                result(J - W + q, J // W - 1, q)


def finish(nc, ctx, t, dram, out):
    def sb(name, shape, dt=F32):
        return ctx.enter_context(nc.sbuf_tensor("sb_f_" + name, shape, dt))

    def sem(name):
        return ctx.enter_context(nc.semaphore("f_" + name))

    X, dest, Y, neg_half = (t[n] for n in ("X", "dest", "Z", "neg_half"))
    stats = sb("stats", [P, TPB, 6])
    mv = sb("mv", [P, TPB, 2])
    rstd = sb("rstd", [P, TPB])
    gathered = [sem(f"gathered{b}") for b in range(B)]
    spare = t["spare"]
    summed, dve_steps, var_done, rstd_done, normed, stored = (sem(n) for n in (
        "summed", "dve_steps", "var_done", "rstd_done", "normed", "stored"))

    with nc.Block() as block:
        @block.gpsimd
        def _(pool):
            for n in range(NT + TPB):
                if n >= TPB and n % TPB == TPB - 1:
                    b = n // TPB - 1
                    pool.wait_ge(var_done, b + 1)
                    pool.tensor_tensor(rstd[:, :], mv[:, :, 1], neg_half[:, :], ALU.pow).then_inc(rstd_done, 1)
                if n >= NT:
                    continue
                pool.indirect_dma_start(Y[:, n, :], None, dram["sorted_out"],
                                        bass.IndirectOffsetOnAxis(ap=dest[:, n:n + 1], axis=0)).then_inc(gathered[n // TPB], 16)

        @block.vector
        def _(dve):
            ch = Chain(dve, dve_steps)
            for b in range(B):
                dve.wait_ge(gathered[b], 16 * TPB)
                tiles = X[:, b * TPB:(b + 1) * TPB, :]
                ch.link(dve.tensor_tensor(tiles, tiles, Y[:, b * TPB:(b + 1) * TPB, :], ALU.add))
                layer_stats(dve, ch, tiles, stats, mv, spare)
                dve.sem_inc(var_done, 1)
                dve.wait_ge(rstd_done, b + 1)
                for n in range(TPB):
                    tp = dve.tensor_scalar(tiles[:, n, :], tiles[:, n, :], mv[:, n, 0:1], rstd[:, n:n + 1],
                                           ALU.subtract, ALU.mult)
                tp.then_inc(normed, 1)

        @block.sync
        def _(sp):
            for b in range(B):
                sp.wait_ge(normed, b + 1)
                sp.dma_start(out[b].rearrange("(n p) d -> p n d", p=P), X[:, b * TPB:(b + 1) * TPB, :]).then_inc(stored, 16)
            sp.wait_ge(stored, 16 * B)


def decoder(nc, dram, out):
    E = dram["gate_w"].shape[1]
    J = B * S // P + E - 1
    dram["q_parts"] = nc.dram_tensor("q_parts", (3, B * D, S), BF16).ap()
    dram["k_parts"] = nc.dram_tensor("k_parts", (3, B * D, S), BF16).ap()
    dram["sorted"] = nc.dram_tensor("sorted", (J * P, D), F32).ap()
    dram["sorted_out"] = nc.dram_tensor("sorted_out", (J * P, D), F32).ap()
    with ExitStack() as ctx:
        def sb(name, shape, dt=F32):
            return ctx.enter_context(nc.sbuf_tensor(name, shape, dt))

        t = {}
        pz = ctx.enter_context(nc.psum_tensor("banks", [P, 8, 512], F32))
        t["pz"], t["ps"] = pz, [pz[:, i, :] for i in range(8)]
        t["X"] = sb("X", [P, NT, D])
        t["ident"] = sb("ident_sb", [P, P])
        t["neg_half"] = sb("neg_half", [P, TPB])
        t["spare"] = ctx.enter_context(nc.semaphore("spare"))
        ident_in = ctx.enter_context(nc.semaphore("ident_in"))
        with nc.Block() as block:
            @block.sync
            def _(sp):
                sp.dma_start(t["ident"][:, :], dram["ident"]).then_inc(ident_in, 16)
                sp.wait_ge(ident_in, 17)

            @block.vector
            def _(dve):
                dve.memset(t["neg_half"][:, :], -0.5).then_inc(ident_in, 1)
        for stage in (autocorrelation, cross_attention):
            with ExitStack() as own:
                stage(nc, own, t, dram)
        with ExitStack() as attention:
            t["y_all"] = attention.enter_context(nc.sbuf_tensor("y_all", [P, B * H, TPB, DK], F32))
            with ExitStack() as own:
                t["v_all"] = own.enter_context(nc.sbuf_tensor("v_all", [P, B * H, TPB, DK], F32))
                with ExitStack() as inner:
                    project_qkv(nc, inner, t, dram)
                with ExitStack() as inner:
                    self_attention(nc, inner, t, dram)
            t["Z"] = attention.enter_context(nc.sbuf_tensor("Z", [P, NT, D], F32))
            t["logits"] = attention.enter_context(nc.sbuf_tensor("logits", [P, NT, E], F32))
            t["dest"] = attention.enter_context(nc.sbuf_tensor("dest", [P, NT], U32))
            t["owner"] = attention.enter_context(nc.sbuf_tensor("owner", [1, J], I32))
            for stage in (gate, route, experts):
                with ExitStack() as own:
                    stage(nc, own, t, dram)
            with ExitStack() as own:
                finish(nc, own, t, dram, out)


def dft_constants():
    s = np.arange(S)
    ang = 2 * np.pi / S
    odd, two, zero = np.arange(1, S // 2, 2), np.arange(2, S // 2, 4), np.arange(0, S // 2, 4)
    a = ang * ((s[:512, None] * odd[None]) % S)
    fwd_odd = np.concatenate([np.cos(a), -np.sin(a)], 1)
    inv_odd = np.concatenate([np.cos(a), -np.sin(a)], 1).T * (2 / S)
    q = s[:256, None]
    a2, a0 = ang * ((q * two[None]) % S), ang * ((q * zero[None]) % S)
    f2 = np.concatenate([np.cos(a2), -np.sin(a2)], 1)
    f0 = np.concatenate([np.cos(a0), -np.sin(a0)], 1)
    f0[:, 128] = (-1.0) ** s[:256]
    i2 = f2.T * (2 / S)
    i0 = f0.T * (2 / S)
    i0[0] /= 2
    i0[128] /= 2
    return (fwd_odd.astype(np.float32), np.concatenate([f2, f0], 0).astype(np.float32),
            inv_odd.astype(np.float32), np.concatenate([i2, i0], 0).astype(np.float32))


def kernel(**inputs):
    import concourse.bacc as bacc
    from concourse.bass_utils import run_bass_kernel_spmd

    def layout(a):
        return np.ascontiguousarray(a)

    def columns(v):
        return layout(np.asarray(v).reshape(-1, P).T)

    f = {n: np.asarray(v) for n, v in inputs.items()}
    E = f["L0_ffn_gate_w"].shape[1]
    J = B * S // P + E - 1
    fwd_odd, fwd_even, inv_odd, inv_even = dft_constants()
    p = np.arange(P)
    at_zero = np.zeros((1, P), np.float32)
    at_zero[0, 0] = S
    arrays = {
        "fwd_odd": fwd_odd, "fwd_even": fwd_even, "inv_odd": inv_odd, "inv_even": inv_even, "f0": at_zero,
        "head_mask": (p[:, None] // DK == np.arange(TOP)[None]).astype(np.float32),
        "ident": np.eye(P, dtype=np.float32),
        "before": (p[:, None] < p[None]).astype(np.float32),
        "prefer": np.tile(np.arange(E, 0, -1, dtype=np.float32), (P, 1)),
        "starts": np.tile(np.arange(NT, dtype=np.float32) * P, (P, 1)),
        "block_no": np.arange(J, dtype=np.float32)[None],
        "x": layout(f["x"]),
        "xT16": layout(f["x"][:, :DK, :].transpose(2, 0, 1).reshape(D, B * DK)),
        "L0_attn_Wq": layout(f["L0_attn_Wq"]), "L0_attn_Wk": layout(f["L0_attn_Wk"]),
        "L0_attn_Wv": layout(f["L0_attn_Wv"]), "L0_attn_Wo": layout(f["L0_attn_Wo"]),
        "b_qk": np.concatenate([f["L0_attn_bq"], f["L0_attn_bk"]])[None],
        "bv_attn": columns(f["L0_attn_bv"]), "bo_attn": layout(f["L0_attn_bo"][None]),
        "WqT": layout(f["L0_xattn_Wq"].T), "WkvT": layout(f["L0_xattn_Wkv"].T), "WoT": layout(f["L0_xattn_Wo"].T),
        "ctxT": layout(f["ctx_1024"].transpose(2, 0, 1).reshape(D, -1)),
        "bq_cross": columns(f["L0_xattn_bq"]), "bk_cross": columns(f["L0_xattn_bkv"][:D]),
        "bv_cross": layout(f["L0_xattn_bkv"][None, D:]), "bo_cross": layout(f["L0_xattn_bo"][None]),
        "w_qkv": layout(f["L0_ffn_w_qkv"]), "w_proj": layout(f["L0_ffn_w_proj"]),
        "ln1_w": columns(f["L0_ffn_ln1_w"]), "ln1_b": columns(f["L0_ffn_ln1_b"]),
        "ln2_w": columns(f["L0_ffn_ln2_w"]), "ln2_b": columns(f["L0_ffn_ln2_b"]),
        "gate_w": layout(f["L0_ffn_gate_w"]), "gate_b": layout(f["L0_ffn_gate_b"][None]),
        "w1": layout(f["L0_ffn_w1"]), "w2": layout(f["L0_ffn_w2"]),
    }
    nc = bacc.Bacc("TRN2", target_bir_lowering=False, num_devices=1)
    given, dram = {}, {}
    for name, a in arrays.items():
        given[f"in_{name}"] = a
        dram[name] = nc.dram_tensor(f"in_{name}", a.shape, mybir.dt.from_np(a.dtype), kind="ExternalInput").ap()
    out = nc.dram_tensor("out_x", (B, S, D), F32, kind="ExternalOutput").ap()
    decoder(nc, dram, out)
    r = run_bass_kernel_spmd(nc, [given], core_ids=[0])
    return r.results[0]["out_x"]
```

```python
from contextlib import ExitStack

import numpy as np

import concourse.bass as bass
from concourse import mybir

F32 = mybir.dt.float32
BF16 = mybir.dt.bfloat16
I32 = mybir.dt.int32
U32 = mybir.dt.uint32
ALU = mybir.AluOpType
ACT = mybir.ActivationFunctionType
AX = mybir.AxisListType
ds = bass.ds

B, S, D, H = 4, 1024, 256, 16
DK = D // H
P = 128
TPB = S // P
NT = B * TPB
KT = D // P
EPS = 1e-5
TOP = 8
G = B * KT
EXP_ZERO = -104.0
LOWEST = -3.0e38


class Chain:

    def __init__(self, eng, sem, base=0):
        self.eng, self.sem, self.base, self.n = eng, sem, base, 0

    def link(self, ins):
        self.n += 1
        ins.then_inc(self.sem, 1)
        self.eng.wait_ge(self.sem, self.base + self.n)


def autocorrelation(nc, ctx, t, dram):
    def sb(name, shape, dt=F32):
        return ctx.enter_context(nc.sbuf_tensor("sb_" + name, shape, dt))

    def sem(name):
        return ctx.enter_context(nc.semaphore(name))

    X, ps = t["X"], t["ps"]
    fold = sb("fold", [P, TPB, D])
    even = sb("even", [P, 4, D])
    fwd_odd = sb("fwd_odd", [P, 4, 512])
    fwd_even = sb("fwd_even", [P, 4, 256])
    inv_odd = sb("inv_odd", [P, 4, 512])
    inv_even = sb("inv_even", [P, 4, 256])
    w_qk = sb("w_qk", [P, KT, 2 * D])
    w_v = sb("w_v", [P, KT, D])
    w_o = sb("w_o", [P, KT, D])
    b_qk = sb("b_qk", [1, 2 * D])
    b_v = sb("b_v", [P, KT])
    bo = sb("bo", [P, D])
    f0 = sb("f0", [1, P])
    xT16 = sb("xT16", [P, KT, B * DK])
    head_mask = sb("head_mask", [P, TOP])
    vT = sb("vT", [P, KT, B * DK])
    vblk = sb("vblk", [P, KT, B, P])
    vwo = sb("vwo", [P, G, D])
    xfT = sb("xfT", [P, KT, 2, 512])
    qk = sb("qk", [P, 8, 2 * D])
    cross = sb("cross", [P, 8, D])
    prod = sb("prod", [P, 4, D])
    corr = sb("corr", [P, G, S])
    w_sort = sb("w_sort", [P, G, S])
    uv = sb("uv", [P, KT, 2, 256])
    m8 = sb("m8", [P, G, TOP])
    d8 = sb("d8", [P, G, TOP])
    e8 = sb("e8", [P, G, TOP])
    wsum = sb("wsum", [P, G])
    wrec = sb("wrec", [P, G])
    neg_m = sb("neg_m", [P, G])
    ones = sb("ones_a", [P, 1])
    tail = sb("tail", [P, 2])
    tail_flag = sb("tail_flag", [1, 1], I32)
    cur8 = sb("cur8", [P, TOP])

    x_in = [sem(f"a_x_in{b}") for b in range(B)]
    fwd_in, qk_in, inv_in, v_in, bo_in = (sem("a_" + n) for n in ("fwd_in", "qk_in", "inv_in", "v_in", "bo_in"))
    zeroed, folded, spectrum, spectrum_T = sem("a_zeroed"), sem("a_folded"), sem("a_spectrum"), sem("a_spectrum_T")
    qk_done, qk_copied, cross_done = sem("a_qk_done"), sem("a_qk_copied"), sem("a_cross_done")
    inv_done, corr_done = sem("a_inv_done"), sem("a_corr_done")
    bo_added = sem("a_bo_added")
    v_done, v_copied, vblk_done, vwo_done, vwo_copied = (sem("a_" + n) for n in (
        "v_done", "v_copied", "vblk_done", "vwo_done", "vwo_copied"))
    tail_local, tail_counted, flag_set = sem("a_tail_local"), sem("a_tail_counted"), sem("a_flag_set")
    diffs, exps, weights, y_done = sem("a_diffs"), sem("a_exps"), sem("a_weights"), sem("a_y_done")
    fold_steps, cross_steps, corr_steps, dve_steps, sort_steps = (sem("a_" + n) for n in (
        "fold_steps", "cross_steps", "corr_steps", "dve_steps", "sort_steps"))
    sorted_done, gen_exps, gen_weights, gen_y, gen_added = (sem("a_" + n) for n in (
        "sorted", "gen_exps", "gen_weights", "gen_y", "gen_added"))

    with nc.Block() as block:
        @block.sync
        def _(sp):
            def load(name, dst, signal):
                sp.dma_start(dst, dram[name].rearrange("(k p) n -> p k n", p=P)).then_inc(signal, 16)

            def load_x(b):
                sp.dma_start(X[:, b * TPB:(b + 1) * TPB, :],
                             dram["x"][b].rearrange("(n p) d -> p n d", p=P)).then_inc(x_in[b], 16)

            load_x(0)
            load("fwd_odd", fwd_odd[:, :, :], fwd_in)
            load("fwd_even", fwd_even[:, :, :], fwd_in)
            load("L0_attn_Wq", w_qk[:, :, 0:D], qk_in)
            load("L0_attn_Wk", w_qk[:, :, D:2 * D], qk_in)
            sp.dma_start(b_qk[:, :], dram["b_qk"]).then_inc(qk_in, 16)
            sp.dma_start(f0[:, :], dram["f0"]).then_inc(qk_in, 16)
            for b in range(1, B):
                load_x(b)
            load("inv_odd", inv_odd[:, :, :], inv_in)
            load("inv_even", inv_even[:, :, :], inv_in)
            sp.dma_start(bo[:, :], dram["bo_attn"].partition_broadcast(P)).then_inc(bo_in, 16)
            load("L0_attn_Wv", w_v[:, :, :], v_in)
            load("L0_attn_Wo", w_o[:, :, :], v_in)
            load("xT16", xT16[:, :, :], v_in)
            sp.dma_start(b_v[:, :], dram["bv_attn"]).then_inc(v_in, 16)
            sp.dma_start(head_mask[:, :], dram["head_mask"]).then_inc(v_in, 16)
            sp.dma_start(t["ident"][:, :], dram["ident"]).then_inc(t["common_in"], 16)
            sp.wait_ge(t["common_in"], 17)

        @block.gpsimd
        def _(pool):
            pool.memset(t["neg_half"][:, :], -0.5).then_inc(t["common_in"], 1)
            pool.memset(ones[:, :], 1.0).then_inc(zeroed, 1)
            pool.memset(w_sort[:, :, :], 0.0).then_inc(zeroed, 1)
            pool.wait_ge(bo_in, 16)
            with pool.Fori(0, B) as b:
                pool.wait_ge(folded, b + 1)
                pool.tensor_tensor(X[:, ds(b * TPB, TPB), :], X[:, ds(b * TPB, TPB), :],
                                   bo[:, :].unsqueeze(1).broadcast_to([P, TPB, D]), ALU.add).then_inc(bo_added, 1)

        @block.tensor
        def _(pe):
            def forward(b):
                pe.wait_ge(folded, b + 1)
                for c in range(KT):
                    for k in range(4):
                        mm = pe.matmul(ps[c][:, :], fold[:, k, c * P:(c + 1) * P], fwd_odd[:, k, :],
                                       start=(k == 0), stop=(k == 3))
                    mm.then_inc(spectrum, 1)
                    for h in range(2):
                        for k in range(2):
                            mm = pe.matmul(ps[2 + c][:, h * 256:(h + 1) * 256],
                                           fold[:, 4 + 2 * h + k, c * P:(c + 1) * P], fwd_even[:, 2 * h + k, :],
                                           start=(k == 0), stop=(k == 1))
                    mm.then_inc(spectrum, 1)

            def batch(b, last):
                pe.wait_ge(spectrum_T, 6 * (b + 1))
                if last:
                    pe.wait_ge(v_in, 80)
                    for c in range(KT):
                        for k in range(KT):
                            mm = pe.matmul(ps[c][:, 0:B * DK], w_v[:, k, c * P:(c + 1) * P], xT16[:, k, :],
                                           start=(k == 0), stop=(k == KT - 1))
                        mm.then_inc(v_done, 1)
                for f in range(8):
                    r, q = f // 4, f % 4
                    if f < 4 and f % 2 == 0:
                        pe.wait_ge(corr_done, 2 + KT * b - 1 + f // 2)
                    elif f >= 4:
                        pe.wait_ge(qk_copied, 8 * b + f - 3)
                    for k in range(KT):
                        mm = pe.matmul(ps[4 + f % 4][:, :], xfT[:, k, r, q * P:(q + 1) * P], w_qk[:, k, :],
                                       start=(k == 0), stop=(k == KT - 1 and f != 3))
                    if f == 3:
                        mm = pe.matmul(ps[7][:, :], f0[:, :], b_qk[:, :], start=False, stop=True)
                    mm.then_inc(qk_done, 1)
                if last:
                    pe.wait_ge(vblk_done, KT)
                    pe.wait_ge(v_copied, KT)
                    for n in range(B):
                        for c in range(KT):
                            pe.matmul(ps[n][:, c * D:(c + 1) * D], vblk[:, c, n, :], w_o[:, c, :],
                                      start=True, stop=True).then_inc(vwo_done, 1)
                else:
                    forward(b + 1)
                pe.wait_ge(cross_done, b + 2)
                for c in range(KT):
                    cs = slice(c * P, (c + 1) * P)
                    for n, f in enumerate((0, 1, 4, 5)):
                        pe.matmul(ps[4 + 2 * c][:, :], cross[:, f, cs], inv_odd[:, n, :], start=(n == 0), stop=(n == 3))
                    for h in range(2):
                        for n in range(2):
                            mm = pe.matmul(ps[5 + 2 * c][:, h * 256:(h + 1) * 256], cross[:, 2 + h + 4 * n, cs],
                                           inv_even[:, 2 * h + n, :], start=(n == 0), stop=(n == 1))
                    mm.then_inc(inv_done, 1)

            pe.wait_ge(fwd_in, 32)
            forward(0)
            pe.wait_ge(qk_in, 64)
            pe.wait_ge(inv_in, 32)
            with pe.Fori(0, B - 1) as b:
                batch(b, False)
            batch(B - 1, True)
            pe.wait_ge(tail_local, 1)
            pe.wait_ge(zeroed, 1)
            pe.matmul(ps[7][0:1, 0:1], tail[:, 1:2], ones[:, :], start=True, stop=True).then_inc(tail_counted, 1)
            pe.wait_ge(flag_set, 1)
            pe.wait_ge(vwo_copied, B)
            general = pe.value_load(tail_flag[0:1, 0:1], min_val=0, max_val=P)
            with pe.If(general > 0):
                pe.wait_ge(gen_weights, G)
                for b in range(B):
                    for i in range(1, TPB):
                        n = b * (TPB - 1) + i - 1
                        if n >= 4:
                            pe.wait_ge(gen_added, n - 3)
                        for k in range(KT):
                            mm = pe.matmul(ps[n % 4][:, 0:D], w_sort[:, b * KT + k, i * P:(i + 1) * P],
                                           vwo[:, b * KT + k, :], start=(k == 0), stop=(k == KT - 1))
                        mm.then_inc(gen_y, 1)
                pe.nop()
            pe.wait_ge(weights, 1)
            for b in range(B):
                for k in range(KT):
                    mm = pe.matmul(ps[4 + b][:, 0:D], w_sort[:, b * KT + k, 0:P], vwo[:, b * KT + k, :],
                                   start=(k == 0), stop=(k == KT - 1))
                mm.then_inc(y_done, 1)

        @block.scalar
        def _(act):
            def turned(b):
                for c in range(KT):
                    act.wait_ge(spectrum, 4 * b + 2 * c + 1)
                    act.activation(xfT[:, c, :, 0:256], ps[c][:, :].rearrange("p (r n) -> p r n", r=2),
                                   ACT.Identity).then_inc(spectrum_T, 1)
                    act.wait_ge(spectrum, 4 * b + 2 * c + 2)
                    for h in range(2):
                        act.activation(xfT[:, c, :, 256 + h * P:256 + (h + 1) * P],
                                       ps[2 + c][:, h * 256:(h + 1) * 256].rearrange("p (r n) -> p r n", r=2),
                                       ACT.Identity).then_inc(spectrum_T, 1)

            def batch(b, last):
                act.wait_ge(cross_done, b + 1)
                if last:
                    act.wait_ge(v_in, 80)
                    for c in range(KT):
                        act.wait_ge(v_done, c + 1)
                        act.activation(vT[:, c, :], ps[c][:, 0:B * DK], ACT.Identity, bias=b_v[:, c:c + 1]).then_inc(v_copied, 1)
                for f in range(8):
                    act.wait_ge(qk_done, 8 * b + f + 1)
                    act.activation(qk[:, f, :], ps[4 + f % 4][:, :], ACT.Identity).then_inc(qk_copied, 1)
                if not last:
                    turned(b + 1)

            turned(0)
            with act.Fori(0, B - 1) as b:
                batch(b, False)
            batch(B - 1, True)
            for b in range(B):
                act.wait_ge(vwo_done, 2 * (b + 1))
                act.activation(vwo[:, b * KT:(b + 1) * KT, :], ps[b][:, :].rearrange("p (k n) -> p k n", k=KT),
                               ACT.Identity).then_inc(vwo_copied, 1)
            act.wait_ge(diffs, 1)
            act.activation(e8[:, :, :], d8[:, :, :], ACT.Exp).then_inc(exps, 1)
            act.wait_ge(flag_set, 1)
            general = act.value_load(tail_flag[0:1, 0:1], min_val=0, max_val=P)
            with act.If(general > 0):
                for g in range(G):
                    act.wait_ge(sorted_done, g + 1)
                    act.activation(w_sort[:, g, :], w_sort[:, g, :], ACT.Exp, bias=neg_m[:, g:g + 1],
                                   accum_out=wsum[:, g:g + 1]).then_inc(gen_exps, 1)
                act.nop()

        @block.vector
        def _(dve):
            dve.sem_inc(cross_done, 1)
            dve.sem_inc(corr_done, 2)

            def folding(b):
                lo, hi = X[:, ds(b * TPB, 4), :], X[:, ds(b * TPB + 4, 4), :]
                ch = Chain(dve, fold_steps, b)
                dve.tensor_tensor(fold[:, 0:4, :], lo, hi, ALU.subtract)
                ch.link(dve.tensor_tensor(even[:, :, :], lo, hi, ALU.add))
                dve.tensor_tensor(fold[:, 4:6, :], even[:, 0:2, :], even[:, 2:4, :], ALU.subtract)
                dve.tensor_tensor(fold[:, 6:8, :], even[:, 0:2, :], even[:, 2:4, :], ALU.add).then_inc(folded, 1)

            def largest(first, end):
                for g in range(first, end):
                    ins = dve.max(m8[:, g, :], corr[:, g, :])
                return ins

            def batch(b, last):
                if not last:
                    dve.wait_ge(spectrum, 4 * (b + 1))
                    folding(b + 1)
                else:
                    dve.wait_ge(v_in, 80)
                    for c in range(KT):
                        dve.wait_ge(v_copied, c + 1)
                        dve.tensor_tensor(
                            vblk[:, c, :, :].rearrange("p b (h i) -> p b h i", h=8),
                            vT[:, c, :].rearrange("p (b i) -> p b i", b=B).unsqueeze(2).broadcast_to([P, B, 8, DK]),
                            head_mask[:, :].unsqueeze(1).unsqueeze(3).broadcast_to([P, B, 8, DK]), ALU.mult).then_inc(vblk_done, 1)
                dve.wait_ge(qk_copied, 8 * (b + 1))
                ch = Chain(dve, cross_steps, 4 * b)
                qr, kr, qi, ki = qk[:, 0:4, 0:D], qk[:, 0:4, D:2 * D], qk[:, 4:8, 0:D], qk[:, 4:8, D:2 * D]
                dve.tensor_tensor(cross[:, 4:8, :], qi, kr, ALU.mult)
                ch.link(dve.tensor_tensor(prod[:, :, :], qr, ki, ALU.mult))
                ch.link(dve.tensor_tensor(cross[:, 4:8, :], cross[:, 4:8, :], prod[:, :, :], ALU.subtract))
                dve.tensor_tensor(cross[:, 0:4, :], qr, kr, ALU.mult)
                ch.link(dve.tensor_tensor(prod[:, :, :], qi, ki, ALU.mult))
                ch.link(dve.tensor_tensor(cross[:, 0:4, :], cross[:, 0:4, :], prod[:, :, :], ALU.add))
                dve.tensor_copy(cross[0:1, 7, :], prod[0:1, 3, :])
                dve.tensor_tensor(cross[0:1, 3, :], qk[0:1, 3, 0:D], qk[0:1, 3, D:2 * D],
                                  ALU.mult).then_inc(cross_done, 1)
                if last:
                    dve.wait_ge(corr_done, 2 + G - KT)
                    largest(0, G - KT)
                ch = Chain(dve, corr_steps, 2 * KT * b)
                for c in range(KT):
                    dve.wait_ge(inv_done, KT * b + c + 1)
                    ch.link(dve.tensor_copy(prod[:, c, :], ps[5 + 2 * c][:, 256:512]))
                    dve.tensor_tensor(uv[:, c, 0, :], ps[5 + 2 * c][:, 0:256], prod[:, c, :], ALU.add)
                    ch.link(dve.tensor_tensor(uv[:, c, 1, :], prod[:, c, :], ps[5 + 2 * c][:, 0:256], ALU.subtract))
                    odd = ps[4 + 2 * c][:, :].rearrange("p (r n) -> p r n", r=2)
                    row = corr[:, ds(b * KT + c, 1), :].rearrange("p o (a r n) -> p (o a) r n", a=2, r=2)
                    dve.tensor_tensor(row[:, 0], uv[:, c, :, :], odd, ALU.add)
                    dve.tensor_tensor(row[:, 1], uv[:, c, :, :], odd, ALU.subtract).then_inc(corr_done, 1)

            dve.wait_ge(x_in[0], 16)
            folding(0)
            for b in range(1, B):
                dve.wait_ge(x_in[b], 16)
            with dve.Fori(0, B - 1) as b:
                batch(b, False)
            batch(B - 1, True)
            ch = Chain(dve, dve_steps)
            dve.wait_ge(corr_done, 2 + G)
            ch.link(largest(G - KT, G))
            ch.link(dve.tensor_tensor(d8[:, :, :], m8[:, :, :], m8[:, :, 0:1].broadcast_to([P, G, TOP]), ALU.subtract))
            dve.sem_inc(diffs, 1)
            ch.link(dve.tensor_reduce(tail[:, 0:1], d8[:, :, TOP - 1], AX.X, ALU.max))
            dve.tensor_scalar(tail[:, 1:2], tail[:, 0:1], EXP_ZERO, None, ALU.is_ge).then_inc(tail_local, 1)
            dve.wait_ge(tail_counted, 1)
            dve.tensor_copy(tail_flag[:, :], ps[7][0:1, 0:1]).then_inc(flag_set, 1)
            dve.wait_ge(exps, 1)
            ch.link(dve.tensor_reduce(wsum[:, :], e8[:, :, :], AX.X, ALU.add))
            ch.link(dve.reciprocal(wrec[:, :], wsum[:, :]))
            dve.wait_ge(zeroed, 2)
            ch.link(dve.tensor_tensor(w_sort[:, :, 0:TOP], e8[:, :, :],
                                      wrec[:, :].unsqueeze(2).broadcast_to([P, G, TOP]), ALU.mult))
            dve.wait_ge(flag_set, 1)
            dve.wait_ge(bo_added, B)
            general = dve.value_load(tail_flag[0:1, 0:1], min_val=0, max_val=P)
            with dve.If(general > 0):
                gs = Chain(dve, sort_steps)
                gs.link(dve.tensor_scalar(neg_m[:, :], m8[:, :, 0], -1.0, None, ALU.mult))
                STEPS = S // TOP
                for g in range(G):
                    with dve.Fori(0, STEPS) as i:
                        st = Chain(dve, sort_steps, 1 + g * STEPS * 2 + i * 2)
                        st.link(dve.max(cur8[:, :], corr[:, g, :]))
                        dve.tensor_copy(w_sort[:, g, ds(i * TOP, TOP)], cur8[:, :])
                        st.link(dve.match_replace(corr[:, g, :], cur8[:, :], corr[:, g, :], LOWEST))
                    dve.sem_inc(sorted_done, 1)
                for g in range(G):
                    dve.wait_ge(gen_exps, g + 1)
                    gs2 = Chain(dve, sort_steps, 1 + G * STEPS * 2 + g)
                    gs2.link(dve.reciprocal(wrec[:, g:g + 1], wsum[:, g:g + 1]))
                    dve.tensor_scalar(w_sort[:, g, :], w_sort[:, g, :], wrec[:, g:g + 1], None,
                                      ALU.mult).then_inc(gen_weights, 1)
                for b in range(B):
                    for i in range(1, TPB):
                        n = b * (TPB - 1) + i - 1
                        dve.wait_ge(gen_y, n + 1)
                        dve.tensor_tensor(X[:, b * TPB + i, :], X[:, b * TPB + i, :], ps[n % 4][:, 0:D],
                                          ALU.add).then_inc(gen_added, 1)
                dve.wait_ge(gen_added, B * (TPB - 1))
                dve.nop()
            dve.sem_inc(weights, 1)
            for b in range(B):
                dve.wait_ge(y_done, b + 1)
                dve.tensor_tensor(X[:, b * TPB, :], X[:, b * TPB, :], ps[4 + b][:, 0:D], ALU.add)

    with nc.Block() as block:
        @block.gpsimd
        def _(pool):
            for signal in (sort_steps, sorted_done, gen_exps, gen_weights, gen_y, gen_added):
                pool.sem_clear(signal)



def alone(eng, spare):
    eng.sem_inc(spare, 1)


def layer_stats(dve, ch, tiles, stats, mv, spare, count=TPB):
    row_stats(dve, ch, tiles, stats, spare, count)
    moments(dve, ch, stats, mv, spare, count)


def row_stats(dve, ch, tiles, stats, spare, count):
    alone(dve, spare)
    for n in range(count):
        last = dve.bn_stats(stats[:, n, :], tiles[:, n, :])
    ch.link(last)


def moments(dve, ch, stats, mv, spare, count):
    alone(dve, spare)
    for n in range(count):
        last = dve.bn_aggr(mv[:, n, :], stats[:, n, :])
    ch.link(last)
    ch.link(dve.tensor_scalar(mv[:, :, 1], mv[:, :, 1], EPS, None, ALU.add))


def cross_attention(nc, ctx, t, dram):
    def sb(name, shape, dt=F32):
        return ctx.enter_context(nc.sbuf_tensor("sb_b_" + name, shape, dt))

    def sem(name):
        return ctx.enter_context(nc.semaphore("b_" + name))

    X, ps, pz, ident, neg_half = t["X"], t["ps"], t["pz"], t["ident"], t["neg_half"]
    C = dram["ctxT"].shape[1] // B
    HP = H // 2
    w_q = sb("w_q", [P, KT, D])
    w_kv = sb("w_kv", [P, KT, 2 * D])
    w_o = sb("w_o", [P, KT, D])
    bias_q = sb("bias_q", [P, KT])
    bias_k = sb("bias_k", [P, KT])
    bias_v = sb("bias_v", [1, D])
    bias_o = sb("bias_o", [P, D])
    mask = sb("mask", [P, TOP])
    ctxT = sb("ctxT", [P, KT, B * C])
    ctxT2 = sb("ctxT2", [P, KT, B, 2, C])
    ones_row = sb("ones_row", [1, P])
    kT = sb("kT", [P, KT, B * C])
    kblk = sb("kblk", [P, KT, B, 8 * C])
    vblk = sb("vblk", [P, B, HP, 2, DK])
    v_cur = sb("v_cur", [P, HP, 2 * DK])
    ones_pair = sb("ones_pair", [P, 2 * DK])
    GT = 4
    NG = NT // GT
    assert TPB == 2 * GT
    stats = sb("stats", [P, GT, 6])
    mv = sb("mv", [P, GT, 2])
    rstd = sb("rstd", [P, GT])
    xs = sb("xs", [P, GT, D])
    xT = sb("xT", [P, KT, GT * P])
    qT = sb("qT", [P, KT, 2, GT * P])
    mx = sb("mx", [P, 2, H])
    pr = sb("pr", [P, 2, H, C])
    prT = sb("prT", [P, 2, HP, P])
    rec = sb("rec", [P, D])
    yT = sb("yT", [P, 2, KT, P])

    w_in, k_in = sem("w_in"), sem("k_in")
    zeroed, k_done, k_copied, v_done = sem("zeroed"), sem("k_done"), sem("k_copied"), sem("v_done")
    kblk_done, vblk_done = sem("kblk_done"), sem("vblk_done")
    dve_steps = sem("dve_steps")
    spare = t["spare"]
    var_done, rstd_done, x_done, xs_done, bo_added, piece_done, piece_copied = (sem(n) for n in (
        "var_done", "rstd_done", "x_done", "xs_done", "bo_added", "piece_done", "piece_copied"))
    max_done, rec_done = sem("max_done"), sem("rec_done")
    scores, shifted, probs, probsT, probsT_copied, v_cur_done, pv, yT_done, out_done, res_done = (
        sem(n) for n in ("scores", "shifted", "probs", "probsT", "probsT_copied", "v_cur_done", "pv", "yT_done",
                         "out_done", "res_done"))
    AHEAD = 6

    def need(eng, signal, value):
        if not isinstance(value, int) or value > 0:
            eng.wait_ge(signal, value)

    def over_slots(eng, slot):
        for r in range(TPB):
            slot(0, r)
        with eng.Fori(1, B - 1) as b:
            for r in range(TPB):
                slot(b, r)
        for r in range(TPB):
            slot(B - 1, r)
        for r in range(3):
            slot(B, r)

    def tile(b, r, lag):
        n = b * TPB + r - lag
        return n if not isinstance(n, int) or 0 <= n < NT else None

    def piece(b, r):
        kind = r % GT // 2
        g = b * 2 + r // GT + 1 + kind
        if isinstance(g, int) and g >= NG:
            return None
        return AHEAD + b * TPB + r, kind, g, (r // GT + 1 + kind) % 2, r % 2

    first_pieces = [(0, 1, 0, 0, 0), (1, 1, 0, 0, 1), (2, 0, 0, 0, 0), (3, 0, 0, 0, 1), (4, 1, 1, 1, 0), (5, 1, 1, 1, 1)]

    k_loads = [
        (w_kv[:, :, :], dram["WkvT"].rearrange("(k p) n -> p k n", p=P)),
        (ctxT[:, :, :], dram["ctxT"].rearrange("(k p) n -> p k n", p=P)),
        (bias_k[:, :], dram["bk_cross"]),
        (mask[:, :], dram["head_mask"]),
    ]
    loads = [(bias_v[:, :], dram["bv_cross"])] + [(ctxT2[:, k, :, r, :], dram["ctxT"][k * P:(k + 1) * P].rearrange("p (b c) -> p b c", b=B))
         for k in range(KT) for r in range(2)] + [
        (w_q[:, :, :], dram["WqT"].rearrange("(k p) n -> p k n", p=P)),
        (bias_q[:, :], dram["bq_cross"]),
        (w_o[:, :, :], dram["WoT"].rearrange("(k p) n -> p k n", p=P)),
        (bias_o[:, :], dram["bo_cross"].partition_broadcast(P)),
    ]

    next_loads = [(t["w_qkv"][:, :, :], dram["w_qkv"].rearrange("(k p) n -> p k n", p=P)),
                  (t["ln1_w"][:, :], dram["ln1_w"]), (t["ln1_b"][:, :], dram["ln1_b"])]

    with nc.Block() as block:
        @block.sync
        def _(sp):
            for dst, src in k_loads:
                sp.dma_start(dst, src).then_inc(k_in, 16)
            for dst, src in loads:
                sp.dma_start(dst, src).then_inc(w_in, 16)
            for dst, src in next_loads:
                sp.dma_start(dst, src).then_inc(t["qkv_in"], 16)

        @block.gpsimd
        def _(pool):
            pool.memset(ones_row[:, :], 1.0).then_inc(zeroed, 1)
            pool.memset(vblk[:, :, :, :, :], 0.0).then_inc(zeroed, 1)
            pool.memset(ones_pair[:, :], 0.0).then_inc(zeroed, 1)
            pool.wait_ge(zeroed, 3)
            pool.memset(ones_pair[0:C, 0:DK], 1.0).then_inc(zeroed, 1)
            pool.memset(ones_pair[C:2 * C, DK:2 * DK], 1.0).then_inc(zeroed, 1)
            pool.wait_ge(zeroed, 5)

            def norm(g):
                need(pool, var_done, g + 1)
                pool.tensor_tensor(rstd[:, :], mv[:, :, 1], neg_half[:, 0:GT], ALU.pow).then_inc(rstd_done, 1)
                pool.wait_ge(xs_done, g + 1)
                pool.tensor_tensor(X[:, ds(g * GT, GT), :], xs[:, :, :],
                                   bias_o[:, :].unsqueeze(1).broadcast_to([P, GT, D]), ALU.add).then_inc(bo_added, 1)

            pool.wait_ge(w_in, 16 * len(loads))
            for g in range(4):
                norm(g)
            with pool.Fori(2, NG // 2) as h:
                norm(2 * h)
                norm(2 * h + 1)
            for c in range(4):
                pool.wait_ge(var_done, NG + c + 1)
                pool.tensor_tensor(rstd[:, :], mv[:, :, 1], neg_half[:, 0:GT], ALU.pow).then_inc(rstd_done, 1)

        @block.tensor
        def _(pe):
            pe.wait_ge(k_in, 16 * len(k_loads))
            for c in range(KT):
                for k in range(KT):
                    mm = pe.matmul(ps[c][:, 0:B * C], w_kv[:, k, c * P:(c + 1) * P], ctxT[:, k, :],
                                   start=(k == 0), stop=(k == KT - 1))
                mm.then_inc(k_done, 1)
            pe.wait_ge(zeroed, 5)
            pe.wait_ge(w_in, 16 * len(loads))
            for b in range(B):
                for k in range(KT):
                    pe.matmul(ps[4 + b][:, 0:D], ctxT2[:, k, b, :, :].rearrange("p r c -> p (r c)"),
                              w_kv[:, k, D:2 * D], start=(k == 0), stop=False)
                pe.matmul(ps[4 + b][:, 0:D], ones_row[:, :], bias_v[:, :], start=False, stop=True).then_inc(v_done, 1)
            pe.wait_ge(k_copied, KT)
            pe.wait_ge(vblk_done, 2 * B)

            def make(number, kind, g, parity, part):
                need(pe, piece_copied, number)
                if kind == 1:
                    pe.wait_ge(xs_done, g + 1)
                    for k in range(KT):
                        for n in range(2):
                            mm = pe.transpose(ps[4][:, (2 * k + n) * P:(2 * k + n + 1) * P],
                                              xs[:, 2 * part + n, k * P:(k + 1) * P], ident[:, :])
                else:
                    for k in range(KT):
                        mm = pe.matmul(ps[4][:, :], w_q[:, k, part * P:(part + 1) * P], xT[:, k, :],
                                       start=(k == 0), stop=(k == KT - 1))
                mm.then_inc(piece_done, 1)

            def slot(b, r):
                n, u, v = tile(b, r, 0), tile(b, r, 2), tile(b, r, 3)
                if u is not None:
                    pe.wait_ge(probs, u + 1)
                    need(pe, probsT_copied, u)
                    pe.wait_ge(piece_copied, AHEAD + u + 2 if not isinstance(u, int) else min(AHEAD + u + 2, 4 * NG))
                    for j in range(HP):
                        tr = pe.transpose(ps[4 + j // 4][:, j % 4 * P:(j % 4 + 1) * P],
                                          pr[:, r % 2, 2 * j:2 * j + 2, :].rearrange("p h c -> p (h c)"), ident[:, :])
                    tr.then_inc(probsT, 1)
                if n is not None:
                    if r % GT == 0:
                        pe.wait_ge(piece_copied, n + 4)
                    need(pe, shifted, n - 1)
                    for c in range(KT):
                        mm = pe.matmul(ps[2 * (r % 2) + c][:, :], qT[:, c, r // GT, r % GT * P:(r % GT + 1) * P],
                                       kblk[:, c, ds(b, 1), :].rearrange("p o n -> p (o n)"), start=True, stop=True)
                    mm.then_inc(scores, 1)
                    if piece(b, r):
                        if u is not None:
                            pe.wait_ge(probsT_copied, u + 1)
                        make(*piece(b, r))
                if v is not None:
                    pe.wait_ge(yT_done, v + 1)
                    need(pe, res_done, v)
                    for k in range(KT):
                        mm = pe.matmul(ps[7][:, 0:D], yT[:, (r - 3) % 2, k, :], w_o[:, k, :],
                                       start=(k == 0), stop=(k == KT - 1))
                    mm.then_inc(out_done, 1)
                if u is not None:
                    pe.wait_ge(probsT_copied, u + 1)
                    need(pe, yT_done, u)
                    if r == 2:
                        pe.wait_ge(v_cur_done, b + 1)
                    for half in range(2):
                        for j in range(HP):
                            at = 2 * DK * (j % 4)
                            mm = pe.matmul(ps[6][at:at + 2 * DK, half * D + j // 4 * P:half * D + (j // 4 + 1) * P],
                                           (v_cur[:, j, :], ones_pair[:, :])[half], prT[:, r % 2, j, :],
                                           start=True, stop=True, skip_group_check=True)
                    mm.then_inc(pv, 1)

            for p in first_pieces:
                make(*p)
            pe.wait_ge(kblk_done, KT)
            over_slots(pe, slot)

        @block.scalar
        def _(act):
            act.wait_ge(k_in, 16 * len(k_loads))
            for c in range(KT):
                act.wait_ge(k_done, c + 1)
                act.activation(kT[:, c, :], ps[c][:, 0:B * C], ACT.Identity, bias=bias_k[:, c:c + 1]).then_inc(k_copied, 1)
            act.wait_ge(zeroed, 5)
            for b in range(B):
                act.wait_ge(v_done, b + 1)
                for r in range(2):
                    act.activation(vblk[r * C:(r + 1) * C, b, :, r, 0:DK],
                                   ps[4 + b][r * C:(r + 1) * C, 0:D].rearrange("p (j q d) -> p j q d", q=2, d=DK)[:, :, r, :],
                                   ACT.Identity).then_inc(vblk_done, 1)

            def take(number, kind, g, parity, part):
                act.wait_ge(piece_done, number + 1)
                if kind == 1:
                    act.activation(xT[:, :, part * 2 * P:(part + 1) * 2 * P], ps[4][:, :].rearrange("p (k n) -> p k n", k=KT),
                                   ACT.Identity).then_inc(piece_copied, 1)
                else:
                    act.activation(qT[:, part, parity, :], ps[4][:, :], ACT.Identity,
                                   bias=bias_q[:, part:part + 1]).then_inc(piece_copied, 1)

            def slot(b, r):
                n, u = tile(b, r, 0), tile(b, r, 2)
                if n is not None and r == 2:
                    need(act, pv, b * TPB)
                    act.activation(v_cur[:, :, :], vblk[:, ds(b, 1), :, :, :].rearrange("p o j r c -> p (o j) (r c)"),
                                   ACT.Identity).then_inc(v_cur_done, 1)
                if u is not None:
                    act.wait_ge(probsT, u + 1)
                    need(act, pv, u - 1)
                    act.activation(prT[:, r % 2, :, :], pz[:, 4:6, :].rearrange("p q (j n) -> p (q j) n", j=4),
                                   ACT.Identity).then_inc(probsT_copied, 1)
                if n is not None:
                    if piece(b, r):
                        take(*piece(b, r))
                    act.wait_ge(shifted, n + 1)
                    act.activation(pr[:, r % 2, :, :], pr[:, r % 2, :, :], ACT.Exp,
                                   scale=float(DK) ** -0.5).then_inc(probs, 1)

            act.wait_ge(w_in, 16 * len(loads))
            act.wait_ge(vblk_done, 2 * B)
            for p in first_pieces:
                take(*p)
            over_slots(act, slot)

        @block.vector
        def _(dve):
            def group_stats(g):
                need(dve, xs_done, g)
                layer_stats(dve, Chain(dve, dve_steps, 3 * g), X[:, ds(g * GT, GT), :], stats, mv, spare, GT)
                dve.sem_inc(var_done, 1)

            def norm(g):
                tiles = X[:, ds(g * GT, GT), :]
                need(dve, bo_added, g)
                need(dve, piece_done, 4 * g - 2 if not isinstance(g, int) or g > 1 else 2 * g)
                dve.wait_ge(rstd_done, g + 1)
                for n in range(GT):
                    tp = dve.tensor_scalar(xs[:, n, :], tiles[:, n, :], mv[:, n, 0:1], rstd[:, n:n + 1],
                                           ALU.subtract, ALU.mult)
                tp.then_inc(xs_done, 1)

            def slot(b, r):
                n, u, v = tile(b, r, 0), tile(b, r, 2), tile(b, r, 3)
                if n is not None:
                    dve.wait_ge(scores, n + 1)
                    sc = pz[:, 2 * (r % 2):2 * (r % 2) + 2, :].rearrange("p q (h n) -> p (q h) n", h=8)
                    dve.tensor_reduce(mx[:, r % 2, :], sc, AX.X, ALU.max).then_inc(max_done, 1)
                    dve.wait_ge(max_done, n + 1)
                    dve.tensor_tensor(pr[:, r % 2, :, :], sc,
                                      mx[:, r % 2, :].unsqueeze(2).broadcast_to([P, H, C]), ALU.subtract).then_inc(shifted, 1)
                g = b * 2 + r // GT + 2
                if r % GT < 2 and (not isinstance(b, int) or g < NG):
                    (group_stats, norm)[r % GT](g)
                if v is not None:
                    dve.wait_ge(out_done, v + 1)
                    if (r - 3) % GT == 0:
                        dve.wait_ge(bo_added, b * 2 + 1 + (r - 3) // GT)
                    row = X[:, ds(v, 1), :].rearrange("p o d -> p (o d)")
                    dve.tensor_tensor(row, row, ps[7][:, 0:D], ALU.add).then_inc(res_done, 1)
                if u is not None:
                    dve.wait_ge(pv, u + 1)
                    dve.reciprocal(rec[:, :], ps[6][:, D:2 * D]).then_inc(rec_done, 1)
                    dve.wait_ge(rec_done, u + 1)
                    need(dve, out_done, u - 1)
                    dve.tensor_tensor(yT[:, r % 2, :, :], ps[6][:, 0:D].rearrange("p (k n) -> p k n", k=KT),
                                      rec[:, :].rearrange("p (k n) -> p k n", k=KT), ALU.mult).then_inc(yT_done, 1)
                if isinstance(b, int) and b == B - 1:
                    (close_stats, close)[r % 2](r // 2)

            def close_stats(c):
                part = c % 2
                dve.wait_ge(res_done, TPB)
                dve.wait_ge(xs_done, NG)
                need(dve, x_done, c)
                layer_stats(dve, Chain(dve, dve_steps, 3 * (NG + c)), X[:, part * GT:(part + 1) * GT, :], stats, mv, spare, GT)
                dve.sem_inc(var_done, 1)

            def close(c):
                part, own = c % 2, c // 2
                tiles = X[:, part * GT:(part + 1) * GT, :]
                dve.wait_ge(rstd_done, NG + c + 1)
                for n in range(GT):
                    tp = dve.tensor_scalar((tiles, t["xs_c"][:, part * GT:(part + 1) * GT, :])[own][:, n, :], tiles[:, n, :],
                                           mv[:, n, 0:1], rstd[:, n:n + 1], ALU.subtract, ALU.mult)
                tp.then_inc(x_done, 1)

            group_stats(0)
            norm(0)
            dve.wait_ge(k_in, 16 * len(k_loads))
            for c in range(KT):
                dve.wait_ge(k_copied, c + 1)
                dve.tensor_tensor(
                    kblk[:, c, :, :].rearrange("p b (h n) -> p b h n", h=8),
                    kT[:, c, :].rearrange("p (b n) -> p b n", b=B).unsqueeze(2).broadcast_to([P, B, 8, C]),
                    mask[:, :].unsqueeze(1).unsqueeze(3).broadcast_to([P, B, 8, C]), ALU.mult).then_inc(kblk_done, 1)
            group_stats(1)
            norm(1)
            over_slots(dve, slot)


def project_qkv(nc, ctx, t, dram):
    def sb(name, shape, dt=F32):
        return ctx.enter_context(nc.sbuf_tensor("sb_c_" + name, shape, dt))

    def sem(name):
        return ctx.enter_context(nc.semaphore("c_" + name))

    X, ps, pz, ident, neg_half, v_all = t["X"], t["ps"], t["pz"], t["ident"], t["neg_half"], t["v_all"]
    w, ln_w, ln_b, xs, w_in = t["w_qkv"], t["ln1_w"], t["ln1_b"], t["xs_c"], t["qkv_in"]
    stats = sb("stats", [P, TPB, 6])
    mv = sb("mv", [P, TPB, 2])
    rstd = sb("rstd", [P, TPB])
    xT = sb("xT", [P, KT, S])
    parts = sb("parts", [P, 2, 3, S], BF16)
    rest = sb("rest", [P, 2, S])
    dve_steps = sem("dve_steps")
    spare = t["spare"]
    var_done, rstd_done, xs_done, xT_done, xT_copied = (sem(n) for n in (
        "var_done", "rstd_done", "xs_done", "xT_done", "xT_copied"))
    qk_done, high_done, rest_done, mid_done, low_done = (sem(n) for n in (
        "qk_done", "high_done", "rest_done", "mid_done", "low_done"))
    stored = [sem("stored0"), sem("stored1")]
    v_done, v_copied = sem("v_done"), sem("v_copied")
    U = 2 * KT

    with nc.Block() as block:
        @block.sync
        def _(sp):
            for q in stored:
                sp.sem_inc(q, 16)
            with sp.Fori(0, B) as b:
                for u in range(U):
                    dst = (dram["q_parts"], dram["k_parts"])[u // KT]
                    sp.wait_ge(low_done, 2 + U * b + u + 1)
                    alone(sp, spare)
                    sp.wait_ge(high_done, U * b + u + 1)
                    sp.wait_ge(mid_done, U * b + u + 1)
                    for i in range(3):
                        sp.dma_start(dst[i, ds(b * D + (u % KT) * P, P), :], parts[:, u % 2, i, :]).then_inc(stored[u % 2], 16)
            for q in stored:
                sp.wait_ge(q, 16 + 3 * 16 * B * U // 2)

        @block.gpsimd
        def _(pool):
            pool.sem_inc(low_done, 2)

            def scale(b, r):
                pool.wait_ge(var_done, 2 * b + r + 1)
                pool.tensor_tensor(rstd[:, :], mv[:, :, 1], neg_half[:, :], ALU.pow).then_inc(rstd_done, 1)

            def units(b, last):
                if not last:
                    scale(b, 0)
                for u in range(U):
                    pool.wait_ge(mid_done, U * b + u + 1)
                    pool.tensor_tensor(parts[:, u % 2, 2, :], rest[:, u % 2, :], parts[:, u % 2, 1, :],
                                       ALU.subtract).then_inc(low_done, 1)
                    if u == 0 and not last:
                        scale(b, 1)

            with pool.Fori(0, B - 1) as b:
                units(b, False)
            units(B - 1, True)

        @block.tensor
        def _(pe):
            pe.wait_ge(w_in, 48)
            with pe.Fori(0, B) as b:
                pe.wait_ge(xs_done, 2 * b + 1)
                for n in range(TPB):
                    for k in range(KT):
                        tr = pe.transpose(ps[2 * (n // 4) + k][:, n % 4 * P:(n % 4 + 1) * P],
                                          xs[:, n, k * P:(k + 1) * P], ident[:, :])
                    if n % 4 == 3:
                        tr.then_inc(xT_done, 1)
                for u in range(U):
                    if u < 2:
                        pe.wait_ge(v_copied, 2 * b + u + 1)
                    else:
                        pe.wait_ge(rest_done, U * b + u - 1)
                    for h in range(2):
                        if u == 0:
                            pe.wait_ge(xT_copied, 4 * b + 2 * h + 2)
                        for k in range(KT):
                            mm = pe.matmul(ps[4 + 2 * (u % 2) + h][:, :], w[:, k, u * P:(u + 1) * P],
                                           xT[:, k, h * 512:(h + 1) * 512], start=(k == 0), stop=(k == KT - 1))
                    mm.then_inc(qk_done, 1)
                for u in range(2):
                    pe.wait_ge(rest_done, U * b + U - 1 + u)
                    for i in range(4 * u, 4 * u + 4):
                        for k in range(KT):
                            mm = pe.matmul(ps[4 + i // 2][:, i % 2 * D:(i % 2 + 1) * D], xT[:, k, i * P:(i + 1) * P],
                                           w[:, k, 2 * D:3 * D], start=(k == 0), stop=(k == KT - 1))
                    mm.then_inc(v_done, 1)

        @block.scalar
        def _(act):
            act.sem_inc(v_copied, 2)
            act.wait_ge(w_in, 48)
            def middle(b, u):
                act.wait_ge(rest_done, U * b + u + 1)
                act.activation(parts[:, u % 2, 1, :], rest[:, u % 2, :], ACT.Identity).then_inc(mid_done, 1)

            with act.Fori(0, B) as b:
                for h in range(2):
                    act.wait_ge(xT_done, 2 * b + h + 1)
                    for k in range(KT):
                        act.activation(xT[:, k, h * 512:(h + 1) * 512], ps[2 * h + k][:, :], ACT.Identity,
                                       bias=ln_b[:, k:k + 1], scale=ln_w[:, k:k + 1]).then_inc(xT_copied, 1)
                for u in range(U):
                    if u >= 1:
                        middle(b, u - 1)
                    act.wait_ge(qk_done, U * b + u + 1)
                    act.wait_ge(stored[u % 2], 16 + 48 * (U // 2 * b + u // 2))
                    act.activation(parts[:, u % 2, 0, :], pz[:, 4 + 2 * (u % 2):6 + 2 * (u % 2), :].rearrange("p q n -> p (q n)"),
                                   ACT.Identity, scale=float(DK) ** -0.5 if u < KT else 1.0).then_inc(high_done, 1)
                middle(b, U - 1)
                for u in range(2):
                    act.wait_ge(v_done, 2 * b + u + 1)
                    act.activation(v_all[:, ds(b * H, H), 4 * u:4 * u + 4, :],
                                   pz[:, 4 + 2 * u:6 + 2 * u, :].rearrange("p q (r h d) -> p h (q r) d", r=2, h=H),
                                   ACT.Identity).then_inc(v_copied, 1)

        @block.vector
        def _(dve):
            dve.sem_inc(xs_done, 1)
            def first_half(b, r):
                row_stats(dve, Chain(dve, dve_steps, 6 * b + 3 * r), X[:, ds((b + 1) * TPB, TPB), :], stats, spare, TPB)

            def second_half(b, r):
                moments(dve, Chain(dve, dve_steps, 6 * b + 3 * r + 1), stats, mv, spare, TPB)
                dve.sem_inc(var_done, 1)

            def norm(b, r):
                tiles = X[:, ds((b + 1) * TPB, TPB), :]
                dve.wait_ge(rstd_done, 2 * b + r + 1)
                for n in range(TPB):
                    tp = dve.tensor_scalar((tiles, xs)[r][:, n, :], tiles[:, n, :], mv[:, n, 0:1], rstd[:, n:n + 1],
                                           ALU.subtract, ALU.mult)
                tp.then_inc(xs_done, 1)
                dve.wait_ge(xs_done, 1 + 2 * b + r + 1)

            def units(b, last):
                if not last:
                    first_half(b, 0)
                    second_half(b, 0)
                    norm(b, 0)
                for u in range(U):
                    dve.wait_ge(high_done, U * b + u + 1)
                    dve.wait_ge(low_done, 2 + U * b + u - 1)
                    dve.scalar_tensor_tensor(out=rest[:, u % 2, :],
                                             in0=pz[:, 4 + 2 * (u % 2):6 + 2 * (u % 2), :].rearrange("p q n -> p (q n)"),
                                             scalar=float(DK) ** -0.5 if u < KT else 1.0, in1=parts[:, u % 2, 0, :],
                                             op0=ALU.mult, op1=ALU.subtract).then_inc(rest_done, 1)
                    if not last and u < 3:
                        (first_half, second_half, norm)[u](b, 1)

            with dve.Fori(0, B - 1) as b:
                units(b, False)
            units(B - 1, True)


def self_attention(nc, ctx, t, dram):
    def sb(name, shape, dt=F32):
        return ctx.enter_context(nc.sbuf_tensor("sb_m_" + name, shape, dt))

    def sem(name):
        return ctx.enter_context(nc.semaphore("m_" + name))

    ps, ident, v_all, y_all = t["ps"], t["ident"], t["v_all"], t["y_all"]
    HEADS = B * H
    R = 6 * DK
    NB = 4
    q_s = sb("q", [R + 3, NB, S], BF16)
    k_s = sb("k", [R + 3, NB, S], BF16)
    v_s = sb("v", [P, 2, TPB, 32])
    pT = sb("pT", [P, 4, S])
    mx2 = sb("mx2", [P, 2, TPB, 2])
    neg_mx = sb("neg_mx", [P, 2, TPB])
    mxT = sb("mxT", [TPB, P])
    mx_rest = sb("mx_rest", [TPB, P])
    mx_parts = sb("mx_parts", [TPB, 2, 3, P], BF16)
    y_raw = sb("y_raw", [P, 256])
    rec = sb("rec", [P, 8])

    q_in = [sem(f"qk_in{i}") for i in range(NB)]
    max_in = [sem(f"max_in{i}") for i in range(NB)]
    set_up, v_in, scores1, maxed, neg_done, mxT_done, mxT_read, split_done = (sem(n) for n in (
        "set_up", "v_in", "scores1", "maxed", "neg_done", "mxT_done", "mxT_read", "split_done"))
    y_rec, spare = sem("y_rec"), t["spare"]
    scores2, exped, pv, y_copied, yT_done, y_stored, pool_steps = (sem(n) for n in (
        "scores2", "exped", "pv", "y_copied", "yT_done", "y_stored", "pool_steps"))
    LINKS1 = 3

    def slots(eng, body):
        for s in range(NB):
            body(s, s, s // NB, 0)
        with eng.Fori(1, HEADS // NB) as it:
            for q in range(NB):
                body(it * NB + q, q, it, None)
        for s in range(HEADS, HEADS + 3):
            body(s, s % NB, s // NB, HEADS)

    def has(s, lag, edge):
        return edge is None or 0 <= s - lag < HEADS

    def turn(par, it, lag):
        return (par - lag) % NB, it + 1 - (1 if par < lag else 0)

    with nc.Block() as block:
        @block.sync
        def _(sp):
            def load(g, i):
                for dst, src, rows in ((q_s, "q_parts", ((0, 3), (0, 2), (0, 1))), (k_s, "k_parts", (0, 1, 2))):
                    at = 0
                    for n, r in zip((3, 2, 1), rows):
                        for j in range(n):
                            part = (r[0] + j) if src == "q_parts" else r
                            sp.dma_start(dst[at:at + DK, i, :], dram[src][part, ds(g * DK, DK), :]).then_inc(q_in[i], 16)
                            at += DK

            load(0, 0)

            def slot(s, par, it, edge):
                if has(s, -1, edge):
                    if not (edge == 0 and s + 1 < NB):
                        sp.wait_ge(scores2, 2 * TPB * (s + 2 - NB))
                    load(s + 1, (par + 1) % NB)
                if has(s, 1, edge):
                    i, _ = turn(par, it, 1)
                    sp.wait_ge(split_done, s)
                    for r in range(3):
                        sp.dma_start(q_s[R + r:R + r + 1, i, :].rearrange("o (t n) -> o t n", t=TPB),
                                     mx_parts[:, (par - 1) % 2, r, :]).then_inc(max_in[i], 16)

            for s in range(NB):
                slot(s, s, 0, 0)
            with sp.Fori(1, HEADS // NB - 1) as it:
                for q in range(NB):
                    slot(it * NB + q, q, it, None)
            for s in range(HEADS - NB, HEADS + 3):
                slot(s, s % NB, s // NB, HEADS)

        @block.gpsimd
        def _(pool):
            pool.memset(v_s[:, :, :, DK + 1:32], 0.0).then_inc(set_up, 1)
            pool.memset(v_s[:, :, :, DK:DK + 1], 1.0).then_inc(set_up, 1)
            pool.wait_ge(set_up, 3)

            def slot(s, par, it, edge):
                if has(s, 2, edge):
                    if not (edge == 0 and s - 4 < 0):
                        pool.wait_ge(pv, TPB * (s - 3))
                    alone(pool, spare)
                    pool.tensor_copy(v_s[:, par % 2, :, 0:DK],
                                     v_all[:, ds(s - 2, 1), :, :].rearrange("p o n d -> p (o n) d")).then_inc(v_in, 1)

                if has(s, 1, edge):
                    c = Chain(pool, pool_steps, (s - 1) * LINKS1)
                    mp = mx_parts[:, (par - 1) % 2, :, :]
                    i, use = turn(par, it, 3)
                    if not (edge == 0 and s < 3):
                        pool.wait_ge(max_in[i], 48 * use)
                    pool.wait_ge(mxT_read, s)
                    alone(pool, spare)
                    c.link(pool.tensor_copy(mp[:, 0, :], mxT[:, :]))
                    c.link(pool.tensor_tensor(mx_rest[:, :], mxT[:, :], mp[:, 0, :], ALU.subtract))
                    alone(pool, spare)
                    c.link(pool.tensor_copy(mp[:, 1, :], mx_rest[:, :]))
                    pool.tensor_tensor(mp[:, 2, :], mx_rest[:, :], mp[:, 1, :], ALU.subtract).then_inc(split_done, 1)

            slots(pool, slot)

        @block.tensor
        def _(pe):
            pe.wait_ge(set_up, 3)

            def free_bank(read, g, par, j, edge):
                n = 2 * TPB * par + j
                if n == 0:
                    need = 2 * TPB * g
                elif n < 3:
                    need = 0
                else:
                    need = 2 * TPB * g + j - 2
                if not isinstance(need, int) or need > 0:
                    pe.wait_ge(read, need)
                return n % 3

            def sums(e, par2, m, edge_first):
                if m == 0 and not edge_first:
                    pe.wait_ge(y_copied, e)
                pe.wait_ge(exped, 2 * TPB * e + 2 * (m + 1))
                for j in range(4):
                    mm = pe.matmul(ps[6][32 * j:32 * j + 32, 0:256], v_s[:, par2, m, :],
                                   pT[:, m % 4, j * 256:(j + 1) * 256], start=(m == 0), stop=(m == TPB - 1),
                                   skip_group_check=True)
                mm.then_inc(pv, 1)

            def slot(s, par, it, edge):
                one, two, three = has(s, 0, edge), has(s, 2, edge), has(s, 3, edge)
                if one:
                    i, use = turn(par, it, 0)
                    pe.wait_ge(q_in[i], 12 * 16 * use)
                if two:
                    i2, use2 = turn(par, it, 2)
                for k in range(TPB):
                    if one:
                        for h in range(2):
                            j = 2 * k + h
                            bank = free_bank(maxed, s, par, j, edge)
                            pe.matmul(ps[bank][:, :], q_s[0:R, i, k * P:(k + 1) * P],
                                      k_s[0:R, i, h * 512:(h + 1) * 512], start=True, stop=True).then_inc(scores1, 1)
                    if two:
                        e = s - 2
                        if k == 0:
                            pe.wait_ge(max_in[i2], 48 * use2)
                            pe.wait_ge(v_in, e + 1)
                        for h in range(2):
                            j = 2 * k + h
                            bank = 3 + free_bank(exped, e, par, j, edge)
                            mm = pe.matmul(ps[bank][:, :], k_s[:, i2, k * P:(k + 1) * P],
                                           q_s[:, i2, h * 512:(h + 1) * 512], start=True, stop=True)
                            mm.then_inc(scores2, 1)
                    if k < 2:
                        if three:
                            sums(s - 3, (par - 3) % 2, TPB - 2 + k, False)
                    elif two:
                        sums(s - 2, par % 2, k - 2, edge == 0 and s == 2)
                    if k == 1 and has(s, 1, edge):
                        pe.wait_ge(neg_done, s)
                        if not (edge == 0 and s < 4):
                            pe.wait_ge(y_stored, s - 3)
                        pe.transpose(ps[7][0:TPB, 0:P], neg_mx[:, (par - 1) % 2, :], ident[:, :]).then_inc(mxT_done, 1)
                    if k == 4 and three:
                        pe.wait_ge(y_copied, s - 2)
                        if has(s, 1, edge):
                            pe.wait_ge(mxT_read, s)
                        else:
                            pe.wait_ge(y_stored, s - 3)
                        for r in range(2):
                            tr = pe.transpose(ps[7][:, r * P:(r + 1) * P], y_raw[:, r * P:(r + 1) * P], ident[:, :])
                        tr.then_inc(yT_done, 1)

            slots(pe, slot)

        @block.scalar
        def _(act):
            def slot(s, par, it, edge):
                two, three = has(s, 2, edge), has(s, 3, edge)
                for k in range(TPB):
                    if two:
                        e = s - 2
                        for h in range(2):
                            j = 2 * k + h
                            act.wait_ge(scores2, 2 * TPB * e + j + 1)
                            if h == 0 and not (edge == 0 and s == 2 and k < 4):
                                act.wait_ge(pv, TPB * e + k - 3)
                            act.activation(pT[:, k % 4, h * 512:(h + 1) * 512], ps[3 + (2 * TPB * par + j) % 3][:, :],
                                           ACT.Exp).then_inc(exped, 1)
                    if k == 2 and has(s, 1, edge):
                        act.wait_ge(mxT_done, s)
                        if not (edge == 0 and s < 2):
                            act.wait_ge(split_done, s - 1)
                        act.activation(mxT[:, :], ps[7][0:TPB, 0:P], ACT.Identity).then_inc(mxT_read, 1)
                    if k == 1 and three:
                        act.wait_ge(pv, TPB * (s - 2))
                        if not (edge == 0 and s == 3):
                            act.wait_ge(yT_done, s - 3)
                        act.activation(y_raw[:, :], ps[6][:, 0:256], ACT.Identity).then_inc(y_copied, 1)

            slots(act, slot)

        @block.vector
        def _(dve):
            dve.memset(k_s[R:R + 3, :, :], 1.0).then_inc(set_up, 1)

            def slot(s, par, it, edge):
                one, three = has(s, 0, edge), has(s, 3, edge)
                for j in range(2 * TPB):
                    if one:
                        dve.wait_ge(scores1, 2 * TPB * s + j + 1)
                        dve.tensor_reduce(mx2[:, par % 2, j // 2, j % 2:j % 2 + 1], ps[(2 * TPB * par + j) % 3][:, :],
                                          AX.X, ALU.max).then_inc(maxed, 1)
                    if j == 0 and has(s, 1, edge):
                        dve.wait_ge(maxed, 2 * TPB * s)
                        dve.tensor_reduce(neg_mx[:, (par - 1) % 2, :], mx2[:, (par - 1) % 2, :, :], AX.X, ALU.max,
                                          negate=True).then_inc(neg_done, 1)
                    yt = ps[7][:, 0:256].rearrange("p (r j d) -> p j r d", r=2, j=4)
                    if j == 10 and three:
                        dve.wait_ge(yT_done, s - 2)
                        dve.reciprocal(rec[:, :].rearrange("p (j r) -> p j r", j=4), yt[:, :, :, DK]).then_inc(y_rec, 1)
                    if j == 11 and three:
                        dve.wait_ge(y_rec, s - 2)
                        dve.tensor_tensor(
                            y_all[:, ds(s - 3, 1), :, :].rearrange("p o (j r) d -> p (o j) r d", j=4), yt[:, :, :, 0:DK],
                            rec[:, :].rearrange("p (j r) -> p j r", j=4).unsqueeze(3).broadcast_to([P, 4, 2, DK]),
                            ALU.mult).then_inc(y_stored, 1)

            slots(dve, slot)


def gate(nc, ctx, t, dram):
    def sb(name, shape, dt=F32):
        return ctx.enter_context(nc.sbuf_tensor("sb_g_" + name, shape, dt))

    def sem(name):
        return ctx.enter_context(nc.semaphore("g_" + name))

    X, ps, pz, ident, neg_half, y_all, logits = (t[n] for n in (
        "X", "ps", "pz", "ident", "neg_half", "y_all", "logits"))
    E = dram["gate_w"].shape[1]
    GT = 4
    NG = NT // GT
    assert TPB == 2 * GT
    w = sb("w", [P, KT, D])
    w_gate = sb("w_gate", [P, KT, E])
    b_gate = sb("b_gate", [P, E])
    ln_w = sb("ln_w", [P, KT])
    ln_b = sb("ln_b", [P, KT])
    stats = sb("stats", [P, GT, 6])
    mv = sb("mv", [P, GT, 2])
    rstd = sb("rstd", [P, GT])
    ys = sb("ys", [P, 2, GT, D])
    yT = sb("yT", [P, 2, KT, GT * P])
    x3 = sb("x3", [P, 2, GT, D])
    zs = sb("zs", [P, 2, GT, D])
    zT = sb("zT", [P, 2, KT, GT * P])
    w_in, dve_steps, stored = sem("w_in"), sem("dve_steps"), sem("stored")
    z_stored = [sem("z_stored0"), sem("z_stored1")]
    ys_done, yT_done, yT_copied, out_done, res_done, x3_added = (sem(n) for n in (
        "ys_done", "yT_done", "yT_copied", "out_done", "res_done", "x3_added"))
    spare = t["spare"]
    var_done, rstd_done, zs_done, zT_done, zT_copied, logits_done, logits_copied = (sem(n) for n in (
        "var_done", "rstd_done", "zs_done", "zT_done", "zT_copied", "logits_done", "logits_copied"))
    loads = [(w[:, :, :], dram["w_proj"].rearrange("(k p) n -> p k n", p=P)),
             (w_gate[:, :, :], dram["gate_w"].rearrange("(k p) n -> p k n", p=P)),
             (b_gate[:, :], dram["gate_b"].partition_broadcast(P)), (ln_w[:, :], dram["ln2_w"]), (ln_b[:, :], dram["ln2_b"])]

    def need(eng, signal, value):
        if not isinstance(value, int) or value > 0:
            eng.wait_ge(signal, value)

    def over_slots(eng, slot):
        for i in range(4):
            slot(i // 2, i % 2)
        with eng.Fori(2, NG // 2) as it:
            for q in range(2):
                slot(it, q)
        for i in range(NG, NG + 3):
            slot(i // 2, i % 2)

    def group(it, q, lag):
        g = it * 2 + q - lag
        if isinstance(g, int) and not 0 <= g < NG:
            return None
        return g, (q - lag) % 2, it + (q - lag) // 2

    with nc.Block() as block:
        @block.sync
        def _(sp):
            for dst, src in loads:
                sp.dma_start(dst, src).then_inc(w_in, 16)
            for name in t["tables"]:
                sp.dma_start(t["tables"][name][:, :], dram[name]).then_inc(t["tables_in"], 16)
            for e in range(E):
                sp.dma_start(t["w2"][:, e, :, :], dram["w2"][e].rearrange("(k p) n -> p k n", p=P)).then_inc(t["w2_in"], 16)
            with sp.Fori(0, NG // 2) as it:
                for q in range(2):
                    g = it * 2 + q
                    x_rows, z_rows = (dram[n][ds(g * GT * P, GT * P), :].rearrange("(n p) d -> p n d", p=P)
                                      for n in ("x_rows", "z_rows"))
                    sp.wait_ge(zs_done, g + 1)
                    sp.dma_start(z_rows, zs[:, q, :, :]).then_inc(z_stored[q], 16)
                    sp.wait_ge(x3_added, g + 1)
                    sp.dma_start(x_rows, X[:, ds(g * GT, GT), :]).then_inc(stored, 16)
            for q in z_stored:
                sp.wait_ge(q, 16 * NG // 2)
            sp.wait_ge(stored, 16 * NG)

        @block.gpsimd
        def _(pool):
            def slot(it, q):
                if group(it, q, 1):
                    g, par, _ = group(it, q, 1)
                    need(pool, zs_done, g)
                    pool.wait_ge(var_done, g + 1)
                    pool.tensor_tensor(rstd[:, :], mv[:, :, 1], neg_half[:, 0:GT], ALU.pow).then_inc(rstd_done, 1)
                    rows = X[:, ds(g * GT, GT), :]
                    pool.tensor_tensor(rows, rows, x3[:, par, :, :], ALU.add).then_inc(x3_added, 1)

            over_slots(pool, slot)

        @block.tensor
        def _(pe):
            def slot(it, q):
                if group(it, q, 3):
                    g, par, _ = group(it, q, 3)
                    pe.wait_ge(zT_copied, 2 * g + 2)
                    need(pe, logits_copied, g)
                    for n in range(GT):
                        for k in range(KT):
                            mm = pe.matmul(ps[6][:, n * E:(n + 1) * E], zT[:, par, k, n * P:(n + 1) * P], w_gate[:, k, :],
                                           start=(k == 0), stop=(k == KT - 1))
                    mm.then_inc(logits_done, 1)
                if group(it, q, 1):
                    g, par, _ = group(it, q, 1)
                    if isinstance(g, int) and g == 0:
                        pe.wait_ge(w_in, 16 * len(loads))
                    pe.wait_ge(yT_copied, g + 1)
                    for n in range(GT):
                        if n % 2 == 0:
                            need(pe, res_done, 2 * g - 1 + n // 2 if not isinstance(g, int) or g > 0 else 0)
                        for k in range(KT):
                            mm = pe.matmul(ps[2 + n // 2][:, n % 2 * D:(n % 2 + 1) * D], yT[:, par, k, n * P:(n + 1) * P],
                                           w[:, k, :], start=(k == 0), stop=(k == KT - 1))
                        if n % 2 == 1:
                            mm.then_inc(out_done, 1)
                if group(it, q, 2):
                    g, par, _ = group(it, q, 2)
                    pe.wait_ge(zs_done, g + 1)
                    need(pe, zT_copied, 2 * g)
                    for n in range(GT):
                        for k in range(KT):
                            tr = pe.transpose(ps[4 + k][:, n * P:(n + 1) * P], zs[:, par, n, k * P:(k + 1) * P], ident[:, :])
                    tr.then_inc(zT_done, 1)
                if group(it, q, 0):
                    g, par, _ = group(it, q, 0)
                    pe.wait_ge(ys_done, g + 1)
                    need(pe, yT_copied, g)
                    for n in range(GT):
                        for k in range(KT):
                            tr = pe.transpose(ps[k][:, n * P:(n + 1) * P], ys[:, par, n, k * P:(k + 1) * P], ident[:, :])
                    tr.then_inc(yT_done, 1)

            over_slots(pe, slot)

        @block.scalar
        def _(act):
            def slot(it, q):
                if group(it, q, 0):
                    _, par, b = group(it, q, 0)
                    act.activation(ys[:, par, :, :].rearrange("p n (h d) -> p h n d", h=H),
                                   y_all[:, ds(b * H, H), par * GT:(par + 1) * GT, :], ACT.Identity).then_inc(ys_done, 1)
                if group(it, q, 2):
                    g, par, _ = group(it, q, 2)
                    if isinstance(g, int) and g == 0:
                        act.wait_ge(w_in, 16 * len(loads))
                    need(act, logits_done, g - 1)
                    act.wait_ge(zT_done, g + 1)
                    for k in range(KT):
                        act.activation(zT[:, par, k, :], ps[4 + k][:, :], ACT.Identity,
                                       bias=ln_b[:, k:k + 1], scale=ln_w[:, k:k + 1]).then_inc(zT_copied, 1)
                if group(it, q, 0):
                    g, par, _ = group(it, q, 0)
                    act.wait_ge(yT_done, g + 1)
                    need(act, out_done, 2 * g - 2)
                    act.activation(yT[:, par, :, :], pz[:, 0:2, :], ACT.Identity).then_inc(yT_copied, 1)

            over_slots(act, slot)

        @block.vector
        def _(dve):
            def slot(it, q):
                if group(it, q, 3):
                    g, _, _ = group(it, q, 3)
                    if isinstance(g, int) and g == 0:
                        dve.wait_ge(w_in, 16 * len(loads))
                    dve.wait_ge(logits_done, g + 1)
                    dve.tensor_tensor(logits[:, ds(g * GT, GT), :], ps[6][:, 0:GT * E].rearrange("p (n e) -> p n e", n=GT),
                                      b_gate[:, :].unsqueeze(1).broadcast_to([P, GT, E]), ALU.add).then_inc(logits_copied, 1)
                if group(it, q, 1):
                    g, par, uses = group(it, q, 1)
                    need(dve, x3_added, g - 1)
                    rows = X[:, ds(g * GT, GT), :]
                    for j in range(2):
                        dve.wait_ge(out_done, 2 * g + j + 1)
                        dve.tensor_tensor(x3[:, par, 2 * j:2 * j + 2, :], rows[:, 2 * j:2 * j + 2, :],
                                          ps[2 + j][:, :].rearrange("p (r d) -> p r d", r=2), ALU.add).then_inc(res_done, 1)
                    dve.wait_ge(res_done, 2 * g + 2)
                    layer_stats(dve, Chain(dve, dve_steps, 3 * g), x3[:, par, :, :], stats, mv, spare, GT)
                    dve.sem_inc(var_done, 1)
                    need(dve, z_stored[par], 16 * uses)
                    need(dve, zT_done, g - 1)
                    dve.wait_ge(rstd_done, g + 1)
                    for n in range(GT):
                        tp = dve.tensor_scalar(zs[:, par, n, :], x3[:, par, n, :], mv[:, n, 0:1], rstd[:, n:n + 1],
                                               ALU.subtract, ALU.mult)
                    tp.then_inc(zs_done, 1)

            over_slots(dve, slot)


def route(nc, ctx, t, dram):
    def sb(name, shape, dt=F32):
        return ctx.enter_context(nc.sbuf_tensor("sb_r_" + name, shape, dt))

    def sem(name):
        return ctx.enter_context(nc.semaphore("r_" + name))

    ps, logits, owner, token_from, token_to = (t[n] for n in ("ps", "logits", "owner", "token_from", "token_to"))
    E = dram["gate_w"].shape[1]
    J = dram["slot"].shape[1]
    before, prefer, starts, count, token, slot_no = (t["tables"][n] for n in (
        "before", "prefer", "starts", "count", "token", "slot"))
    w1, w1_in, tables_in = t["w1"], t["w1_in"], t["tables_in"]
    TABLES = 16 * len(t["tables"])
    every = sb("every", [P, P])
    best = sb("best", [P, NT])
    hot = sb("hot", [P, NT, E])
    rank = sb("rank", [P, NT])
    ranked = sb("ranked", [P, NT, E])
    total = sb("total", [P, E, NT])
    until = sb("until", [P, E, NT])
    place = sb("place", [P, E, NT])
    wide = sb("wide", [P, E, NT])
    blocks = sb("blocks", [P, E])
    blocks_until = sb("blocks_until", [P, E])
    base = sb("base", [P, E])
    row = sb("row", [P, NT])
    row_i = sb("row_i", [P, NT], I32)
    block_i = sb("block_i", [P, NT], I32)
    in_block_i = sb("in_block_i", [P, NT], I32)
    block_of = sb("block_of", [P, NT])
    in_block = sb("in_block", [P, NT])
    less = sb("less", [P, NT])
    less_i = sb("less_i", [P, NT], I32)
    part_i = sb("part_i", [P, 2, NT], I32)
    part = sb("part", [P, 2, NT])
    at_block = sb("at_block", [P, NT, J])
    less_at = sb("less_at", [P, NT, 2, J], BF16)
    at_place = sb("at_place", [P, NT, P], BF16)
    found_high = sb("found_high", [P, J])
    found = sb("found", [P, J])
    nearest = sb("nearest", [P, J])
    reached = sb("reached", [1, J, E])
    owner_f = sb("owner_f", [1, J])
    ones_set, owner_done, hot_done, counted, steps, at_done, found_done = (sem(n) for n in (
        "ones_set", "owner_done", "hot_done", "counted", "steps", "at_done", "found_done"))
    CH = 8
    assert B * S + J * P < 1 << 16

    with nc.Block() as block:
        @block.sync
        def _(sp):
            sp.wait_ge(owner_done, 1)
            for j in range(len(w1_in)):
                e = sp.value_load(owner[0:1, j:j + 1], min_val=0, max_val=E - 1)
                sp.dma_start(w1[:, j, :, :], dram["w1"][ds(e, 1), :, :].rearrange("o (k p) n -> p (o k) n", p=P)).then_inc(w1_in[j], 16)

        @block.gpsimd
        def _(pool):
            pool.memset(every[:, :], 1.0).then_inc(ones_set, 1)

        @block.tensor
        def _(pe):
            pe.wait_ge(tables_in, TABLES)
            pe.wait_ge(ones_set, 1)
            pe.wait_ge(hot_done, 1)
            flat = hot[:, :, :].rearrange("p n e -> p (n e)")
            pe.matmul(ps[0][:, 0:NT * E], before[:, :], flat, start=True, stop=True).then_inc(counted, 1)
            pe.matmul(ps[1][:, 0:NT * E], every[:, :], flat, start=True, stop=True).then_inc(counted, 1)
            for n in range(NT):
                if n % CH == 0:
                    pe.wait_ge(at_done, n // CH + 2)
                mm = pe.matmul(ps[2][:, 0:2 * J], at_place[:, n, :], less_at[:, n, :, :].rearrange("p r j -> p (r j)"),
                               start=(n == 0), stop=(n == NT - 1))
            mm.then_inc(found_done, 1)

        @block.vector
        def _(dve):
            dve.wait_ge(tables_in, TABLES)
            ch = Chain(dve, steps)

            def over_e(ap):
                return ap.unsqueeze(2).broadcast_to([P, NT, E])

            ch.link(dve.tensor_reduce(best[:, :], logits[:, :, :], AX.X, ALU.max))
            ch.link(dve.tensor_tensor(hot[:, :, :], logits[:, :, :], over_e(best[:, :]), ALU.is_equal))
            ch.link(dve.tensor_tensor(ranked[:, :, :], hot[:, :, :],
                                      prefer[:, :].unsqueeze(1).broadcast_to([P, NT, E]), ALU.mult))
            ch.link(dve.tensor_reduce(rank[:, :], ranked[:, :, :], AX.X, ALU.max))
            dve.tensor_tensor(hot[:, :, :], over_e(rank[:, :]),
                              prefer[:, :].unsqueeze(1).broadcast_to([P, NT, E]), ALU.is_equal).then_inc(hot_done, 1)
            dve.wait_ge(hot_done, 1)
            dve.wait_ge(counted, 2)
            ch.link(dve.tensor_copy(total[:, :, :], ps[1][:, 0:NT * E].rearrange("p (n e) -> p e n", e=E)))
            for e in range(E):
                sc = dve.tensor_tensor_scan(until[:, e, :], every[:, 0:NT], total[:, e, :], 0.0, ALU.mult, ALU.add)
            ch.link(sc)
            ch.link(dve.tensor_tensor(place[:, :, :], until[:, :, :], total[:, :, :], ALU.subtract))
            ch.link(dve.tensor_tensor(place[:, :, :], place[:, :, :],
                                      ps[0][:, 0:NT * E].rearrange("p (n e) -> p e n", e=E), ALU.add))
            ch.link(dve.tensor_tensor(wide[:, :, :], until[:, :, NT - 1:NT].broadcast_to([P, E, NT]),
                                      starts[:, :].unsqueeze(1).broadcast_to([P, E, NT]), ALU.is_gt))
            ch.link(dve.tensor_reduce(blocks[:, :], wide[:, :, :], AX.X, ALU.add))
            ch.link(dve.tensor_tensor_scan(blocks_until[:, :], every[:, 0:E], blocks[:, :], 0.0, ALU.mult, ALU.add))
            ch.link(dve.tensor_tensor(reached[:, :, :], blocks_until[0:1, :].unsqueeze(1).broadcast_to([1, J, E]),
                                      count[0:1, 0:J].unsqueeze(2).broadcast_to([1, J, E]), ALU.is_le))
            ch.link(dve.tensor_reduce(owner_f[:, :], reached[:, :, :], AX.X, ALU.add))
            ch.link(dve.tensor_scalar(owner_f[:, :], owner_f[:, :], float(E - 1), None, ALU.min))
            dve.tensor_copy(owner[:, :], owner_f[:, :]).then_inc(owner_done, 1)
            ch.link(dve.tensor_tensor(base[:, :], blocks_until[:, :], blocks[:, :], ALU.subtract))
            ch.link(dve.tensor_scalar(base[:, :], base[:, :], float(P), None, ALU.mult))
            ch.link(dve.tensor_tensor(place[:, :, :], place[:, :, :],
                                      base[:, :].unsqueeze(2).broadcast_to([P, E, NT]), ALU.add))
            ch.link(dve.tensor_tensor(ranked[:, :, :], place[:, :, :].rearrange("p e n -> p n e"), hot[:, :, :], ALU.mult))
            ch.link(dve.tensor_reduce(row[:, :], ranked[:, :, :], AX.X, ALU.add))
            ch.link(dve.tensor_copy(row_i[:, :], row[:, :]))
            dve.tensor_scalar(block_i[:, :], row_i[:, :], P.bit_length() - 1, None, ALU.logical_shift_right)
            ch.link(dve.tensor_scalar(in_block_i[:, :], row_i[:, :], P - 1, None, ALU.bitwise_and))
            dve.tensor_copy(block_of[:, :], block_i[:, :])
            ch.link(dve.tensor_copy(in_block[:, :], in_block_i[:, :]))
            ch.link(dve.scalar_tensor_tensor(out=less[:, :], in0=row[:, :], scalar=float(B * S), in1=token[:, :],
                                             op0=ALU.add, op1=ALU.subtract))
            ch.link(dve.tensor_copy(less_i[:, :], less[:, :]))
            dve.tensor_scalar(part_i[:, 0, :], less_i[:, :], 8, None, ALU.logical_shift_right)
            ch.link(dve.tensor_scalar(part_i[:, 1, :], less_i[:, :], 255, None, ALU.bitwise_and))
            ch.link(dve.tensor_copy(part[:, :, :], part_i[:, :, :]))
            ch.link(dve.tensor_tensor(at_block[:, :, :], count[:, 0:J].unsqueeze(1).broadcast_to([P, NT, J]),
                                      block_of[:, :].unsqueeze(2).broadcast_to([P, NT, J]), ALU.is_equal))
            for q in range(2):
                last = dve.tensor_tensor(less_at[:, :, q, :], at_block[:, :, :],
                                         part[:, q, :].unsqueeze(2).broadcast_to([P, NT, J]), ALU.mult)
            last.then_inc(at_done, 1)
            for n in range(0, NT, CH):
                dve.tensor_tensor(at_place[:, n:n + CH, :], count[:, :].unsqueeze(1).broadcast_to([P, CH, P]),
                                  in_block[:, n:n + CH].unsqueeze(2).broadcast_to([P, CH, P]),
                                  ALU.is_equal).then_inc(at_done, 1)
            dve.wait_ge(found_done, 1)
            ch.link(dve.scalar_tensor_tensor(out=found_high[:, :], in0=ps[2][:, 0:J], scalar=-256.0, in1=slot_no[:, :],
                                             op0=ALU.mult, op1=ALU.add))
            ch.link(dve.tensor_tensor(found[:, :], found_high[:, :], ps[2][:, J:2 * J], ALU.subtract))
            ch.link(dve.tensor_scalar(nearest[:, :], found[:, :], float(B * S - 1), None, ALU.min))
            dve.tensor_copy(token_to[:, :], found[:, :])
            ch.link(dve.tensor_copy(token_from[:, :], nearest[:, :]))


def experts(nc, ctx, t, dram):
    def sb(name, shape, dt=F32):
        return ctx.enter_context(nc.sbuf_tensor("sb_e_" + name, shape, dt))

    def sem(name):
        return ctx.enter_context(nc.semaphore("e_" + name))

    ps, ident, owner, w2, w2_in, neg_half, token_from, token_to = (t[n] for n in (
        "ps", "ident", "owner", "w2", "w2_in", "neg_half", "token_from", "token_to"))
    E, _, HID = dram["w1"].shape
    HT = HID // P
    J = dram["slot"].shape[1]
    W = len(t["w1_in"])
    FIRST = 2 * W + 1
    assert J % W == 0
    w1, w1_in = t["w1"], t["w1_in"]
    ln_w, ln_b, tables_in = t["tables"]["ln2_w"], t["tables"]["ln2_b"], t["tables_in"]
    z = sb("z", [P, W, D])
    x = sb("x", [P, W, D])
    xT = sb("xT", [P, W, KT, P])
    hT = sb("hT", [P, W, HT, P])
    y = sb("y", [P, W, D])
    numbers = sb("numbers", [P, 3, W], U32)
    stats = sb("stats", [P, 6])
    mv = sb("mv", [P, 2])
    rstd = sb("rstd", [P, 1])
    dve_steps = sem("dve_steps")
    number_done = sem("number_done")
    z_in = [sem(f"z_in{i}") for i in range(W)]
    x_in = [sem(f"x_in{i}") for i in range(W)]
    stored = [sem(f"stored{i}") for i in range(W)]
    xT_done, xT_copied, h_done, h_copied, y_done, summed, var_done, rstd_done, normed = (sem(n) for n in (
        "xT_done", "xT_copied", "h_done", "h_copied", "y_done", "summed", "var_done", "rstd_done", "normed"))
    spare = t["spare"]

    with nc.Block() as block:
        @block.sync
        def _(sp):
            def load(j, q):
                e = sp.value_load(owner[0:1, ds(j, 1)], min_val=0, max_val=E - 1)
                sp.wait_ge(h_done, 2 * (j - W + 1))
                sp.dma_start(w1[:, q, :, :], dram["w1"][ds(e, 1), :, :].rearrange("o (k p) n -> p (o k) n", p=P)).then_inc(w1_in[q], 16)

            with sp.Fori(1, J // W) as it:
                for q in range(W):
                    load(it * W + q, q)

        @block.gpsimd
        def _(pool):
            def number(which, table, j, it, q, last, count):
                if not isinstance(it, int) or it > 0:
                    pool.wait_ge(last[q], 16 * it)
                    alone(pool, spare)
                pool.tensor_copy(numbers[:, which, q:q + 1], table[:, ds(j, 1)]).then_inc(number_done, 1)
                pool.wait_ge(number_done, count)
                alone(pool, spare)
                return bass.IndirectOffsetOnAxis(ap=numbers[:, which, q:q + 1], axis=0)

            def gather_z(j, it, q, count):
                at = number(0, token_from, j, it, q, z_in, count)
                pool.indirect_dma_start(z[:, q, :], None, dram["z_rows"], at).then_inc(z_in[q], 16)

            def gather_x(j, it, q, count):
                at = number(1, token_from, j, it, q, x_in, count)
                pool.indirect_dma_start(x[:, q, :], None, dram["x_rows"], at).then_inc(x_in[q], 16)

            def scatter(j, it, q, count):
                pool.wait_ge(var_done, j + 1)
                pool.tensor_tensor(rstd[:, :], mv[:, 1:2], neg_half[:, 0:1], ALU.pow).then_inc(rstd_done, 1)
                at = number(2, token_to, j, it, q, stored, count)
                pool.wait_ge(normed, j + 1)
                alone(pool, spare)
                pool.indirect_dma_start(dram["out"], at, y[:, q, :], None).then_inc(stored[q], 16)

            for q in range(W):
                gather_z(q, 0, q, 2 * q + 1)
                gather_x(q, 0, q, 2 * q + 2)
            pool.wait_ge(xT_done, 1)
            gather_z(W, 1, 0, FIRST)

            def step(j, it, q, count):
                scatter(j, it, q, count + 1)
                if not isinstance(j, int) or j + W < J:
                    gather_x(j + W, it + 1, q, count + 2)
                if not isinstance(j, int) or j + W + 1 < J:
                    pool.wait_ge(xT_done, j + 2)
                    alone(pool, spare)
                    gather_z(j + W + 1, it + 1 + (q + 1) // W, (q + 1) % W, count + 3)

            for q in range(W):
                step(q, 0, q, FIRST + 3 * q)
            with pool.Fori(1, J // W - 2) as it:
                for q in range(W):
                    step(it * W + q, it, q, FIRST + 3 * (it * W + q))
            for j in range(J - 2 * W, J):
                step(j, j // W, j % W, min(FIRST + 3 * j, 3 * J - (J - j)))
            for q in range(W):
                pool.wait_ge(stored[q], 16 * (J // W))

        @block.tensor
        def _(pe):
            def turn(j, it, q):
                pe.wait_ge(z_in[q], 16 * (it + 1))
                pe.wait_ge(xT_copied, 2 * j)
                for k in range(KT):
                    tr = pe.transpose(ps[7][:, k * P:(k + 1) * P], z[:, q, k * P:(k + 1) * P], ident[:, :])
                tr.then_inc(xT_done, 1)

            def up(j, it, q):
                pe.wait_ge(xT_copied, 2 * (j + 1))
                pe.wait_ge(w1_in[q], 16 * (it + 1))
                for m in range(HT):
                    for k in range(KT):
                        mm = pe.matmul(ps[2 * q + m // 4][:, m % 4 * P:(m % 4 + 1) * P],
                                       w1[:, q, k, m * P:(m + 1) * P], xT[:, q, k, :], start=(k == 0), stop=(k == KT - 1))
                    if m % 4 == 3:
                        mm.then_inc(h_done, 1)

            def down(j, q):
                e = pe.value_load(owner[0:1, ds(j, 1)], min_val=0, max_val=E - 1)
                pe.wait_ge(summed, 1 + j)
                for m in range(HT):
                    if m % 4 == 0:
                        pe.wait_ge(h_copied, 2 * j + m // 4 + 1)
                    mm = pe.matmul(ps[6][:, 0:D], hT[:, q, m, :],
                                   w2[:, ds(e, 1), m, :].rearrange("p o n -> p (o n)"), start=(m == 0), stop=(m == HT - 1))
                mm.then_inc(y_done, 1)

            turn(0, 0, 0)
            up(0, 0, 0)
            turn(1, 0, 1)
            pe.wait_ge(w2_in, 16 * E)
            with pe.Fori(0, J // W - 1) as it:
                for q in range(W):
                    j = it * W + q
                    up(j + 1, it + (q + 1) // W, (q + 1) % W)
                    turn(j + 2, it + (q + 2) // W, (q + 2) % W)
                    down(j, q)
            for q in range(W):
                j = J - W + q
                if j + 1 < J:
                    up(j + 1, J // W - 1, q + 1)
                if j + 2 < J:
                    turn(j + 2, J // W - 1, q + 2)
                down(j, q)

        @block.scalar
        def _(act):
            with act.Fori(0, J // W) as it:
                for q in range(W):
                    j = it * W + q
                    for h in range(2):
                        act.wait_ge(h_done, 2 * j + h + 1)
                        act.activation(hT[:, q, 4 * h:4 * h + 4, :], ps[2 * q + h][:, :].rearrange("p (m n) -> p m n", m=4),
                                       ACT.Gelu_apprx_tanh).then_inc(h_copied, 1)

        @block.vector
        def _(dve):
            dve.sem_inc(summed, 1)

            def turned(j, q):
                dve.wait_ge(xT_done, j + 1)
                for k in range(KT):
                    dve.tensor_scalar(xT[:, q, k, :], ps[7][:, k * P:(k + 1) * P], ln_w[:, k:k + 1], ln_b[:, k:k + 1],
                                      ALU.mult, ALU.add).then_inc(xT_copied, 1)

            def result(j, it, q):
                dve.wait_ge(y_done, j + 1)
                dve.wait_ge(x_in[q], 16 * (it + 1))
                dve.tensor_tensor(x[:, q, :], x[:, q, :], ps[6][:, 0:D], ALU.add).then_inc(summed, 1)
                dve.wait_ge(summed, 1 + j + 1)
                alone(dve, spare)
                dve.bn_stats(stats[:, :], x[:, q, :]).then_inc(dve_steps, 1)
                dve.wait_ge(dve_steps, 3 * j + 1)
                alone(dve, spare)
                dve.bn_aggr(mv[:, :], stats[:, :]).then_inc(dve_steps, 1)
                dve.wait_ge(dve_steps, 3 * j + 2)
                dve.tensor_scalar(mv[:, 1:2], mv[:, 1:2], EPS, None, ALU.add).then_inc(dve_steps, 1)
                dve.wait_ge(dve_steps, 3 * j + 3)
                dve.sem_inc(var_done, 1)
                dve.wait_ge(rstd_done, j + 1)
                if not isinstance(it, int) or it > 0:
                    dve.wait_ge(stored[q], 16 * it)
                dve.tensor_scalar(y[:, q, :], x[:, q, :], mv[:, 0:1], rstd[:, 0:1], ALU.subtract, ALU.mult).then_inc(normed, 1)

            dve.wait_ge(tables_in, 16 * len(t["tables"]))
            turned(0, 0)
            turned(1, 1)
            for q in range(W):
                turned(q + 2, (q + 2) % W)
                result(q, 0, q)
            with dve.Fori(1, J // W - 1) as it:
                for q in range(W):
                    turned(it * W + q + 2, (q + 2) % W)
                    result(it * W + q, it, q)
            for q in range(W):
                if q + 2 < W:
                    turned(J - W + q + 2, q + 2)
                result(J - W + q, J // W - 1, q)


def decoder(nc, dram, out):
    E = dram["gate_w"].shape[1]
    HT = dram["w2"].shape[1] // P
    J = B * S // P + E - 1
    W = 3
    dram["out"] = out
    dram["q_parts"] = nc.dram_tensor("q_parts", (3, B * D, S), BF16).ap()
    dram["k_parts"] = nc.dram_tensor("k_parts", (3, B * D, S), BF16).ap()
    dram["x_rows"] = nc.dram_tensor("x_rows", (B * S, D), F32).ap()
    dram["z_rows"] = nc.dram_tensor("z_rows", (B * S, D), F32).ap()
    with ExitStack() as ctx:
        def sb(name, shape, dt=F32):
            return ctx.enter_context(nc.sbuf_tensor(name, shape, dt))

        t = {}
        pz = ctx.enter_context(nc.psum_tensor("banks", [P, 8, 512], F32))
        t["pz"], t["ps"] = pz, [pz[:, i, :] for i in range(8)]
        t["X"] = sb("X", [P, NT, D])
        t["ident"] = sb("ident_sb", [P, P])
        t["neg_half"] = sb("neg_half", [P, TPB])
        t["spare"] = ctx.enter_context(nc.semaphore("spare"))
        t["common_in"] = ctx.enter_context(nc.semaphore("common_in"))

        def tensors(scope, shapes):
            for name, shape, dt in shapes:
                t[name] = scope.enter_context(nc.sbuf_tensor(name, shape, dt))

        def run(stage):
            with ExitStack() as own:
                stage(nc, own, t, dram)

        run(autocorrelation)
        with ExitStack() as attention:
            tensors(attention, [("y_all", [P, B * H, TPB, DK], F32)])
            with ExitStack() as inner:
                tensors(inner, [("v_all", [P, B * H, TPB, DK], F32)])
                with ExitStack() as ahead:
                    tensors(ahead, [("w_qkv", [P, KT, 3 * D], F32), ("ln1_w", [P, KT], F32), ("ln1_b", [P, KT], F32),
                                    ("xs_c", [P, TPB, D], F32)])
                    t["qkv_in"] = ahead.enter_context(nc.semaphore("qkv_in"))
                    run(cross_attention)
                    run(project_qkv)
                run(self_attention)
            tensors(attention, [("w2", [P, E, HT, D], F32), ("logits", [P, NT, E], F32), ("token_from", [P, J], U32),
                                ("token_to", [P, J], U32), ("owner", [1, J], I32)])
            t["w2_in"] = attention.enter_context(nc.semaphore("w2_in"))
            t["tables_in"] = attention.enter_context(nc.semaphore("tables_in"))
            t["tables"] = {name: attention.enter_context(nc.sbuf_tensor("table_" + name, [P, dram[name].shape[1]], F32))
                           for name in ("before", "prefer", "starts", "count", "token", "slot", "ln2_w", "ln2_b")}
            run(gate)
            tensors(attention, [("w1", [P, W, KT, HT * P], F32)])
            t["w1_in"] = [attention.enter_context(nc.semaphore(f"w1_in{i}")) for i in range(W)]
            run(route)
            run(experts)


def dft_constants():
    s = np.arange(S)
    ang = 2 * np.pi / S
    odd, two, zero = np.arange(1, S // 2, 2), np.arange(2, S // 2, 4), np.arange(0, S // 2, 4)
    a = ang * ((s[:512, None] * odd[None]) % S)
    fwd_odd = np.concatenate([np.cos(a), -np.sin(a)], 1)
    inv_odd = np.concatenate([np.cos(a), -np.sin(a)], 1).T * (2 / S)
    q = s[:256, None]
    a2, a0 = ang * ((q * two[None]) % S), ang * ((q * zero[None]) % S)
    f2 = np.concatenate([np.cos(a2), -np.sin(a2)], 1)
    f0 = np.concatenate([np.cos(a0), -np.sin(a0)], 1)
    f0[:, 128] = (-1.0) ** s[:256]
    i2 = f2.T * (2 / S)
    i0 = f0.T * (2 / S)
    i0[0] /= 2
    i0[128] /= 2
    return (fwd_odd.astype(np.float32), np.concatenate([f2, f0], 0).astype(np.float32),
            inv_odd.astype(np.float32), np.concatenate([i2, i0], 0).astype(np.float32))


def kernel(**inputs):
    import concourse.bacc as bacc
    from concourse.bass_utils import run_bass_kernel_spmd

    def layout(a):
        return np.ascontiguousarray(a)

    def columns(v):
        return layout(np.asarray(v).reshape(-1, P).T)

    f = {n: np.asarray(v) for n, v in inputs.items()}
    E = f["L0_ffn_gate_w"].shape[1]
    J = B * S // P + E - 1
    fwd_odd, fwd_even, inv_odd, inv_even = dft_constants()
    p = np.arange(P)
    at_zero = np.zeros((1, P), np.float32)
    at_zero[0, 0] = S
    arrays = {
        "fwd_odd": fwd_odd, "fwd_even": fwd_even, "inv_odd": inv_odd, "inv_even": inv_even, "f0": at_zero,
        "head_mask": (p[:, None] // DK == np.arange(TOP)[None]).astype(np.float32),
        "ident": np.eye(P, dtype=np.float32),
        "before": (p[:, None] < p[None]).astype(np.float32),
        "prefer": np.tile(np.arange(E, 0, -1, dtype=np.float32), (P, 1)),
        "starts": np.tile(np.arange(NT, dtype=np.float32) * P, (P, 1)),
        "count": np.tile(np.arange(P, dtype=np.float32), (P, 1)),
        "token": (np.arange(NT)[None] * P + p[:, None]).astype(np.float32),
        "slot": (B * S + np.arange(J)[None] * P + p[:, None]).astype(np.float32),
        "x": layout(f["x"]),
        "xT16": layout(f["x"][:, :DK, :].transpose(2, 0, 1).reshape(D, B * DK)),
        "L0_attn_Wq": layout(f["L0_attn_Wq"]), "L0_attn_Wk": layout(f["L0_attn_Wk"]),
        "L0_attn_Wv": layout(f["L0_attn_Wv"]), "L0_attn_Wo": layout(f["L0_attn_Wo"]),
        "b_qk": np.concatenate([f["L0_attn_bq"], f["L0_attn_bk"]])[None],
        "bv_attn": columns(f["L0_attn_bv"]), "bo_attn": layout(f["L0_attn_bo"][None]),
        "WqT": layout(f["L0_xattn_Wq"].T), "WkvT": layout(f["L0_xattn_Wkv"].T), "WoT": layout(f["L0_xattn_Wo"].T),
        "ctxT": layout(f["ctx_1024"].transpose(2, 0, 1).reshape(D, -1)),
        "bq_cross": columns(f["L0_xattn_bq"]), "bk_cross": columns(f["L0_xattn_bkv"][:D]),
        "bv_cross": layout(f["L0_xattn_bkv"][None, D:]), "bo_cross": layout(f["L0_xattn_bo"][None]),
        "w_qkv": layout(f["L0_ffn_w_qkv"]), "w_proj": layout(f["L0_ffn_w_proj"]),
        "ln1_w": columns(f["L0_ffn_ln1_w"]), "ln1_b": columns(f["L0_ffn_ln1_b"]),
        "ln2_w": columns(f["L0_ffn_ln2_w"]), "ln2_b": columns(f["L0_ffn_ln2_b"]),
        "gate_w": layout(f["L0_ffn_gate_w"]), "gate_b": layout(f["L0_ffn_gate_b"][None]),
        "w1": layout(f["L0_ffn_w1"]), "w2": layout(f["L0_ffn_w2"]),
    }
    nc = bacc.Bacc("TRN2", target_bir_lowering=False, num_devices=1)
    given, dram = {}, {}
    for name, a in arrays.items():
        given[f"in_{name}"] = a
        dram[name] = nc.dram_tensor(f"in_{name}", a.shape, mybir.dt.from_np(a.dtype), kind="ExternalInput").ap()
    out = nc.dram_tensor("out_x", (B * S + J * P, D), F32, kind="ExternalOutput").ap()
    decoder(nc, dram, out)
    r = run_bass_kernel_spmd(nc, [given], core_ids=[0])
    return r.results[0]["out_x"][:B * S].reshape(B, S, D)
```
